# Optimizing a Trainium2 kernel written in Bass

```python
import numpy as np
import jax
import jax.numpy as jnp

def _softmax(x, axis=-1):
    return jax.nn.softmax(x, axis=axis)

def _gelu(x):
    return jax.nn.gelu(x, approximate=True)

def _silu(x):
    return jax.nn.silu(x)

def _sigmoid(x):
    return jax.nn.sigmoid(x)

def _layernorm(x, axis=-1, eps=1e-05):
    m = jnp.mean(x, axis=axis, keepdims=True)
    v = jnp.var(x, axis=axis, keepdims=True)
    return (x - m) / jnp.sqrt(v + eps)

def _scatter_add(tgt, idx, src, axis=0):
    return tgt.at[idx].add(src)

def _segment_sum(src, seg, n):
    return jax.ops.segment_sum(src, seg, n)
kernel_name = 'mk_adj_ffn_d1_adj_r2_c212f1'

def setup_inputs(seed: int=0):
    np.random.seed(seed)
    _w = jnp.asarray

    def _rec_inputs():
        import jax
        import jax.numpy as jnp
        _gk = jax.random.key(seed)
        x = -0.0005207 + 1.001 * jax.random.normal(jax.random.fold_in(_gk, 1), (16, 512, 128), jnp.float32)
        _a = jax.random.bernoulli(jax.random.fold_in(_gk, 2), 0.00390625, (16, 512, 512))
        _a = jnp.logical_or(_a, jnp.swapaxes(_a, -1, -2))
        _a = jnp.logical_or(_a, jnp.eye(512, dtype=bool))
        adj = _a.astype(jnp.int32)
        return (x, adj)
    x, adj = _rec_inputs()

    def _L0_gnn_setup():
        import jax, jax.numpy as jnp
        import numpy as np
        B, N, F_IN, F_OUT, H = (8, 512, 128, 128, 4)
        HD = F_OUT // H
        NEG_SLOPE = 0.2
        key = jax.random.key(seed)
        k1, k2, k3 = jax.random.split(key, 3)
        x = jax.random.normal(k1, (B, N, F_IN), dtype=jnp.float32)
        adj = jnp.ones((B, N, N), dtype=jnp.int32)
        W = jax.random.normal(k2, (F_IN, F_OUT), dtype=jnp.float32) / np.sqrt(F_IN)
        a = jax.random.normal(k3, (H, 2 * HD), dtype=jnp.float32) * np.sqrt(2.0 / (H + 2 * HD))
        return {'x': x, 'adj': adj, 'W': W, 'a': a}
    _L0_gnn_all = _L0_gnn_setup()
    _L0_gnn_in = {k: v for k, v in _L0_gnn_all.items() if k in ('W', 'a')}
    del _L0_gnn_all

    def _L0_ffn_setup():
        import jax, jax.numpy as jnp
        import numpy as np
        B, S, D, H, E, K = (8, 4096, 128, 512, 8, 2)
        key = jax.random.key(seed)
        ks = jax.random.split(key, 7)
        s_in = 1.0 / np.sqrt(D)
        s_hid = 1.0 / np.sqrt(H)
        return {'x': jax.random.normal(ks[0], (B, S, D), dtype=jnp.float32), 'Wg': jax.random.uniform(ks[1], (E, D), jnp.float32, -s_in, s_in), 'bg': jax.random.uniform(ks[2], (E,), jnp.float32, -s_in, s_in), 'W1': jax.random.uniform(ks[3], (E, H, D), jnp.float32, -s_in, s_in), 'b1': jax.random.uniform(ks[4], (E, H), jnp.float32, -s_in, s_in), 'W2': jax.random.uniform(ks[5], (E, D, H), jnp.float32, -s_hid, s_hid), 'b2': jax.random.uniform(ks[6], (E, D), jnp.float32, -s_hid, s_hid)}
    _L0_ffn_all = _L0_ffn_setup()
    _L0_ffn_in = {k: v for k, v in _L0_ffn_all.items() if k in ('Wg', 'bg', 'W1', 'b1', 'W2', 'b2')}
    del _L0_ffn_all
    return {'x': x, 'adj': adj, 'L0_gnn_W': _L0_gnn_in['W'], 'L0_gnn_a': _L0_gnn_in['a'], 'L0_ffn_Wg': _L0_ffn_in['Wg'], 'L0_ffn_bg': _L0_ffn_in['bg'], 'L0_ffn_W1': _L0_ffn_in['W1'], 'L0_ffn_b1': _L0_ffn_in['b1'], 'L0_ffn_W2': _L0_ffn_in['W2'], 'L0_ffn_b2': _L0_ffn_in['b2']}

def reference(x, adj, L0_gnn_W, L0_gnn_a, L0_ffn_Wg, L0_ffn_bg, L0_ffn_W1, L0_ffn_b1, L0_ffn_W2, L0_ffn_b2):
    import jax
    import jax.numpy as jnp

    def _L0_gnn_ref(x, adj, W, a):
        import jax, jax.numpy as jnp
        import numpy as np
        B, N, F_IN, F_OUT, H = (8, 512, 128, 128, 4)
        HD = F_OUT // H
        NEG_SLOPE = 0.2
        Bq, Nq, _ = x.shape
        h = (x @ W).reshape(Bq, Nq, H, HD).transpose(0, 2, 1, 3)
        a1, a2 = (a[:, :HD], a[:, HD:])
        s1 = jnp.einsum('bhnd,hd->bhn', h, a1)
        s2 = jnp.einsum('bhmd,hd->bhm', h, a2)
        e = jax.nn.leaky_relu(s1[:, :, :, None] + s2[:, :, None, :], NEG_SLOPE)
        e = jnp.where(adj[:, None, :, :] == 0, -jnp.inf, e)
        attention = jax.nn.softmax(e, axis=-1)
        out = jnp.einsum('bhnm,bhmd->bhnd', attention, h)
        return out.transpose(0, 2, 1, 3).reshape(Bq, Nq, H * HD)

    def _L0_ffn_ref(x, Wg, bg, W1, b1, W2, b2):
        import jax, jax.numpy as jnp
        import numpy as np
        B, S, D, H, E, K = (8, 4096, 128, 512, 8, 2)
        gate_scores = jnp.einsum('bsd,ed->bse', x, Wg) + bg
        topk_scores, topk_idx = jax.lax.top_k(gate_scores, K)
        topk_probs = jax.nn.softmax(topk_scores, axis=-1)
        combine = jnp.sum(topk_probs[..., None] * jax.nn.one_hot(topk_idx, E, dtype=x.dtype), axis=-2)
        out = jnp.zeros_like(x)
        for e in range(E):
            h = jax.nn.relu(jnp.einsum('bsd,hd->bsh', x, W1[e]) + b1[e])
            y = jnp.einsum('bsh,dh->bsd', h, W2[e]) + b2[e]
            out = out + combine[..., e:e + 1] * y
        return out
    x = x + _L0_gnn_ref(_layernorm(x, axis=-1), adj, L0_gnn_W, L0_gnn_a)
    x = x + _L0_ffn_ref(_layernorm(x, axis=-1), L0_ffn_Wg, L0_ffn_bg, L0_ffn_W1, L0_ffn_b1, L0_ffn_W2, L0_ffn_b2)
    return x

_drawn_inputs = setup_inputs


def setup_inputs(seed=0):
    import zlib

    import numpy as np

    out = dict(_drawn_inputs(seed))
    spreads = {}
    factors = {'L0_ffn_b1': 4.41, 'L0_ffn_b2': 3.514}
    for name, (base, spread) in spreads.items():
        noise = np.random.default_rng([zlib.crc32(name.encode()), seed]).standard_normal(out[name].shape)
        drawn = base * np.exp(spread * noise) if base else spread * noise
        out[name] = jnp.asarray(drawn.astype(out[name].dtype))
    for name, factor in factors.items():
        out[name] = (out[name] * factor).astype(out[name].dtype)
    return out
```

```python
from contextlib import ExitStack

import concourse.bass as bass
from concourse import mybir

ALU = mybir.AluOpType
ACT = mybir.ActivationFunctionType
AX = mybir.AxisListType
F32 = mybir.dt.float32
BF16 = mybir.dt.bfloat16
FP16 = mybir.dt.float16
I32 = mybir.dt.int32

P = 128
NB = 16
N = 512
D = 128
NT = N // P
H = 4
HD = D // H
E = 8
HID = 512
NC = HID // P
TOK = NB * N
TILES = TOK // P
EPS = 1e-5
SLOPE = 0.2
SHIFT = 60.0
VW = 2 * (HD + 1)
BLK = 256
BT = BLK // P
CAP = TOK + BLK
BLOCKS = 2 * TOK // BLK + E - 1
TAB = BLOCKS + 1
XS_ROWS = E * CAP + BLK
ROW = D + 2
XSCALE = 1024.0

C_ID, C_TRI, C_SEL, C_MASK, C_REV, C_BASE, C_TOK, C_IOTA, C_HALF, C_ONE = range(10)
_W = [P, P, H * P, H, E, E, TILES, TAB, NT, P]
_O = [sum(_W[:k]) for k in range(len(_W))]
NCONST = sum(_W)


def constants(np):
    c = np.zeros((P, NCONST), np.float32)
    r = np.arange(P)

    def put(k, v):
        c[:, _O[k]:_O[k] + _W[k]] = v

    put(C_ID, np.eye(P))
    put(C_TRI, r[:, None] < r[None, :])
    for h in range(H):
        for part in range(3):
            c[8 * part + H + h, _O[C_SEL] + h * P:_O[C_SEL] + (h + 1) * P] = 1
    put(C_MASK, (r[:, None] // HD) == np.arange(H)[None, :])
    put(C_REV, E - np.arange(E)[None, :])
    put(C_BASE, np.arange(E)[None, :] * CAP)
    put(C_TOK, np.arange(TILES)[None, :] * P + r[:, None])
    put(C_IOTA, np.arange(TAB)[None, :])
    put(C_HALF, -0.5)
    put(C_ONE, 1.0)
    return c


class Batch:

    def __init__(self, base, i=None, unroll=2):
        self.p, self.q = base % 2, base % 4
        if i is None:
            self.n, self.h, self.f = base, base // 2, base // 4
        else:
            self.n, self.h = i * unroll + base, i * (unroll // 2) + base // 2
            self.f = i + base // 4


def ge(eng, sem, value):
    if isinstance(value, int) and value <= 0:
        return
    eng.wait_ge(sem, value)


def hold(eng, sem, value, turns):
    if isinstance(value, int) and value <= 0:
        return
    eng.wait_ge(sem, value)
    eng.sem_inc(turns, 1)


class Chain:

    def __init__(self, eng, sem, per, n):
        self.eng, self.sem, self.per, self.n, self.k = eng, sem, per, n, 0

    def did(self, ins):
        self.k += 1
        ins.then_inc(self.sem, 1)

    def now(self):
        return self.n * self.per + self.k

    def wait(self):
        self.eng.wait_ge(self.sem, self.now())

    def after(self, k):
        self.eng.wait_ge(self.sem, self.n * self.per + k)


LN_STEPS, S_STEPS, MX_STEPS, ARG_STEPS, X_STEPS, T_STEPS, ATT_STEPS, RT_STEPS = 8, 6, 2, 6, 4, 8, 2, 24
RT_SEL, RT_DM = 13, 14


def build(nc, x, adj, W, a, Wg, bg, W1, b1, W2, b2, const, out):
    with ExitStack() as ctx:
        def sb(name, shape, dt=F32):
            return ctx.enter_context(nc.sbuf_tensor(name, shape, dt))

        def ps(name, shape, dt=F32):
            return ctx.enter_context(nc.psum_tensor(name, shape, dt))

        def sem(name):
            return ctx.enter_context(nc.semaphore(name))

        xs = nc.dram_tensor("expert_rows", [XS_ROWS, ROW], F32, kind="Internal").ap()
        ybuf = nc.dram_tensor("expert_out", [2 * TOK, D], F32, kind="Internal").ap()

        cst = sb("cst", [P, NCONST])

        def C(k, rows=P):
            return cst[0:rows, _O[k]:_O[k] + _W[k]]

        ident = C(C_ID)
        identb = sb("identb", [P, P], BF16)
        identh = sb("identh", [P, P], FP16)
        trib = sb("trib", [P, P], BF16)
        onesb = sb("onesb", [P, P], BF16)
        selb = sb("selb", [24, H * P], BF16)
        xr = sb("xr", [P, TILES, D])
        adji = sb("adji", [P, 2, NT, N], I32)
        adjb = sb("adjb", [P, NT, N], BF16)
        adjn = sb("adjn", [P, 2, NT, N], BF16)
        G = sb("G", [P, 2, H, NT, N], BF16)
        mv1 = sb("mv1", [P, NT, 2])
        bs1 = sb("bs1", [P, NT, 6])
        rs1 = sb("rs1", [P, NT])
        xn = sb("xn", [P, NT, D])
        xnT = sb("xnT", [P, N])
        sN = sb("sN", [P, NT, 8])
        sneg = sb("sneg", [P, 2, NT, H])
        sr = sb("sr", [P, NT, 8])
        sp3 = sb("sp3", [P, NT, 3, 8], BF16)
        rows = sb("rows", [24, 2, N], BF16)
        mx = sb("mx", [H, 1])
        diag = sb("diag", [H, H])
        arg = sb("arg", [P, 4, NT, H])
        zt = sb("zt", [P, NT, H])
        Mt = sb("Mt", [P, NT, H])
        Ex = sb("Ex", [P, 2, 4, NT, H])
        V = sb("V", [P, NT, H, VW])
        V1 = sb("V1", [P, NT, H, VW])
        Vp = sb("Vp", [P, 2, NT, 3, H, VW], BF16)
        T1 = sb("T1", [P, NT, H, HD + 1])
        T2 = sb("T2", [P, NT, H, HD + 1])
        rec = sb("rec", [P, NT, H])
        att = sb("att", [P, NT, D])
        mv2 = sb("mv2", [P, NT, 2])
        bs2 = sb("bs2", [P, NT, 6])
        rs2 = sb("rs2", [P, NT])
        xn2 = sb("xn2", [P, NT, D])
        xn2T = sb("xn2T", [P, N])
        g8 = sb("g8", [P, NT, E])
        m01 = sb("m01", [P, 2, NT])
        v01 = sb("v01", [P, 2, NT])
        eq = sb("eq", [P, NT, E])
        cand = sb("cand", [P, NT, E])
        OH = sb("OH", [P, 2, NT, E])
        g2 = sb("g2", [P, NT, E])
        sel = sb("sel", [P, NT, E], BF16)
        dm = sb("dm", [P, NT])
        ed = sb("ed", [P, NT])
        den = sb("den", [P, NT])
        PR = sb("PR", [P, 2, TILES])
        pos = sb("pos", [P, NT, E])
        carry = sb("carry", [P, E])
        prod = sb("prod", [P, 2, NT, E])
        slotf = sb("slotf", [P, 2, NT])
        idx = sb("idx", [P, 2, 2, NT], I32)
        rowt = sb("rowt", [P, 2, NT, ROW])
        Wr = sb("Wr", [P, D])
        WT = sb("WT", [P, D])
        acol = sb("acol", [P, 2])
        Am = sb("Am", [P, 2 * H])
        Wa = sb("Wa", [P, 2 * H])
        Wgr = sb("Wgr", [E, D])
        WgT = sb("WgT", [P, E])
        bgb = sb("bgb", [P, E])
        b1r = sb("b1r", [E * NC, P])
        b1s = sb("b1s", [P, E * NC])
        b2b = sb("b2b", [P, E, D])
        W1h = sb("W1h", [P, 2, E, HID], FP16)
        W2h = sb("W2h", [P, 2, E, NC, D], FP16)
        sc = sb("sc", [P, 16])
        Gf = G[:, :, :, :, :].rearrange("p a h t n -> p (a h t n)").bitcast(F32)
        W1r = Gf[:, 0:E * NC * D].rearrange("p (t d) -> p t d", d=D)
        W2r = Gf[:, E * NC * D:2 * E * NC * D].rearrange("p (e h) -> p e h", h=HID)
        tf = sb("tf", [P, 8, TAB])
        cube = sb("cube", [P, TAB, E])
        cnt = sb("cnt", [P, 6, E])
        cnti = sb("cnti", [P, 2, E], I32)
        tab = sb("tab", [P, 2, TAB], I32)
        padrow = sb("padrow", [P, BT, ROW])
        h32 = Gf[:, 0:2 * NC * BLK].rearrange("p (a c n) -> p a c n", a=2, c=NC)
        hp = G[:, :, :, :, :].rearrange("p a h t n -> p (a h t n)")[:, 4 * NC * BLK:8 * NC * BLK] \
            .bitcast(FP16).rearrange("p (a q c n) -> p a q c n", a=2, q=2, c=NC)
        xb = sb("xb", [P, 4, BT, ROW])
        xt = sb("xt", [P, 2, 2, BLK], FP16)
        ysb = sb("ysb", [P, 4, BT, D])
        bk = sb("bk", [P, 2, BT])
        bidx = sb("bidx", [P, 4, BT], I32)
        yin = adji[:, :, :, :].rearrange("p a t n -> p (a t n)").bitcast(F32) \
            .rearrange("p (b k t d) -> p b k t d", b=4, k=2, d=D)

        bank = [ps(f"bank{k}", [P, 512]) for k in range(8)]
        bc = [bank[0], bank[1]]
        Ob = [bank[2], bank[3]]
        TR = bank[4]
        HP = bank[5]
        MS = bank[7]
        AD = bank[6][:, :].bitcast(BF16).rearrange("p (a n) -> p a n", a=2)
        s12p = MS[:, 0:32].rearrange("p (t c) -> p t c", c=8)
        Sp = MS[:, 32:36]
        gp = TR[:, 0:32].rearrange("p (t e) -> p t e", e=E)
        rkp = MS[:, 96:128].rearrange("p (t e) -> p t e", e=E)
        totp = MS[:, 128:136]
        rowp = bank[6][0:24, 0:256].bitcast(BF16)
        Up = [[bank[0], bank[1]], [bank[2], bank[3]]]
        XTp = [bank[4][:, :].bitcast(FP16)[:, 0:2 * BLK].rearrange("p (q n) -> p q n", q=2),
               bank[5][:, :].bitcast(FP16)[:, 0:2 * BLK].rearrange("p (q n) -> p q n", q=2)]
        Yp = [bank[6][:, 0:BT * D].rearrange("p (t d) -> p t d", d=D),
              bank[7][:, 0:BT * D].rearrange("p (t d) -> p t d", d=D)]

        names = """ld_const ld_small ld_w1 ld_w2 ld_x0 ld_x1 ld_adj0 ld_adj1
            const_ready prep_step prep_pe prep_act w_pe w_act w_dve scale_ready small_ready
            ln1 rstd1 xn_ready xT_ready xnT_ready h_ready s_steps sT_ready rows_ready mx_steps S_ready
            arg_steps exp_ready v_steps part1_ready rest_ready part2_ready part3_ready
            adj_cast adjT_ready adjn_ready bc_ready g_ready o_ready t_steps sum_ready att_steps x1_ready
            ln2 rstd2 xn2_ready x2T_ready xn2T_ready gate_ready rt_steps ed_ready rank_ready
            hi_ready lo_ready scattered0 scattered1 tab_steps tab_ready padded pads_ready
            ld_rows0 ld_rows1 ld_rows2 ld_rows3 bt_ready xt_ready up_ready hid_ready split_steps down_ready y_ready
            bidx_steps back0 back1 back2 back3 ld_y0 ld_y1 ld_y2 ld_y3 o1_steps final_ready stored0 stored1 stored2 stored3 pool_turns dve_turns"""
        S = {n: sem(n) for n in names.split()}
        ld_adj = [S["ld_adj0"], S["ld_adj1"]]
        scattered = [S["scattered0"], S["scattered1"]]
        ld_rows = [S[f"ld_rows{k}"] for k in range(4)]
        back = [S[f"back{k}"] for k in range(4)]
        ld_y = [S[f"ld_y{k}"] for k in range(4)]
        stored = [S[f"stored{k}"] for k in range(4)]

        xd = x.rearrange("b (t p) d -> p (b t) d", p=P)
        outd = out.rearrange("b (t p) d -> p (b t) d", p=P)
        adjd = adj.rearrange("b (t p) m -> b p t m", p=P)
        yd = ybuf.rearrange("(k t p) d -> p k t d", k=2, p=P)
        XSPLIT = 3 * NT
        SMALL = 8

        def slots(eng, body, last):
            for s in range(-1, 4):
                body(lambda k, s=s: Batch(s + k) if 0 <= s + k < NB else None)
            with eng.Fori(0, 5) as i:
                for u in range(2):
                    body(lambda k, u=u: Batch(4 + u + k, i))
            for s in range(14, last + 1):
                body(lambda k, s=s: Batch(s + k) if 0 <= s + k < NB else None)

        def blocks(eng, body):
            for k in range(4):
                body(Batch(k))
            with eng.Fori(0, BLOCKS // 4 - 1) as i:
                for k in range(4):
                    body(Batch(4 + k, i, 4))
            for k in range(BLOCKS // 4 * 4, BLOCKS):
                body(Batch(k))

        def steps(eng, body):
            def fixed(s):
                return lambda k: Batch(s + k) if 0 <= s + k < BLOCKS else None
            for s in range(-2, 2):
                body(fixed(s))
            with eng.Fori(0, (BLOCKS - 4) // 4) as i:
                for u in range(4):
                    body(lambda k, u=u: Batch(2 + u + k, i, 4))
            for s in range(2 + (BLOCKS - 4) // 4 * 4, BLOCKS):
                body(fixed(s))

        block = ctx.enter_context(nc.Block())

        @block.sync
        def _(sp):
            sp.dma_start(cst[:, :], const).then_inc(S["ld_const"], 16)
            sp.dma_start(Wr[:, :], W).then_inc(S["ld_small"], 16)
            for k in range(2):
                for h in range(H):
                    lo = HD * (1 - k)
                    sp.dma_start(acol[HD * h:HD * (h + 1), k:k + 1],
                                 a[h:h + 1, lo:lo + HD].rearrange("h d -> d h")).then_inc(S["ld_small"], 16)
            sp.dma_start(Wgr[:, :], Wg).then_inc(S["ld_small"], 16)
            sp.dma_start(b1r[:, :], b1.rearrange("e (c p) -> (e c) p", p=P)).then_inc(S["ld_small"], 16)
            sp.dma_start(xr[:, 0:XSPLIT, :], xd[:, 0:XSPLIT, :]).then_inc(S["ld_x0"], 16)
            sp.dma_start(W1r, W1.rearrange("e (c p) d -> p (e c) d", p=P)).then_inc(S["ld_w1"], 16)
            sp.dma_start(W2r, W2.rearrange("e d h -> d e h")).then_inc(S["ld_w2"], 16)

            def load_adj(B):
                ge(sp, S["adj_cast"], B.n - 1)
                sp.dma_start(adji[:, B.p], adjd[bass.ds(B.n, 1)].rearrange("b p t m -> p (b t) m")) \
                  .then_inc(ld_adj[B.p], 16)
            load_adj(Batch(0))
            load_adj(Batch(1))
            sp.dma_start(xr[:, XSPLIT:TILES, :], xd[:, XSPLIT:TILES, :]).then_inc(S["ld_x1"], 16)
            with sp.Fori(0, (NB - 2) // 2) as i:
                load_adj(Batch(2, i))
                load_adj(Batch(3, i))

            sp.wait_ge(S["tab_ready"], 1)
            for e in range(E):
                r = sp.value_load(cnti[0:1, 0, e:e + 1], min_val=e * CAP, max_val=e * CAP + TOK)
                sp.dma_start(xs[bass.ds(r, BLK), :].rearrange("(t p) w -> p t w", p=P), padrow[:, :, :]) \
                  .then_inc(S["pads_ready"], 16)
            sp.dma_start(xs[E * CAP:E * CAP + BLK, :].rearrange("(t p) w -> p t w", p=P), padrow[:, :, :]) \
              .then_inc(S["pads_ready"], 16)
            sp.wait_ge(S["pads_ready"], 16 * (E + 1))
            sp.wait_ge(scattered[0], 16 * 2 * NT * NB // 2)
            sp.wait_ge(scattered[1], 16 * 2 * NT * NB // 2)

            def load_rows(B):
                ge(sp, S["bt_ready"], B.n - 3)
                ge(sp, S["bidx_steps"], B.n * 2 - 6)
                r = sp.value_load(tab[0:1, 0, bass.ds(B.n, 1)], min_val=0, max_val=E * CAP)
                sp.dma_start(xb[:, B.q], xs[bass.ds(r, BLK), :].rearrange("(t p) w -> p t w", p=P)) \
                  .then_inc(ld_rows[B.q], 16)
            blocks(sp, load_rows)

            for k in range(4):
                sp.wait_ge(back[k], 16 * BT * ((BLOCKS + 3 - k) // 4))

            def load_y(n, q, k):
                ge(sp, stored[k], q * 16)
                for c in range(2):
                    sp.dma_start(yin[:, k, c], yd[:, c, bass.ds(n * NT, NT), :]).then_inc(ld_y[k], 16)
            for k in range(4):
                load_y(k, 0, k)
            with sp.Fori(1, 4) as q:
                for k in range(4):
                    load_y(q * 4 + k, q, k)
            for k in range(4):
                sp.wait_ge(stored[k], 16 * 4)

        @block.gpsimd
        def _(pool):
            def rstd(name, steps, mv, rs, B, ready):
                hold(pool, ready, B.n * LN_STEPS + LN_STEPS, S["pool_turns"])
                c = Chain(pool, S[name], 2, B.n)
                c.did(pool.tensor_scalar(rs[:, :], mv[:, :, 1], 1.0, EPS, ALU.mult, ALU.add))
                hold(pool, S[name], c.now(), S["pool_turns"])
                c.did(pool.tensor_tensor(rs[:, :], rs[:, :], C(C_HALF), ALU.pow))

            def scatter(Z, js):
                if js[0] == 0:
                    hold(pool, S["rt_steps"], Z.n * RT_STEPS + RT_STEPS, S["pool_turns"])
                    hold(pool, S["hi_ready"], Z.n + 1, S["pool_turns"])
                    hold(pool, S["lo_ready"], Z.n + 1, S["pool_turns"])
                for j in js:
                    for k in range(2):
                        pool.indirect_dma_start(
                            xs, bass.IndirectOffsetOnAxis(ap=idx[:, Z.p, k, j:j + 1], axis=0),
                            rowt[:, Z.p, j, :], None).then_inc(scattered[Z.p], 16)

            def body(at):
                F, R, Z = at(1), at(-1), at(-3)
                if Z:
                    scatter(Z, [0])
                if F:
                    hold(pool, S["xn_ready"], F.n * NT, S["pool_turns"])
                    rstd("rstd1", 2, mv1, rs1, F, S["ln1"])
                if Z:
                    scatter(Z, [1, 2, 3])
                if R:
                    hold(pool, S["t_steps"], R.n * T_STEPS + T_STEPS, S["pool_turns"])
                    c = Chain(pool, S["sum_ready"], 1, R.n)
                    c.did(pool.tensor_tensor(T1[:, :, :, :], T1[:, :, :, :], T2[:, :, :, :], ALU.add))
                    hold(pool, S["att_steps"], R.n * ATT_STEPS + ATT_STEPS, S["pool_turns"])
                    xt4 = xr[:, bass.ds(R.n * NT, NT), :]
                    pool.tensor_tensor(xt4, xt4, att[:, :, :], ALU.add).then_inc(S["x1_ready"], 1)
                    hold(pool, S["xn2_ready"], R.n * NT, S["pool_turns"])
                    rstd("rstd2", 2, mv2, rs2, R, S["ln2"])

            hold(pool, S["ld_const"], 16, S["pool_turns"])
            pool.dma_start(b2b[:, :, :].rearrange("p e d -> p (e d)"),
                           b2.rearrange("e d -> (e d)").partition_broadcast(P)).then_inc(S["small_ready"], 16)
            pool.dma_start(bgb[:, :], bg.partition_broadcast(P)).then_inc(S["small_ready"], 16)
            slots(pool, body, 18)

            def send(B):
                hold(pool, S["bidx_steps"], B.n * 2 + 2, S["pool_turns"])
                hold(pool, S["y_ready"], B.n + 1, S["pool_turns"])
                for t in range(BT):
                    pool.indirect_dma_start(
                        ybuf, bass.IndirectOffsetOnAxis(ap=bidx[:, B.q, t:t + 1], axis=0),
                        ysb[:, B.q, t, :], None, bounds_check=2 * TOK - 1, oob_is_err=False) \
                        .then_inc(back[B.q], 16)
            blocks(pool, send)

        @block.scalar
        def _(act):
            act.wait_ge(S["scale_ready"], 1)
            for u in range(2 * E):
                act.wait_ge(S["w_pe"], u + 1)
                dst = W1h[:, 0, u, :] if u < E else W2h[:, 0, u - E, :, :].rearrange("p c d -> p (c d)")
                act.activation(dst, bank[u % 4][:, :], ACT.Copy,
                               scale=sc[:, 3:4] if u < E else sc[:, 7:8]).then_inc(S["w_act"], 1)

            def body(at):
                F, Q = at(1), at(-2)
                if Q:
                    act.wait_ge(S["x2T_ready"], Q.n + 1)
                    ge(act, S["gate_ready"], Q.n)
                    act.activation(xn2T[:, :], TR[:, :], ACT.Copy).then_inc(S["xn2T_ready"], 1)
                    ge(act, scattered[Q.p], Q.h * 16 * 2 * NT)
                    act.activation(rowt[:, Q.p, :, 0:D // 2].bitcast(FP16), xn2[:, :, :], ACT.Copy,
                                   scale=XSCALE).then_inc(S["hi_ready"], 1)
                if F:
                    act.wait_ge(S["xT_ready"], F.n + 1)
                    ge(act, S["h_ready"], F.n)
                    act.activation(xnT[:, :], TR[:, :], ACT.Copy).then_inc(S["xnT_ready"], 1)
                    act.wait_ge(S["sT_ready"], F.n + 1)
                    ge(act, S["bc_ready"], (F.n - 1) * H)
                    ge(act, S["mx_steps"], (F.n - 1) * MX_STEPS)
                    act.activation(rows[:, F.p, :], rowp, ACT.Copy).then_inc(S["rows_ready"], 1)
                if Q:
                    act.wait_ge(S["rt_steps"], Q.n * RT_STEPS + RT_DM)
                    act.activation(ed[:, :], dm[:, :], ACT.Exp).then_inc(S["ed_ready"], 1)
                if F:
                    act.wait_ge(S["arg_steps"], F.n * ARG_STEPS + ARG_STEPS)
                    ge(act, S["t_steps"], (F.n - 1) * T_STEPS)
                    act.activation(Ex[:, F.p], arg[:, :, :, :], ACT.Exp).then_inc(S["exp_ready"], 1)
                    for g in range(2):
                        act.wait_ge(S["adjT_ready"], F.n * 2 + g + 1)
                        if g == 0:
                            ge(act, S["g_ready"], (F.n - 1) * H * NT)
                            ge(act, S["o_ready"], (F.n - 1) * NT)
                        act.activation(adjn[:, F.p, 2 * g:2 * g + 2, :], AD[:, :, 0:N], ACT.Copy, scale=-1.0) \
                           .then_inc(S["adjn_ready"], 1)
                    act.wait_ge(S["v_steps"], F.n * X_STEPS + X_STEPS)
                    ge(act, S["o_ready"], (F.n - 1) * NT)
                    act.activation(Vp[:, F.p, :, 0].rearrange("p t h v -> p t (h v)"),
                                   V[:, :, :, :].rearrange("p t h v -> p t (h v)"),
                                   ACT.Copy).then_inc(S["part1_ready"], 1)
                    act.wait_ge(S["rest_ready"], F.n + 1)
                    act.activation(Vp[:, F.p, :, 1].rearrange("p t h v -> p t (h v)"),
                                   V1[:, :, :, :].rearrange("p t h v -> p t (h v)"),
                                   ACT.Copy).then_inc(S["part2_ready"], 1)
            slots(act, body, 17)

            def hidden(at):
                X, U = at(2), at(1)
                if X:
                    act.wait_ge(S["bt_ready"], X.n + 1)
                    ge(act, S["up_ready"], (X.n - 1) * NC)
                    act.activation(xt[:, X.p], XTp[X.p], ACT.Copy).then_inc(S["xt_ready"], 1)
                if U:
                    ge(act, S["split_steps"], (U.n - 1) * 2)
                    ex = act.value_load(tab[0:1, 1, bass.ds(U.n, 1)], min_val=0, max_val=E - 1)
                    for c in range(NC):
                        if c % 2 == 0:
                            act.wait_ge(S["up_ready"], U.n * NC + c + 2)
                        act.activation(h32[:, U.p, c, :], Up[U.p][c // 2][:, (c % 2) * BLK:(c % 2 + 1) * BLK],
                                       ACT.Relu, bias=b1s[:, bass.ds(ex * NC + c, 1)], scale=sc[:, 10:11]) \
                           .then_inc(S["hid_ready"], 1)
            act.wait_ge(S["tab_ready"], 1)
            steps(act, hidden)

            def store(n, q, k):
                act.wait_ge(S["final_ready"], n * NT + NT)
                act.dma_start(outd[:, bass.ds(n * NT, NT), :], yin[:, k, 1]).then_inc(stored[k], 16)
            with act.Fori(0, 4) as q:
                for k in range(4):
                    store(q * 4 + k, q, k)
            for k in range(4):
                act.wait_ge(stored[k], 16 * 4)

        @block.vector
        def _(dve):
            dve.wait_ge(S["ld_const"], 16)
            for dst, src in ((identb, ident), (identh, ident), (trib, C(C_TRI)), (onesb, C(C_ONE)),
                             (selb, C(C_SEL, 24))):
                dve.tensor_copy(dst[:, :], src).then_inc(S["const_ready"], 1)
            dve.tensor_copy(carry[:, :], C(C_BASE)).then_inc(S["const_ready"], 1)
            dve.memset(padrow[:, :, 0:D], 0.0).then_inc(S["const_ready"], 1)
            dve.memset(padrow[:, :, D:D + 1], float(2 * TOK)).then_inc(S["const_ready"], 1)
            dve.memset(padrow[:, :, D + 1:D + 2], 0.0).then_inc(S["const_ready"], 1)
            dve.wait_ge(S["const_ready"], 9)

            dve.wait_ge(S["ld_small"], 16 * (2 * H + 3))
            k = Chain(dve, S["prep_step"], 0, 0)
            k.did(dve.tensor_scalar(Am[:, 0:H], C(C_MASK), acol[:, 0:1], None, ALU.mult))
            k.did(dve.tensor_scalar(Am[:, H:2 * H], C(C_MASK), acol[:, 1:2], None, ALU.mult))
            dve.wait_ge(S["prep_pe"], 1)
            k.did(dve.tensor_copy(WT[:, :], bank[4][:, 0:D]))
            k.did(dve.tensor_copy(WgT[:, :], bank[5][:, 0:E]))
            k.did(dve.tensor_copy(b1s[:, :], bank[6][:, 0:E * NC]))
            dve.wait_ge(S["prep_pe"], 2)
            k.did(dve.tensor_copy(Wa[:, :], bank[4][:, D:D + 2 * H]))
            dve.wait_ge(S["ld_w1"], 16)
            k.did(dve.tensor_reduce(sc[:, 0:1], W1r, AX.XY, ALU.max, apply_absolute_value=True))
            dve.wait_ge(S["ld_w2"], 16)
            k.did(dve.tensor_reduce(sc[:, 1:2], W2r, AX.XY, ALU.max, apply_absolute_value=True))
            k.wait()
            k.did(dve.tensor_reduce(sc[:, 2:3], b1s[:, :], AX.X, ALU.max, apply_absolute_value=True))
            dve.wait_ge(S["prep_pe"], 3)
            k.did(dve.tensor_reduce(tf[0:1, 0, 0:1], bank[5][0:1, 128:256], AX.X, ALU.max))
            k.did(dve.tensor_reduce(tf[0:1, 0, 1:2], bank[5][0:1, 256:384], AX.X, ALU.max))
            k.did(dve.tensor_reduce(tf[0:1, 0, 2:3], bank[5][0:1, 384:512], AX.X, ALU.max))
            dve.wait_ge(S["prep_pe"], 4)
            k.did(dve.tensor_scalar(sc[:, 0:1], bank[4][:, 256:257], 1e-20, None, ALU.max))
            k.did(dve.tensor_scalar(sc[:, 1:2], bank[4][:, 257:258], 1e-20, None, ALU.max))
            k.wait()
            k.did(dve.scalar_tensor_tensor(sc[:, 2:3], sc[:, 0:1], 128.0, bank[4][:, 258:259], ALU.mult, ALU.add))
            k.wait()
            k.did(dve.tensor_scalar(sc[:, 4:7].bitcast(I32), sc[:, 0:3].bitcast(I32), 0x7F800000, None,
                                    ALU.bitwise_and))
            k.wait()
            k.did(dve.reciprocal(sc[:, 12:15], sc[:, 4:7]))
            k.wait()
            k.did(dve.tensor_scalar(sc[:, 3:4], sc[:, 12:13], 2.0 ** 13, None, ALU.mult))
            k.did(dve.tensor_scalar(sc[:, 7:8], sc[:, 13:14], 2.0 ** 13, None, ALU.mult))
            k.did(dve.tensor_scalar(sc[:, 8:9], sc[:, 14:15], 2.0 ** 13, None, ALU.mult))
            k.did(dve.tensor_scalar(sc[:, 9:10], sc[:, 4:5], 2.0 ** -13 / XSCALE, None, ALU.mult))
            k.did(dve.tensor_scalar(sc[:, 11:12], sc[:, 6:7], 2.0 ** -13, None, ALU.mult))
            k.did(dve.tensor_scalar(sc[:, 15:16], sc[:, 5:6], 2.0 ** -13, None, ALU.mult))
            k.wait()
            k.did(dve.tensor_tensor(sc[:, 10:11], sc[:, 9:10], sc[:, 8:9], ALU.mult))
            k.did(dve.tensor_tensor(sc[:, 11:12], sc[:, 11:12], sc[:, 15:16], ALU.mult))
            k.did(dve.tensor_scalar(b1s[:, :], b1s[:, :], sc[:, 8:9], None, ALU.mult))
            k.wait()
            dve.sem_inc(S["scale_ready"], 1)
            for u in range(2 * E):
                dve.wait_ge(S["w_act"], u + 1)
                part = [(W1h[:, q, u, :] if u < E else W2h[:, q, u - E, :, :].rearrange("p c d -> p (c d)"))
                        for q in range(2)]
                dve.scalar_tensor_tensor(part[1], bank[u % 4][:, :], sc[:, 3:4] if u < E else sc[:, 7:8],
                                         part[0], ALU.mult, ALU.subtract).then_inc(S["w_dve"], 1)

            def stats(c, src, bs, mv):
                for j in range(NT):
                    c.did(dve.bn_stats(bs[:, j, :], src[:, j, :]))
                hold(dve, c.sem, c.now(), S["dve_turns"])
                for j in range(NT):
                    c.did(dve.bn_aggr(mv[:, j, :], bs[:, j, :]))

            def normalise(dst, src, mv, rs, ready):
                for j in range(NT):
                    dve.tensor_scalar(dst[:, j, :], src[:, j, :], mv[:, j, 0:1], rs[:, j:j + 1],
                                      ALU.subtract, ALU.mult).then_inc(ready, 1)

            def mask(M, h, mts):
                for mt in mts:
                    if h == 0:
                        dve.wait_ge(S["adjn_ready"], M.n * 2 + mt // 2 + 1)
                        if mt == 0:
                            dve.wait_ge(S["s_steps"], M.n * S_STEPS + S_STEPS)
                            ge(dve, S["o_ready"], (M.n - 1) * NT)
                    if mt == mts[0]:
                        dve.wait_ge(S["bc_ready"], M.n * H + h + 1)
                    dve.scalar_tensor_tensor(G[:, M.p, h, mt, :], bc[h % 2][:, :], sneg[:, M.p, mt, h:h + 1],
                                             adjn[:, M.p, mt, :], ALU.is_gt, ALU.logical_and) \
                       .then_inc(S["g_ready"], 1)

            def scaled_sums(R, nt):
                dve.wait_ge(S["o_ready"], R.n * NT + nt + 1)
                if nt == 0:
                    dve.wait_ge(S["exp_ready"], R.n + 1)
                    ge(dve, S["sum_ready"], R.n)
                    ge(dve, S["att_steps"], R.n * ATT_STEPS)
                o = Ob[nt % 2][:, 0:H * VW].rearrange("p (h v) -> p h v", v=VW)
                for q, T in enumerate((T1, T2)):
                    f = Ex[:, R.p, 2 + q, nt, :].unsqueeze(2).to_broadcast([P, H, HD + 1])
                    dve.tensor_tensor(T[:, nt], o[:, :, q * (HD + 1):(q + 1) * (HD + 1)], f, ALU.mult) \
                       .then_inc(S["t_steps"], 1)

            rev = C(C_REV).unsqueeze(1).to_broadcast([P, NT, E])

            def body(at):
                F, M, R, Q = at(1), at(0), at(-1), at(-2)
                if Q:
                    rt = Chain(dve, S["rt_steps"], RT_STEPS, Q.n)
                    dve.wait_ge(S["rstd2"], Q.n * 2 + 2)
                    ge(dve, S["x2T_ready"], Q.n)
                    ge(dve, S["hi_ready"], Q.n)
                    ge(dve, S["lo_ready"], Q.n)
                    x4 = xr[:, bass.ds(Q.n * NT, NT), :]
                    normalise(xn2, x4, mv2, rs2, S["xn2_ready"])
                if F:
                    if isinstance(F.n, int):
                        dve.wait_ge(S["ld_x0"], 16)
                        if F.n * NT >= XSPLIT:
                            dve.wait_ge(S["ld_x1"], 16)
                    l1 = Chain(dve, S["ln1"], LN_STEPS, F.n)
                    ge(dve, S["xn_ready"], F.n * NT)
                    xf = xr[:, bass.ds(F.n * NT, NT), :]
                    stats(l1, xf, bs1, mv1)
                    dve.wait_ge(ld_adj[F.p], F.h * 16 + 16)
                    ge(dve, S["adjT_ready"], F.n * 2)
                    dve.tensor_scalar(adjb[:, :, :], adji[:, F.p], 0.0, None, ALU.not_equal) \
                       .then_inc(S["adj_cast"], 1)
                if M:
                    mask(M, 0, [0, 1])
                if Q:
                    dve.wait_ge(S["hi_ready"], Q.n + 1)
                    dve.scalar_tensor_tensor(rowt[:, Q.p, :, D // 2:D].bitcast(FP16), xn2[:, :, :], XSCALE,
                                             rowt[:, Q.p, :, 0:D // 2].bitcast(FP16), ALU.mult, ALU.subtract) \
                       .then_inc(S["lo_ready"], 1)
                if M:
                    mask(M, 0, [2, 3])
                if F:
                    dve.wait_ge(S["rstd1"], F.n * 2 + 2)
                    ge(dve, S["xT_ready"], F.n)
                    normalise(xn, xf, mv1, rs1, S["xn_ready"])
                if R:
                    scaled_sums(R, 0)
                if Q:
                    dve.wait_ge(S["gate_ready"], Q.n + 1)
                    rt.did(dve.tensor_tensor(g8[:, :, :], gp, bgb[:, :].unsqueeze(1).to_broadcast([P, NT, E]), ALU.add))
                if M:
                    mask(M, 1, [0])
                if Q:
                    rt.wait()
                    rt.did(dve.tensor_reduce(m01[:, 0, :], g8[:, :, :], AX.X, ALU.max))
                if M:
                    mask(M, 1, [1])
                if Q:
                    rt.wait()
                    rt.did(dve.tensor_tensor(eq[:, :, :], g8[:, :, :], m01[:, 0, :].unsqueeze(2).to_broadcast([P, NT, E]),
                                             ALU.is_equal))
                if F:
                    st = Chain(dve, S["s_steps"], S_STEPS, F.n)
                    dve.wait_ge(S["h_ready"], F.n + 1)
                    ge(dve, S["sT_ready"], F.n)
                    ge(dve, S["arg_steps"], F.n * ARG_STEPS)
                    st.did(dve.tensor_copy(sN[:, :, :], s12p))
                    st.did(dve.tensor_copy(sp3[:, :, 0, :], s12p))
                    st.did(dve.tensor_scalar(sneg[:, F.p], s12p[:, :, 0:H], -1.0, None, ALU.mult))
                if Q:
                    rt.wait()
                    rt.did(dve.tensor_tensor(cand[:, :, :], eq[:, :, :], rev, ALU.mult))
                if F:
                    st.after(2)
                    st.did(dve.tensor_tensor(sr[:, :, :], sN[:, :, :], sp3[:, :, 0, :], ALU.subtract))
                if M:
                    mask(M, 1, [2])
                if F:
                    st.wait()
                    st.did(dve.tensor_copy(sp3[:, :, 1, :], sr[:, :, :]))
                if Q:
                    rt.wait()
                    rt.did(dve.tensor_reduce(v01[:, 0, :], cand[:, :, :], AX.X, ALU.max))
                if M:
                    mask(M, 1, [3])
                if F:
                    st.wait()
                    st.did(dve.tensor_tensor(sp3[:, :, 2, :], sr[:, :, :], sp3[:, :, 1, :], ALU.subtract))
                if Q:
                    rt.wait()
                    rt.did(dve.tensor_tensor(OH[:, 0], rev, v01[:, 0, :].unsqueeze(2).to_broadcast([P, NT, E]),
                                             ALU.is_equal))
                if R:
                    scaled_sums(R, 1)
                if Q:
                    rt.wait()
                    rt.did(dve.scalar_tensor_tensor(g2[:, :, :], OH[:, 0], -1e30, g8[:, :, :], ALU.mult, ALU.add))
                if M:
                    mask(M, 2, [0])
                if Q:
                    rt.wait()
                    rt.did(dve.tensor_reduce(m01[:, 1, :], g2[:, :, :], AX.X, ALU.max))
                if M:
                    mask(M, 2, [1])
                if Q:
                    rt.wait()
                    rt.did(dve.tensor_tensor(eq[:, :, :], g2[:, :, :], m01[:, 1, :].unsqueeze(2).to_broadcast([P, NT, E]),
                                             ALU.is_equal))
                if F:
                    mc = Chain(dve, S["mx_steps"], MX_STEPS, F.n)
                    dve.wait_ge(S["rows_ready"], F.n + 1)
                    mc.did(dve.tensor_reduce(mx[:, :], rows[0:H, F.p, :], AX.X, ALU.max))
                if Q:
                    rt.wait()
                    rt.did(dve.tensor_tensor(cand[:, :, :], eq[:, :, :], rev, ALU.mult))
                if M:
                    mask(M, 2, [2])
                if F:
                    mc.wait()
                    ge(dve, S["S_ready"], F.n)
                    mc.did(dve.tensor_scalar(diag[:, :], C(C_ID, H)[:, 0:H], mx[:, 0:1], None, ALU.mult))
                if Q:
                    rt.wait()
                    rt.did(dve.tensor_reduce(v01[:, 1, :], cand[:, :, :], AX.X, ALU.max))
                if M:
                    mask(M, 2, [3])
                if Q:
                    rt.wait()
                    rt.did(dve.tensor_tensor(OH[:, 1], rev, v01[:, 1, :].unsqueeze(2).to_broadcast([P, NT, E]),
                                             ALU.is_equal))
                if R:
                    scaled_sums(R, 2)
                if Q:
                    rt.wait()
                    ge(dve, S["rank_ready"], Q.n)
                    rt.did(dve.tensor_tensor(sel[:, :, :], OH[:, 0], OH[:, 1], ALU.add))
                    assert rt.k == RT_SEL
                    ge(dve, S["ed_ready"], Q.n)
                    rt.did(dve.tensor_tensor(dm[:, :], m01[:, 1, :], m01[:, 0, :], ALU.subtract))
                    assert rt.k == RT_DM
                if M:
                    mask(M, 3, [0])
                if R:
                    scaled_sums(R, 3)
                if F:
                    ac = Chain(dve, S["arg_steps"], ARG_STEPS, F.n)
                    dve.wait_ge(S["S_ready"], F.n + 1)
                    ge(dve, S["exp_ready"], F.n)
                    Sb = Sp.unsqueeze(1).to_broadcast([P, NT, H])
                    ac.did(dve.scalar_tensor_tensor(arg[:, 0], sN[:, :, 0:H], SHIFT, Sb, ALU.add, ALU.subtract))
                    ac.did(dve.tensor_tensor(zt[:, :, :], sN[:, :, H:2 * H], Sb, ALU.add))
                if M:
                    mask(M, 3, [1])
                if Q:
                    dve.wait_ge(S["ed_ready"], Q.n + 1)
                    rt.did(dve.tensor_scalar(den[:, :], ed[:, :], 1.0, None, ALU.add))
                if F:
                    ac.after(2)
                    ac.did(dve.scalar_tensor_tensor(Mt[:, :, :], zt[:, :, :], SLOPE, zt[:, :, :], ALU.mult, ALU.max))
                    ac.did(dve.tensor_scalar(arg[:, 1], arg[:, 0], SLOPE, (1 - SLOPE) * SHIFT, ALU.mult, ALU.add))
                if Q:
                    rt.wait()
                    rt.did(dve.reciprocal(PR[:, 0, bass.ds(Q.n * NT, NT)], den[:, :]))
                if F:
                    ac.after(3)
                    ac.did(dve.tensor_tensor(arg[:, 2], zt[:, :, :], Mt[:, :, :], ALU.subtract))
                    ac.did(dve.scalar_tensor_tensor(arg[:, 3], zt[:, :, :], SLOPE, Mt[:, :, :], ALU.mult, ALU.subtract))
                if M:
                    mask(M, 3, [2])
                if Q:
                    rt.wait()
                    rt.did(dve.tensor_tensor(PR[:, 1, bass.ds(Q.n * NT, NT)], ed[:, :],
                                             PR[:, 0, bass.ds(Q.n * NT, NT)], ALU.mult))
                    dve.wait_ge(S["rank_ready"], Q.n + 1)
                    rt.did(dve.tensor_tensor(pos[:, :, :], rkp, carry[:, :].unsqueeze(1).to_broadcast([P, NT, E]),
                                             ALU.add))
                    rt.wait()
                    rt.did(dve.tensor_tensor(carry[:, :], totp, carry[:, :], ALU.add))
                if M:
                    mask(M, 3, [3])
                if Q:
                    rt.after(RT_DM + 4)
                    rt.did(dve.tensor_tensor(prod[:, :, :, :], OH[:, :, :, :],
                                             pos[:, :, :].unsqueeze(1).to_broadcast([P, 2, NT, E]), ALU.mult))
                if F:
                    vc = Chain(dve, S["v_steps"], X_STEPS, F.n)
                    dve.wait_ge(S["exp_ready"], F.n + 1)
                    ge(dve, S["part1_ready"], F.n)
                    h3 = HP[:, :].rearrange("p (g d) -> p g d", d=HD)
                    Vg = V[:, :, :, :].rearrange("p t h v -> p (t h) v")
                    eB = Ex[:, F.p, 0].rearrange("p t h -> p (t h)")
                    eD = Ex[:, F.p, 1].rearrange("p t h -> p (t h)")
                    vc.did(dve.tensor_tensor(Vg[:, :, 0:HD], h3, eB.unsqueeze(2).to_broadcast([P, NT * H, HD]), ALU.mult))
                    vc.did(dve.scalar_tensor_tensor(Vg[:, :, HD + 1:2 * HD + 1], h3, -1.0,
                                                    eD.unsqueeze(2).to_broadcast([P, NT * H, HD]), ALU.mult, ALU.mult))
                    vc.did(dve.tensor_copy(Vg[:, :, HD], eB))
                    vc.did(dve.tensor_scalar(Vg[:, :, 2 * HD + 1], eD, -1.0, None, ALU.mult))
                if Q:
                    rt.wait()
                    rt.did(dve.tensor_reduce(slotf[:, :, :], prod[:, :, :, :], AX.X, ALU.add))
                    ge(dve, scattered[Q.p], Q.h * 16 * 2 * NT)
                    rt.did(dve.tensor_copy(rowt[:, Q.p, :, D + 1], v01[:, 0, :]))
                    rt.did(dve.tensor_copy(rowt[:, Q.p, :, D], C(C_TOK)[:, bass.ds(Q.n * NT, NT)]))
                    rt.after(RT_DM + 7)
                    rt.did(dve.tensor_copy(idx[:, Q.p], slotf[:, :, :]))
                    assert rt.k == RT_STEPS
                if R:
                    at_ = Chain(dve, S["att_steps"], ATT_STEPS, R.n)
                    dve.wait_ge(S["sum_ready"], R.n + 1)
                    ge(dve, S["x1_ready"], R.n)
                    at_.did(dve.reciprocal(rec[:, :, :], T1[:, :, :, HD]))
                    at_.wait()
                    at_.did(dve.tensor_tensor(
                        att[:, :, :].rearrange("p t (h d) -> p (t h) d", d=HD),
                        T1[:, :, :, :].rearrange("p t h v -> p (t h) v")[:, :, 0:HD],
                        rec[:, :, :].rearrange("p t h -> p (t h)").unsqueeze(2).to_broadcast([P, NT * H, HD]), ALU.mult))
                if F:
                    dve.wait_ge(S["part1_ready"], F.n + 1)
                    ge(dve, S["part2_ready"], F.n)
                    dve.tensor_tensor(V1[:, :, :, :].rearrange("p t h v -> p t (h v)"),
                                      V[:, :, :, :].rearrange("p t h v -> p t (h v)"),
                                      Vp[:, F.p, :, 0].rearrange("p t h v -> p t (h v)"), ALU.subtract) \
                       .then_inc(S["rest_ready"], 1)
                if R:
                    dve.wait_ge(S["x1_ready"], R.n + 1)
                    l2 = Chain(dve, S["ln2"], LN_STEPS, R.n)
                    stats(l2, xr[:, bass.ds(R.n * NT, NT), :], bs2, mv2)
                if F:
                    dve.wait_ge(S["part2_ready"], F.n + 1)
                    dve.tensor_tensor(Vp[:, F.p, :, 2].rearrange("p t h v -> p t (h v)"),
                                      V1[:, :, :, :].rearrange("p t h v -> p t (h v)"),
                                      Vp[:, F.p, :, 1].rearrange("p t h v -> p t (h v)"), ALU.subtract) \
                       .then_inc(S["part3_ready"], 1)
            dve.wait_ge(S["small_ready"], 32)
            slots(dve, body, 17)

            t = Chain(dve, S["tab_steps"], 0, 0)
            dve.wait_ge(S["rt_steps"], NB * RT_STEPS)

            def step(ins):
                t.did(ins)
                t.wait()
            step(dve.tensor_copy(cnti[:, 0, :], carry[:, :]))
            step(dve.tensor_tensor(cnt[:, 0, :], carry[:, :], C(C_BASE), ALU.subtract))
            step(dve.tensor_scalar(cnti[:, 1, :], cnt[:, 0, :], float(BLK - 1), None, ALU.add))
            step(dve.tensor_scalar(cnti[:, 1, :], cnti[:, 1, :], BLK.bit_length() - 1, None, ALU.arith_shift_right))
            step(dve.tensor_copy(cnt[:, 1, :], cnti[:, 1, :]))
            cur = 1
            for d in (1, 2, 4):
                step(dve.tensor_copy(cnt[:, cur + 1, 0:d], cnt[:, cur, 0:d]))
                step(dve.tensor_tensor(cnt[:, cur + 1, d:E], cnt[:, cur, d:E], cnt[:, cur, 0:E - d], ALU.add))
                cur += 1
            ends = cnt[:, cur, :].unsqueeze(1).to_broadcast([P, TAB, E])
            io = C(C_IOTA).unsqueeze(2).to_broadcast([P, TAB, E])
            step(dve.tensor_tensor(cube[:, :, :], io, ends, ALU.is_ge))
            step(dve.tensor_reduce(tf[:, 0, :], cube[:, :, :], AX.X, ALU.add))
            step(dve.tensor_tensor(cube[:, :, :], cube[:, :, :], ends, ALU.mult))
            step(dve.tensor_reduce(tf[:, 1, :], cube[:, :, :], AX.X, ALU.max))
            step(dve.tensor_tensor(tf[:, 2, :], C(C_IOTA), tf[:, 1, :], ALU.subtract))
            step(dve.tensor_scalar(tf[:, 3, :], tf[:, 0, :], float(CAP), None, ALU.mult))
            step(dve.scalar_tensor_tensor(tf[:, 4, :], tf[:, 2, :], float(BLK), tf[:, 3, :], ALU.mult, ALU.add))
            step(dve.tensor_scalar(tab[:, 0, :], tf[:, 4, :], float(E * CAP), None, ALU.min))
            step(dve.tensor_scalar(tab[:, 1, :], tf[:, 0, :], float(E - 1), None, ALU.min))
            step(dve.tensor_scalar(tf[:, 5, :], tf[:, 0, :], -1.0, float(E), ALU.mult, ALU.add))
            dve.sem_inc(S["tab_ready"], 1)

            def split(U):
                dve.wait_ge(S["hid_ready"], U.n * NC + NC)
                ge(dve, S["down_ready"], U.n - 1)
                c = Chain(dve, S["split_steps"], 2, U.n)
                c.did(dve.tensor_copy(hp[:, U.p, 0], h32[:, U.p]))
                c.wait()
                c.did(dve.tensor_tensor(hp[:, U.p, 1], h32[:, U.p], hp[:, U.p, 0], ALU.subtract))

            def work(at):
                X, U, Y = at(2), at(1), at(0)
                if U:
                    dve.wait_ge(ld_rows[U.q], U.f * 16 + 16)
                    ge(dve, back[U.q], U.f * 16 * BT)
                    c = Chain(dve, S["bidx_steps"], 2, U.n)
                    c.did(dve.tensor_scalar(bk[:, U.p, :], xb[:, U.q, :, D + 1], tf[:, 5, bass.ds(U.n, 1)],
                                            float(TOK), ALU.not_equal, ALU.mult))
                if U:
                    c.wait()
                    c.did(dve.tensor_tensor(bidx[:, U.q, :], bk[:, U.p, :], xb[:, U.q, :, D], ALU.add))
                    split(U)
                if Y:
                    ex = dve.value_load(tab[0:1, 1, bass.ds(Y.n, 1)], min_val=0, max_val=E - 1)
                    dve.wait_ge(S["down_ready"], Y.n + 1)
                    ge(dve, back[Y.q], Y.f * 16 * BT)
                    dve.scalar_tensor_tensor(ysb[:, Y.q], Yp[Y.p], sc[:, 11:12],
                                             b2b[:, bass.ds(ex, 1), :].to_broadcast([P, BT, D]),
                                             ALU.mult, ALU.add).then_inc(S["y_ready"], 1)
            steps(dve, work)

            def final(n, q, k):
                dve.wait_ge(ld_y[k], q * 32 + 32)
                for j in range(NT):
                    xt1 = xr[:, bass.ds(n * NT + j, 1), :].rearrange("p a d -> p (a d)")
                    dve.scalar_tensor_tensor(xt1, yin[:, k, 0, j, :], PR[:, 0, bass.ds(n * NT + j, 1)], xt1,
                                             ALU.mult, ALU.add).then_inc(S["o1_steps"], 1)
                for j in range(NT):
                    xt1 = xr[:, bass.ds(n * NT + j, 1), :].rearrange("p a d -> p (a d)")
                    dve.wait_ge(S["o1_steps"], n * NT + j + 1)
                    dve.scalar_tensor_tensor(yin[:, k, 1, j, :], yin[:, k, 1, j, :], PR[:, 1, bass.ds(n * NT + j, 1)],
                                             xt1, ALU.mult, ALU.add).then_inc(S["final_ready"], 1)
            with dve.Fori(0, 4) as q:
                for k in range(4):
                    final(q * 4 + k, q, k)

        @block.tensor
        def _(pe):
            mm = pe.matmul
            pe.wait_ge(S["ld_const"], 16)
            pe.wait_ge(S["ld_small"], 16 * (2 * H + 3))
            pe.transpose(bank[4][:, 0:D], Wr[:, :], ident)
            pe.transpose(bank[5][:, 0:E], Wgr[:, :], C(C_ID, E)[:, 0:E])
            pe.transpose(bank[6][:, 0:E * NC], b1r[:, :], C(C_ID, E * NC)[:, 0:E * NC]).then_inc(S["prep_pe"], 1)
            pe.wait_ge(S["prep_step"], 5)
            mm(bank[4][:, D:D + 2 * H], WT[:, :], Am[:, :], start=True, stop=True).then_inc(S["prep_pe"], 1)
            pe.wait_ge(S["prep_step"], 9)
            for q in range(3):
                last = pe.transpose(bank[5][0:1, 128 * (q + 1):128 * (q + 2)], sc[:, q:q + 1], ident)
            last.then_inc(S["prep_pe"], 1)
            pe.wait_ge(S["prep_step"], 12)
            mm(bank[4][:, 256:259], C(C_ONE, 1), tf[0:1, 0, 0:3], start=True, stop=True).then_inc(S["prep_pe"], 1)
            for u in range(2 * E):
                ge(pe, S["w_dve"], u - 3)
                ge(pe, S["w_act"], u - 3)
                for c in range(NC):
                    src = W1r[:, u * NC + c, :] if u < E else W2r[:, u - E, c * P:(c + 1) * P]
                    last = pe.transpose(bank[u % 4][:, c * P:(c + 1) * P], src, ident)
                last.then_inc(S["w_pe"], 1)
            pe.wait_ge(S["w_dve"], 2 * E)
            pe.wait_ge(S["const_ready"], 9)

            def broadcast(M, h):
                if h == 0:
                    pe.wait_ge(S["rows_ready"], M.n + 1)
                ge(pe, S["g_ready"], (M.n * H + h - 1) * NT)
                mm(bc[h % 2][:, :], selb[:, h * P:(h + 1) * P], rows[:, M.p, :], start=True, stop=True) \
                    .then_inc(S["bc_ready"], 1)

            def sums(R, nt):
                ge(pe, S["t_steps"], R.n * T_STEPS + 2 * (nt - 1))
                if nt == 0:
                    pe.wait_ge(S["part2_ready"], R.n + 1)
                    pe.wait_ge(S["part3_ready"], R.n + 1)
                o = Ob[nt % 2][:, 0:H * VW].rearrange("p (h v) -> p h v", v=VW)
                first = True
                for mt in range(NT):
                    for q in range(3):
                        mm(o[:, :, HD + 1:VW], adjn[:, R.p, mt, nt * P:(nt + 1) * P],
                           Vp[:, R.p, mt, q, :, HD + 1:VW], start=first, stop=False, skip_group_check=True)
                        first = False
                for h in range(H):
                    for mt in range(NT):
                        for q in range(3):
                            last = mm(o[:, h, :], G[:, R.p, h, mt, nt * P:(nt + 1) * P], Vp[:, R.p, mt, q, h, :],
                                      start=False, stop=(h == H - 1 and mt == NT - 1 and q == 2),
                                      skip_group_check=True)
                last.then_inc(S["o_ready"], 1)

            def transpose_adj(F, g):
                if g == 0:
                    pe.wait_ge(S["adj_cast"], F.n + 1)
                    pe.wait_ge(S["rows_ready"], F.n + 1)
                else:
                    pe.wait_ge(S["adjn_ready"], F.n * 2 + 1)
                for mt in (2 * g, 2 * g + 1):
                    for nt in range(NT):
                        last = pe.transpose(AD[:, mt % 2, nt * P:(nt + 1) * P],
                                            adjb[:, nt, mt * P:(mt + 1) * P], identb[:, :])
                last.then_inc(S["adjT_ready"], 1)

            def body(at):
                F, M, R, Q = at(1), at(0), at(-1), at(-2)
                if M:
                    broadcast(M, 0)
                    broadcast(M, 1)
                if Q:
                    pe.wait_ge(S["xn2_ready"], Q.n * NT + NT)
                    pe.wait_ge(S["xnT_ready"], Q.n + 3 if F else NB)
                    for j in range(NT):
                        last = pe.transpose(TR[:, j * P:(j + 1) * P], xn2[:, j, :], ident)
                    last.then_inc(S["x2T_ready"], 1)
                if R:
                    pe.wait_ge(S["g_ready"], R.n * H * NT + H * NT)
                    sums(R, 0)
                if Q:
                    pe.wait_ge(S["xn2T_ready"], Q.n + 1)
                    for j in range(NT):
                        last = mm(gp[:, j, :], xn2T[:, j * P:(j + 1) * P], WgT[:, :], start=True, stop=True)
                    last.then_inc(S["gate_ready"], 1)
                if F:
                    pe.wait_ge(S["xn_ready"], F.n * NT + NT)
                    if Q:
                        pe.wait_ge(S["rt_steps"], Q.n * RT_STEPS + 1)
                    for j in range(NT):
                        last = pe.transpose(TR[:, j * P:(j + 1) * P], xn[:, j, :], ident)
                    last.then_inc(S["xT_ready"], 1)
                if R:
                    sums(R, 1)
                if M:
                    broadcast(M, 2)
                if F:
                    pe.wait_ge(S["xnT_ready"], F.n + 1)
                    if Q:
                        ge(pe, S["rt_steps"], Q.n * RT_STEPS)
                    ge(pe, S["v_steps"], F.n * X_STEPS)
                    for j in range(NT):
                        mm(HP[:, j * P:(j + 1) * P], xnT[:, j * P:(j + 1) * P], Wr[:, :], start=True, stop=True)
                        last = mm(s12p[:, j, :], xnT[:, j * P:(j + 1) * P], Wa[:, :], start=True, stop=True)
                    last.then_inc(S["h_ready"], 1)
                if R:
                    sums(R, 2)
                if F:
                    pe.wait_ge(S["s_steps"], F.n * S_STEPS + S_STEPS)
                    ge(pe, S["adjn_ready"], F.n * 2)
                    for j in range(NT):
                        last = pe.transpose(rowp[:, j * P:(j + 1) * P],
                                            sp3[:, j].rearrange("p q c -> p (q c)"), identb[:, :])
                    last.then_inc(S["sT_ready"], 1)
                if M:
                    broadcast(M, 3)
                if F:
                    pe.wait_ge(S["mx_steps"], F.n * MX_STEPS + MX_STEPS)
                    mm(Sp, C(C_ONE, H), diag[:, :], start=True, stop=True).then_inc(S["S_ready"], 1)
                if R:
                    sums(R, 3)
                if Q:
                    pe.wait_ge(S["rt_steps"], Q.n * RT_STEPS + RT_SEL)
                    if F:
                        pe.wait_ge(S["arg_steps"], F.n * ARG_STEPS + 2)
                    mm(rkp, trib[:, :], sel[:, :, :], start=True, stop=False, skip_group_check=True)
                    for j in range(NT - 1):
                        mm(rkp[:, j + 1:NT, :], onesb[:, :], sel[:, j:j + 1, :].to_broadcast([P, NT - 1 - j, E]),
                           start=False, stop=(j == NT - 2), skip_group_check=True)
                    for j in range(NT):
                        last = mm(totp, onesb[:, :], sel[:, j, :], start=(j == 0), stop=(j == NT - 1),
                                  skip_group_check=True)
                    last.then_inc(S["rank_ready"], 1)
                if F:
                    transpose_adj(F, 0)
                    transpose_adj(F, 1)
            slots(pe, body, 17)

            def layers(at):
                X, U, Y = at(2), at(1), at(0)
                if X:
                    pe.wait_ge(ld_rows[X.q], X.f * 16 + 16)
                    ge(pe, S["xt_ready"], X.n - 1)
                    xv = xb[:, X.q, :, 0:D].bitcast(FP16).rearrange("p t (q d) -> p t q d", q=2)
                    for q in range(2):
                        for t in range(BT):
                            last = pe.transpose(XTp[X.p][:, q, t * P:(t + 1) * P], xv[:, t, q, :], identh[:, :])
                    last.then_inc(S["bt_ready"], 1)
                if Y:
                    ey = pe.value_load(tab[0:1, 1, bass.ds(Y.n, 1)], min_val=0, max_val=E - 1)
                if U:
                    pe.wait_ge(S["xt_ready"], U.n + 1)
                    ge(pe, S["hid_ready"], (U.n - 1) * NC)
                    ex = pe.value_load(tab[0:1, 1, bass.ds(U.n, 1)], min_val=0, max_val=E - 1)
                    for c in range(NC):
                        o = Up[U.p][c // 2][:, (c % 2) * BLK:(c % 2 + 1) * BLK]
                        for n, (wq, xq) in enumerate(((0, 0), (0, 1), (1, 0))):
                            w = W1h[:, wq, bass.ds(ex, 1), c * P:(c + 1) * P].rearrange("p e h -> p (e h)")
                            last = mm(o, w, xt[:, U.p, xq, :], start=(n == 0), stop=(n == 2))
                        last.then_inc(S["up_ready"], 1)
                if Y:
                    pe.wait_ge(S["split_steps"], Y.n * 2 + 2)
                    ge(pe, S["y_ready"], Y.n - 1)
                    for t in range(BT):
                        for c in range(NC):
                            for n, (hq, wq) in enumerate(((0, 0), (0, 1), (1, 0))):
                                w = W2h[:, wq, bass.ds(ey, 1), c, :].rearrange("p e d -> p (e d)")
                                last = mm(Yp[Y.p][:, t, :], hp[:, Y.p, hq, c, t * P:(t + 1) * P], w,
                                          start=(c == 0 and n == 0), stop=(c == NC - 1 and n == 2))
                    last.then_inc(S["down_ready"], 1)
            pe.wait_ge(S["tab_ready"], 1)
            steps(pe, layers)


_INS = ["x", "adj", "L0_gnn_W", "L0_gnn_a", "L0_ffn_Wg", "L0_ffn_bg", "L0_ffn_W1", "L0_ffn_b1", "L0_ffn_W2", "L0_ffn_b2"]


def kernel(**inputs):
    import numpy as np
    import concourse.bacc as bacc
    from concourse.bass_utils import run_bass_kernel_spmd

    nc = bacc.Bacc("TRN2", target_bir_lowering=False, num_devices=1)
    arrays, args = {}, []
    for name in _INS:
        arr = np.ascontiguousarray(inputs[name])
        arrays[f"in_{name}"] = arr
        args.append(nc.dram_tensor(f"in_{name}", arr.shape, mybir.dt.from_np(arr.dtype), kind="ExternalInput").ap())
    arrays["in_const"] = constants(np)
    args.append(nc.dram_tensor("in_const", (P, NCONST), F32, kind="ExternalInput").ap())
    args.append(nc.dram_tensor("out_0", (NB, N, D), F32, kind="ExternalOutput").ap())
    build(nc, *args)
    r = run_bass_kernel_spmd(nc, [arrays], core_ids=[0])
    return r.results[0]["out_0"]
```

```python
from contextlib import ExitStack

import concourse.bass as bass
from concourse import mybir

ALU = mybir.AluOpType
ACT = mybir.ActivationFunctionType
AX = mybir.AxisListType
F32 = mybir.dt.float32
BF16 = mybir.dt.bfloat16
FP16 = mybir.dt.float16
I32 = mybir.dt.int32

P = 128
NB = 16
N = 512
D = 128
NT = N // P
H = 4
HD = D // H
E = 8
HID = 512
NC = HID // P
TOK = NB * N
TILES = TOK // P
EPS = 1e-5
SLOPE = 0.2
SHIFT = 60.0
VW = 2 * (HD + 1)
BLK = 256
BT = BLK // P
CAP = TOK + BLK
BLOCKS = 2 * TOK // BLK + E - 1
TAB = BLOCKS + 1
XS_ROWS = E * CAP + BLK
ROW = D + 2
XSCALE = 1024.0

C_ID, C_TRI, C_SEL, C_MASK, C_REV, C_BASE, C_TOK, C_IOTA, C_HALF, C_ONE = range(10)
_W = [P, P, H * P, H, E, E, TILES, TAB, NT, P]
_O = [sum(_W[:k]) for k in range(len(_W))]
NCONST = sum(_W)


def constants(np):
    c = np.zeros((P, NCONST), np.float32)
    r = np.arange(P)

    def put(k, v):
        c[:, _O[k]:_O[k] + _W[k]] = v

    put(C_ID, np.eye(P))
    put(C_TRI, r[:, None] < r[None, :])
    for h in range(H):
        for part in range(3):
            c[8 * part + H + h, _O[C_SEL] + h * P:_O[C_SEL] + (h + 1) * P] = 1
    put(C_MASK, (r[:, None] // HD) == np.arange(H)[None, :])
    put(C_REV, E - np.arange(E)[None, :])
    put(C_BASE, np.arange(E)[None, :] * CAP)
    put(C_TOK, np.arange(TILES)[None, :] * P + r[:, None])
    put(C_IOTA, np.arange(TAB)[None, :])
    put(C_HALF, -0.5)
    put(C_ONE, 1.0)
    return c


class Batch:

    def __init__(self, base, i=None, unroll=2):
        self.p, self.q = base % 2, base % 4
        if i is None:
            self.n, self.h, self.f = base, base // 2, base // 4
        else:
            self.n, self.h = i * unroll + base, i * (unroll // 2) + base // 2
            self.f = i + base // 4


def ge(eng, sem, value):
    if isinstance(value, int) and value <= 0:
        return
    eng.wait_ge(sem, value)


def hold(eng, sem, value, turns):
    if isinstance(value, int) and value <= 0:
        return
    eng.wait_ge(sem, value)
    eng.sem_inc(turns, 1)


class Chain:

    def __init__(self, eng, sem, per, n):
        self.eng, self.sem, self.per, self.n, self.k = eng, sem, per, n, 0

    def did(self, ins):
        self.k += 1
        ins.then_inc(self.sem, 1)

    def now(self):
        return self.n * self.per + self.k

    def wait(self):
        self.eng.wait_ge(self.sem, self.now())

    def after(self, k):
        self.eng.wait_ge(self.sem, self.n * self.per + k)


FAR = 1e30
ACT_HEADS = H - 1
FILLS = ACT_HEADS * NT
LN_STEPS, S_STEPS, MX_STEPS, ARG_STEPS, X_STEPS, ATT_STEPS, RT_STEPS = 8, 4, 2, 6, 4, 4, 24
RT_SEL, RT_DM = 13, 14


def build(nc, x, adj, W, a, Wg, bg, W1, b1, W2, b2, const, out):
    with ExitStack() as ctx:
        def sb(name, shape, dt=F32):
            return ctx.enter_context(nc.sbuf_tensor(name, shape, dt))

        def ps(name, shape, dt=F32):
            return ctx.enter_context(nc.psum_tensor(name, shape, dt))

        def sem(name):
            return ctx.enter_context(nc.semaphore(name))

        xs = nc.dram_tensor("expert_rows", [XS_ROWS, ROW], F32, kind="Internal").ap()
        ybuf = nc.dram_tensor("expert_out", [2 * TOK, D], F32, kind="Internal").ap()

        cst = sb("cst", [P, NCONST])

        def C(k, rows=P):
            return cst[0:rows, _O[k]:_O[k] + _W[k]]

        ident = C(C_ID)
        identb = sb("identb", [P, P], BF16)
        identh = sb("identh", [P, P], FP16)
        trib = sb("trib", [P, P], BF16)
        onesb = sb("onesb", [P, P], BF16)
        negb = sb("negb", [P, P], BF16)
        selb = sb("selb", [24, H * P], BF16)
        xr = sb("xr", [P, TILES, D])
        adji = sb("adji", [P, 2, NT, N], I32)
        away = sb("away", [P, NT, N], BF16)
        thr = sb("thr", [P, 2, NT, N], BF16)
        adjn = sb("adjn", [P, 2, NT, N], BF16)
        G = sb("G", [P, 2, H, NT, N], BF16)
        mv1 = sb("mv1", [P, NT, 2])
        bs1 = sb("bs1", [P, NT, 6])
        rs1 = sb("rs1", [P, NT])
        nb1 = sb("nb1", [P, NT])
        xn = sb("xn", [P, NT, D])
        xnT = sb("xnT", [P, N])
        s3 = sb("s3", [P, NT, 3, 8])
        s2c = sb("s2c", [P, 2, NT, H])
        rows = sb("rows", [24, 2, N], BF16)
        mx = sb("mx", [H, 1])
        diag = sb("diag", [H, H])
        arg = sb("arg", [P, 4, NT, H])
        zt = sb("zt", [P, NT, H])
        Mt = sb("Mt", [P, NT, H])
        Ex = sb("Ex", [P, 2, 4, NT, H])
        V = sb("V", [P, 2, 2, NT, H, VW])
        V3 = sb("V3", [P, 2, NT, H, VW], BF16)
        T = sb("T", [P, NT, H, 2, HD + 1])
        rec = sb("rec", [P, NT, H])
        att = sb("att", [P, NT, D])
        mv2 = sb("mv2", [P, NT, 2])
        bs2 = sb("bs2", [P, NT, 6])
        rs2 = sb("rs2", [P, NT])
        nb2 = sb("nb2", [P, NT])
        xn2 = sb("xn2", [P, NT, D])
        xn2T = sb("xn2T", [P, N])
        g8 = sb("g8", [P, NT, E])
        m01 = sb("m01", [P, 2, NT])
        v01 = sb("v01", [P, 2, NT])
        eq = sb("eq", [P, NT, E])
        cand = sb("cand", [P, NT, E])
        OH = sb("OH", [P, 2, NT, E])
        g2 = sb("g2", [P, NT, E])
        sel = sb("sel", [P, NT, E], BF16)
        dm = sb("dm", [P, NT])
        ed = sb("ed", [P, NT])
        den = sb("den", [P, NT])
        PR = sb("PR", [P, 2, TILES])
        pos = sb("pos", [P, NT, E])
        carry = sb("carry", [P, E])
        prod = sb("prod", [P, 2, NT, E])
        slotf = sb("slotf", [P, 2, NT])
        idx = sb("idx", [P, 2, 2, NT], I32)
        rowt = sb("rowt", [P, 2, NT, ROW])
        Wr = sb("Wr", [P, D])
        WT = sb("WT", [P, D])
        acol = sb("acol", [P, 2])
        Am = sb("Am", [P, 2 * H])
        Wa = sb("Wa", [P, 2 * H])
        Wgr = sb("Wgr", [E, D])
        WgT = sb("WgT", [P, E])
        bgb = sb("bgb", [P, E])
        b1r = sb("b1r", [E * NC, P])
        b1s = sb("b1s", [P, E * NC])
        b2b = sb("b2b", [P, E, D])
        W1h = sb("W1h", [P, 2, E, HID], FP16)
        W2h = sb("W2h", [P, 2, E, NC, D], FP16)
        sc = sb("sc", [P, 16])
        Gf = G[:, :, :, :, :].rearrange("p a h t n -> p (a h t n)").bitcast(F32)
        W1r = Gf[:, 0:E * NC * D].rearrange("p (t d) -> p t d", d=D)
        W2r = Gf[:, E * NC * D:2 * E * NC * D].rearrange("p (e h) -> p e h", h=HID)
        tf = sb("tf", [P, 8, TAB])
        cube = sb("cube", [P, TAB, E])
        cnt = sb("cnt", [P, 6, E])
        cnti = sb("cnti", [P, 2, E], I32)
        tab = sb("tab", [P, 2, TAB], I32)
        padrow = sb("padrow", [P, BT, ROW])
        h32 = Gf[:, 0:2 * NC * BLK].rearrange("p (a c n) -> p a c n", a=2, c=NC)
        hp = G[:, :, :, :, :].rearrange("p a h t n -> p (a h t n)")[:, 4 * NC * BLK:8 * NC * BLK] \
            .bitcast(FP16).rearrange("p (a q c n) -> p a q c n", a=2, q=2, c=NC)
        xb = sb("xb", [P, 4, BT, ROW])
        xt = sb("xt", [P, 2, 2, BLK], FP16)
        ysb = sb("ysb", [P, 4, BT, D])
        bk = sb("bk", [P, 2, BT])
        bidx = sb("bidx", [P, 4, BT], I32)
        yin = adji[:, :, :, :].rearrange("p a t n -> p (a t n)").bitcast(F32) \
            .rearrange("p (b k t d) -> p b k t d", b=4, k=2, d=D)

        bank = [ps(f"bank{k}", [P, 512]) for k in range(8)]
        zb = [bank[0], bank[1]]
        hb = bank[6]
        Ob = [bank[2], bank[3]]
        TR = bank[4]
        HP = bank[5]
        MS = bank[7]
        AD = bank[4][:, :].bitcast(BF16).rearrange("p (a n) -> p a n", a=2)
        s12p = MS[:, 0:32].rearrange("p (t c) -> p t c", c=8)
        Sp = MS[:, 32:36]
        gp = TR[:, 0:32].rearrange("p (t e) -> p t e", e=E)
        rkp = MS[:, 96:128].rearrange("p (t e) -> p t e", e=E)
        totp = MS[:, 128:136]
        rowp = MS[0:24, 256:512].bitcast(BF16)
        Vhi = V[:, :, :, :, :, :].rearrange("p a q t h v -> p (a q t h v)").bitcast(BF16) \
            .rearrange("p (a q t h v w) -> p a q t h v w", a=2, q=2, t=NT, h=H, w=2)[:, :, :, :, :, :, 1]
        s3hi = s3[:, :, :, :].rearrange("p t q c -> p (t q c)").bitcast(BF16) \
            .rearrange("p (t q c w) -> p t q c w", t=NT, q=3, w=2)[:, :, :, :, 1]
        Up = [[bank[0], bank[1]], [bank[2], bank[3]]]
        XTp = [bank[4][:, :].bitcast(FP16)[:, 0:2 * BLK].rearrange("p (q n) -> p q n", q=2),
               bank[5][:, :].bitcast(FP16)[:, 0:2 * BLK].rearrange("p (q n) -> p q n", q=2)]
        Yp = [bank[6][:, 0:BT * D].rearrange("p (t d) -> p t d", d=D),
              bank[7][:, 0:BT * D].rearrange("p (t d) -> p t d", d=D)]

        names = """ld_const ld_small ld_w1 ld_w2 ld_x0 ld_x1 ld_adj0 ld_adj1
            const_ready prep_step prep_pe prep_act w_pe w_act w_dve scale_ready small_ready
            ln1 rstd1 nb1_ready xn_ready xT_ready xnT_ready h_ready s_steps sT_ready rows_ready mx_steps S_ready
            arg_steps exp_ready v_steps rest_ready part3_ready
            adj_cast awayT_ready thr_ready adjn_ready z_ready z_used bc_ready gh_ready g_ready
            o_ready t_steps sum_ready att_steps x1_ready
            ln2 rstd2 nb2_ready xn2_ready x2T_ready xn2T_ready gate_ready rt_steps ed_ready rank_ready
            hi_ready lo_ready scattered0 scattered1 tab_steps tab_ready padded pads_ready
            ld_rows0 ld_rows1 ld_rows2 ld_rows3 bt_ready xt_ready up_ready hid_ready split_steps down_ready y_ready
            bidx_steps back0 back1 back2 back3 ld_y0 ld_y1 ld_y2 ld_y3 o1_steps final_ready stored0 stored1 stored2 stored3 pool_turns dve_turns"""
        S = {n: sem(n) for n in names.split()}
        ld_adj = [S["ld_adj0"], S["ld_adj1"]]
        scattered = [S["scattered0"], S["scattered1"]]
        ld_rows = [S[f"ld_rows{k}"] for k in range(4)]
        back = [S[f"back{k}"] for k in range(4)]
        ld_y = [S[f"ld_y{k}"] for k in range(4)]
        stored = [S[f"stored{k}"] for k in range(4)]

        xd = x.rearrange("b (t p) d -> p (b t) d", p=P)
        outd = out.rearrange("b (t p) d -> p (b t) d", p=P)
        adjd = adj.rearrange("b (t p) m -> b p t m", p=P)
        yd = ybuf.rearrange("(k t p) d -> p k t d", k=2, p=P)
        XSPLIT = 3 * NT
        SMALL = 8

        def slots(eng, body, last, first=-1):
            for s in range(first, 4):
                body(lambda k, s=s: Batch(s + k) if 0 <= s + k < NB else None)
            with eng.Fori(0, 5) as i:
                for u in range(2):
                    body(lambda k, u=u: Batch(4 + u + k, i))
            for s in range(14, last + 1):
                body(lambda k, s=s: Batch(s + k) if 0 <= s + k < NB else None)

        def blocks(eng, body):
            for k in range(4):
                body(Batch(k))
            with eng.Fori(0, BLOCKS // 4 - 1) as i:
                for k in range(4):
                    body(Batch(4 + k, i, 4))
            for k in range(BLOCKS // 4 * 4, BLOCKS):
                body(Batch(k))

        def steps(eng, body):
            def fixed(s):
                return lambda k: Batch(s + k) if 0 <= s + k < BLOCKS else None
            for s in range(-2, 2):
                body(fixed(s))
            with eng.Fori(0, (BLOCKS - 4) // 4) as i:
                for u in range(4):
                    body(lambda k, u=u: Batch(2 + u + k, i, 4))
            for s in range(2 + (BLOCKS - 4) // 4 * 4, BLOCKS):
                body(fixed(s))

        block = ctx.enter_context(nc.Block())

        @block.sync
        def _(sp):
            sp.dma_start(cst[:, :], const).then_inc(S["ld_const"], 16)
            sp.dma_start(Wr[:, :], W).then_inc(S["ld_small"], 16)
            for k in range(2):
                for h in range(H):
                    lo = HD * (1 - k)
                    sp.dma_start(acol[HD * h:HD * (h + 1), k:k + 1],
                                 a[h:h + 1, lo:lo + HD].rearrange("h d -> d h")).then_inc(S["ld_small"], 16)
            sp.dma_start(Wgr[:, :], Wg).then_inc(S["ld_small"], 16)
            sp.dma_start(b1r[:, :], b1.rearrange("e (c p) -> (e c) p", p=P)).then_inc(S["ld_small"], 16)
            sp.dma_start(xr[:, 0:XSPLIT, :], xd[:, 0:XSPLIT, :]).then_inc(S["ld_x0"], 16)
            sp.dma_start(W1r, W1.rearrange("e (c p) d -> p (e c) d", p=P)).then_inc(S["ld_w1"], 16)
            sp.dma_start(W2r, W2.rearrange("e d h -> d e h")).then_inc(S["ld_w2"], 16)

            def load_adj(B):
                ge(sp, S["adj_cast"], B.n - 1)
                sp.dma_start(adji[:, B.p], adjd[bass.ds(B.n, 1)].rearrange("b p t m -> p (b t) m")) \
                  .then_inc(ld_adj[B.p], 16)
            load_adj(Batch(0))
            load_adj(Batch(1))
            sp.dma_start(xr[:, XSPLIT:TILES, :], xd[:, XSPLIT:TILES, :]).then_inc(S["ld_x1"], 16)
            with sp.Fori(0, (NB - 2) // 2) as i:
                load_adj(Batch(2, i))
                load_adj(Batch(3, i))

            sp.wait_ge(S["tab_ready"], 1)
            for e in range(E):
                r = sp.value_load(cnti[0:1, 0, e:e + 1], min_val=e * CAP, max_val=e * CAP + TOK)
                sp.dma_start(xs[bass.ds(r, BLK), :].rearrange("(t p) w -> p t w", p=P), padrow[:, :, :]) \
                  .then_inc(S["pads_ready"], 16)
            sp.dma_start(xs[E * CAP:E * CAP + BLK, :].rearrange("(t p) w -> p t w", p=P), padrow[:, :, :]) \
              .then_inc(S["pads_ready"], 16)
            sp.wait_ge(S["pads_ready"], 16 * (E + 1))
            sp.wait_ge(scattered[0], 16 * 2 * NT * NB // 2)
            sp.wait_ge(scattered[1], 16 * 2 * NT * NB // 2)

            def load_rows(B):
                ge(sp, S["bt_ready"], B.n - 3)
                ge(sp, S["bidx_steps"], B.n * 2 - 6)
                r = sp.value_load(tab[0:1, 0, bass.ds(B.n, 1)], min_val=0, max_val=E * CAP)
                sp.dma_start(xb[:, B.q], xs[bass.ds(r, BLK), :].rearrange("(t p) w -> p t w", p=P)) \
                  .then_inc(ld_rows[B.q], 16)
            blocks(sp, load_rows)

            for k in range(4):
                sp.wait_ge(back[k], 16 * BT * ((BLOCKS + 3 - k) // 4))

            def load_y(n, q, k):
                ge(sp, stored[k], q * 16)
                for c in range(2):
                    sp.dma_start(yin[:, k, c], yd[:, c, bass.ds(n * NT, NT), :]).then_inc(ld_y[k], 16)
            for k in range(4):
                load_y(k, 0, k)
            with sp.Fori(1, 4) as q:
                for k in range(4):
                    load_y(q * 4 + k, q, k)
            for k in range(4):
                sp.wait_ge(stored[k], 16 * 4)

        @block.gpsimd
        def _(pool):
            def rstd(name, mv, rs, B, ready):
                hold(pool, ready, B.n * LN_STEPS + LN_STEPS, S["pool_turns"])
                c = Chain(pool, S[name], 2, B.n)
                c.did(pool.tensor_scalar(rs[:, :], mv[:, :, 1], 1.0, EPS, ALU.mult, ALU.add))
                hold(pool, S[name], c.now(), S["pool_turns"])
                c.did(pool.tensor_tensor(rs[:, :], rs[:, :], C(C_HALF), ALU.pow))

            def scatter(Z, js):
                if js[0] == 0:
                    hold(pool, S["rt_steps"], Z.n * RT_STEPS + RT_STEPS, S["pool_turns"])
                    hold(pool, S["hi_ready"], Z.n + 1, S["pool_turns"])
                    hold(pool, S["lo_ready"], Z.n + 1, S["pool_turns"])
                for j in js:
                    for k in range(2):
                        pool.indirect_dma_start(
                            xs, bass.IndirectOffsetOnAxis(ap=idx[:, Z.p, k, j:j + 1], axis=0),
                            rowt[:, Z.p, j, :], None).then_inc(scattered[Z.p], 16)

            def residual(R, half):
                ts = slice(2 * half, 2 * half + 2)
                hold(pool, S["t_steps"], R.n * NT + 2 * half + 2, S["pool_turns"])
                pool.tensor_tensor(T[:, ts, :, 0, :], T[:, ts, :, 0, :], T[:, ts, :, 1, :], ALU.add) \
                    .then_inc(S["sum_ready"], 1)

            def add(R, half):
                hold(pool, S["att_steps"], R.n * ATT_STEPS + 2 * half + 2, S["pool_turns"])
                xh = xr[:, bass.ds(R.n * NT + 2 * half, 2), :]
                pool.tensor_tensor(xh, xh, att[:, 2 * half:2 * half + 2, :], ALU.add).then_inc(S["x1_ready"], 1)

            def body(at):
                L, M, R, Q, Z = at(2), at(0), at(-1), at(-2), at(-3)
                if Q:
                    add(Q, 1)
                if Z:
                    scatter(Z, [0])
                if Q:
                    hold(pool, S["xn2_ready"], Q.n * NT, S["pool_turns"])
                    hold(pool, S["nb2_ready"], Q.n, S["pool_turns"])
                    rstd("rstd2", mv2, rs2, Q, S["ln2"])
                if M:
                    hold(pool, S["v_steps"], M.n * X_STEPS + X_STEPS, S["pool_turns"])
                    hold(pool, S["o_ready"], (M.n - 1) * NT, S["pool_turns"])
                    pool.tensor_tensor(V[:, M.p, 1].rearrange("p t h v -> p (t h v)"),
                                       V[:, M.p, 0].rearrange("p t h v -> p (t h v)"),
                                       Vhi[:, M.p, 0].rearrange("p t h v -> p (t h v)"), ALU.subtract) \
                        .then_inc(S["rest_ready"], 1)
                if Z:
                    scatter(Z, [1])
                if R:
                    residual(R, 0)
                if Z:
                    scatter(Z, [2])
                if R:
                    add(R, 0)
                if L:
                    hold(pool, S["xn_ready"], L.n * NT, S["pool_turns"])
                    hold(pool, S["nb1_ready"], L.n, S["pool_turns"])
                    rstd("rstd1", mv1, rs1, L, S["ln1"])
                if Z:
                    scatter(Z, [3])
                if R:
                    residual(R, 1)

            hold(pool, S["ld_const"], 16, S["pool_turns"])
            pool.dma_start(b2b[:, :, :].rearrange("p e d -> p (e d)"),
                           b2.rearrange("e d -> (e d)").partition_broadcast(P)).then_inc(S["small_ready"], 16)
            pool.dma_start(bgb[:, :], bg.partition_broadcast(P)).then_inc(S["small_ready"], 16)
            slots(pool, body, 18, -2)

            def send(B):
                hold(pool, S["bidx_steps"], B.n * 2 + 2, S["pool_turns"])
                hold(pool, S["y_ready"], B.n + 1, S["pool_turns"])
                for t in range(BT):
                    pool.indirect_dma_start(
                        ybuf, bass.IndirectOffsetOnAxis(ap=bidx[:, B.q, t:t + 1], axis=0),
                        ysb[:, B.q, t, :], None, bounds_check=2 * TOK - 1, oob_is_err=False) \
                        .then_inc(back[B.q], 16)
            blocks(pool, send)

        @block.scalar
        def _(act):
            act.wait_ge(S["scale_ready"], 1)
            for u in range(2 * E):
                act.wait_ge(S["w_pe"], u + 1)
                dst = W1h[:, 0, u, :] if u < E else W2h[:, 0, u - E, :, :].rearrange("p c d -> p (c d)")
                act.activation(dst, bank[u % 4][:, :], ACT.Copy,
                               scale=sc[:, 3:4] if u < E else sc[:, 7:8]).then_inc(S["w_act"], 1)

            def relu(M, ks):
                for k in ks:
                    h, mt = k // NT, k % NT
                    act.wait_ge(S["z_ready"], M.n * FILLS + k + 1)
                    if k == 0:
                        act.wait_ge(S["s_steps"], M.n * S_STEPS + S_STEPS)
                        ge(act, S["o_ready"], (M.n - 1) * NT)
                    act.activation(G[:, M.p, h, mt, :], zb[k % 2][:, :], ACT.Relu,
                                   bias=s2c[:, M.p, mt, h:h + 1]).then_inc(S["z_used"], 1)

            def normalise(dst, src, rs, nb, ready):
                for j in range(NT):
                    act.activation(dst[:, j, :], src[:, j, :], ACT.Identity, bias=nb[:, j:j + 1],
                                   scale=rs[:, j:j + 1]).then_inc(ready, 1)

            def body(at):
                F, M, Q = at(1), at(0), at(-2)
                if F:
                    act.wait_ge(S["nb1_ready"], F.n + 1)
                    ge(act, S["xT_ready"], F.n)
                    normalise(xn, xr[:, bass.ds(F.n * NT, NT), :], rs1, nb1, S["xn_ready"])
                if M:
                    relu(M, [0, 1])
                    act.wait_ge(S["arg_steps"], M.n * ARG_STEPS + ARG_STEPS)
                    ge(act, S["t_steps"], (M.n - 1) * NT)
                    act.activation(Ex[:, M.p], arg[:, :, :, :], ACT.Exp).then_inc(S["exp_ready"], 1)
                if F:
                    act.wait_ge(S["xT_ready"], F.n + 1)
                    ge(act, S["h_ready"], F.n)
                    act.activation(xnT[:, :], TR[:, :], ACT.Copy).then_inc(S["xnT_ready"], 1)
                if M:
                    relu(M, [2, 3])
                if Q:
                    act.wait_ge(S["nb2_ready"], Q.n + 1)
                    ge(act, S["x2T_ready"], Q.n)
                    ge(act, S["lo_ready"], Q.n)
                    normalise(xn2, xr[:, bass.ds(Q.n * NT, NT), :], rs2, nb2, S["xn2_ready"])
                if M:
                    relu(M, [4])
                if Q:
                    act.wait_ge(S["x2T_ready"], Q.n + 1)
                    ge(act, S["gate_ready"], Q.n)
                    act.activation(xn2T[:, :], TR[:, :], ACT.Copy).then_inc(S["xn2T_ready"], 1)
                if M:
                    relu(M, [5])
                if F:
                    act.wait_ge(S["sT_ready"], F.n + 1)
                    ge(act, S["z_ready"], (F.n - 1) * FILLS)
                    ge(act, S["bc_ready"], F.n - 1)
                    ge(act, S["mx_steps"], (F.n - 1) * MX_STEPS)
                    act.activation(rows[:, F.p, :], rowp, ACT.Copy).then_inc(S["rows_ready"], 1)
                if M:
                    relu(M, [6])
                if Q:
                    act.wait_ge(S["xn2_ready"], Q.n * NT + NT)
                    ge(act, scattered[Q.p], Q.h * 16 * 2 * NT)
                    act.activation(rowt[:, Q.p, :, 0:D // 2].bitcast(FP16), xn2[:, :, :], ACT.Copy,
                                   scale=XSCALE).then_inc(S["hi_ready"], 1)
                for g in range(2):
                    if M:
                        relu(M, [7 + g])
                    if F:
                        act.wait_ge(S["awayT_ready"], F.n * 2 + g + 1)
                        if g == 0:
                            ge(act, S["z_ready"], (F.n - 1) * FILLS)
                            ge(act, S["gh_ready"], (F.n - 1) * NT)
                            ge(act, S["adjn_ready"], F.n - 1)
                        act.activation(thr[:, F.p, 2 * g:2 * g + 2, :], AD[:, :, 0:N], ACT.Copy) \
                           .then_inc(S["thr_ready"], 1)
                if M:
                    relu(M, [9, 10])
                if Q:
                    act.wait_ge(S["rt_steps"], Q.n * RT_STEPS + RT_DM)
                    act.activation(ed[:, :], dm[:, :], ACT.Exp).then_inc(S["ed_ready"], 1)
                if M:
                    relu(M, [11])
            slots(act, body, 17)

            def hidden(at):
                X, U = at(2), at(1)
                if X:
                    act.wait_ge(S["bt_ready"], X.n + 1)
                    ge(act, S["up_ready"], (X.n - 1) * NC)
                    act.activation(xt[:, X.p], XTp[X.p], ACT.Copy).then_inc(S["xt_ready"], 1)
                if U:
                    ge(act, S["split_steps"], (U.n - 1) * 2)
                    ex = act.value_load(tab[0:1, 1, bass.ds(U.n, 1)], min_val=0, max_val=E - 1)
                    for c in range(NC):
                        if c % 2 == 0:
                            act.wait_ge(S["up_ready"], U.n * NC + c + 2)
                        act.activation(h32[:, U.p, c, :], Up[U.p][c // 2][:, (c % 2) * BLK:(c % 2 + 1) * BLK],
                                       ACT.Relu, bias=b1s[:, bass.ds(ex * NC + c, 1)], scale=sc[:, 10:11]) \
                           .then_inc(S["hid_ready"], 1)
            act.wait_ge(S["tab_ready"], 1)
            steps(act, hidden)

            def store(n, q, k):
                act.wait_ge(S["final_ready"], n * NT + NT)
                act.dma_start(outd[:, bass.ds(n * NT, NT), :], yin[:, k, 1]).then_inc(stored[k], 16)
            with act.Fori(0, 4) as q:
                for k in range(4):
                    store(q * 4 + k, q, k)
            for k in range(4):
                act.wait_ge(stored[k], 16 * 4)

        @block.vector
        def _(dve):
            dve.wait_ge(S["ld_const"], 16)
            for dst, src in ((identb, ident), (identh, ident), (trib, C(C_TRI)), (onesb, C(C_ONE)),
                             (selb, C(C_SEL, 24))):
                dve.tensor_copy(dst[:, :], src).then_inc(S["const_ready"], 1)
            dve.tensor_scalar(negb[:, :], ident, -1.0, None, ALU.mult).then_inc(S["const_ready"], 1)
            dve.tensor_copy(carry[:, :], C(C_BASE)).then_inc(S["const_ready"], 1)
            dve.memset(padrow[:, :, 0:D], 0.0).then_inc(S["const_ready"], 1)
            dve.memset(padrow[:, :, D:D + 1], float(2 * TOK)).then_inc(S["const_ready"], 1)
            dve.memset(padrow[:, :, D + 1:D + 2], 0.0).then_inc(S["const_ready"], 1)
            dve.wait_ge(S["const_ready"], 10)

            dve.wait_ge(S["ld_small"], 16 * (2 * H + 3))
            k = Chain(dve, S["prep_step"], 0, 0)
            k.did(dve.tensor_scalar(Am[:, 0:H], C(C_MASK), acol[:, 0:1], None, ALU.mult))
            k.did(dve.tensor_scalar(Am[:, H:2 * H], C(C_MASK), acol[:, 1:2], None, ALU.mult))
            dve.wait_ge(S["prep_pe"], 1)
            k.did(dve.tensor_copy(WT[:, :], bank[4][:, 0:D]))
            k.did(dve.tensor_copy(WgT[:, :], bank[5][:, 0:E]))
            k.did(dve.tensor_copy(b1s[:, :], bank[6][:, 0:E * NC]))
            dve.wait_ge(S["prep_pe"], 2)
            k.did(dve.tensor_copy(Wa[:, :], bank[4][:, D:D + 2 * H]))
            dve.wait_ge(S["ld_w1"], 16)
            k.did(dve.tensor_reduce(sc[:, 0:1], W1r, AX.XY, ALU.max, apply_absolute_value=True))
            dve.wait_ge(S["ld_w2"], 16)
            k.did(dve.tensor_reduce(sc[:, 1:2], W2r, AX.XY, ALU.max, apply_absolute_value=True))
            k.wait()
            k.did(dve.tensor_reduce(sc[:, 2:3], b1s[:, :], AX.X, ALU.max, apply_absolute_value=True))
            dve.wait_ge(S["prep_pe"], 3)
            k.did(dve.tensor_reduce(tf[0:1, 0, 0:1], bank[5][0:1, 128:256], AX.X, ALU.max))
            k.did(dve.tensor_reduce(tf[0:1, 0, 1:2], bank[5][0:1, 256:384], AX.X, ALU.max))
            k.did(dve.tensor_reduce(tf[0:1, 0, 2:3], bank[5][0:1, 384:512], AX.X, ALU.max))
            dve.wait_ge(S["prep_pe"], 4)
            k.did(dve.tensor_scalar(sc[:, 0:1], bank[4][:, 256:257], 1e-20, None, ALU.max))
            k.did(dve.tensor_scalar(sc[:, 1:2], bank[4][:, 257:258], 1e-20, None, ALU.max))
            k.wait()
            k.did(dve.scalar_tensor_tensor(sc[:, 2:3], sc[:, 0:1], 128.0, bank[4][:, 258:259], ALU.mult, ALU.add))
            k.wait()
            k.did(dve.tensor_scalar(sc[:, 4:7].bitcast(I32), sc[:, 0:3].bitcast(I32), 0x7F800000, None,
                                    ALU.bitwise_and))
            k.wait()
            k.did(dve.reciprocal(sc[:, 12:15], sc[:, 4:7]))
            k.wait()
            k.did(dve.tensor_scalar(sc[:, 3:4], sc[:, 12:13], 2.0 ** 13, None, ALU.mult))
            k.did(dve.tensor_scalar(sc[:, 7:8], sc[:, 13:14], 2.0 ** 13, None, ALU.mult))
            k.did(dve.tensor_scalar(sc[:, 8:9], sc[:, 14:15], 2.0 ** 13, None, ALU.mult))
            k.did(dve.tensor_scalar(sc[:, 9:10], sc[:, 4:5], 2.0 ** -13 / XSCALE, None, ALU.mult))
            k.did(dve.tensor_scalar(sc[:, 11:12], sc[:, 6:7], 2.0 ** -13, None, ALU.mult))
            k.did(dve.tensor_scalar(sc[:, 15:16], sc[:, 5:6], 2.0 ** -13, None, ALU.mult))
            k.wait()
            k.did(dve.tensor_tensor(sc[:, 10:11], sc[:, 9:10], sc[:, 8:9], ALU.mult))
            k.did(dve.tensor_tensor(sc[:, 11:12], sc[:, 11:12], sc[:, 15:16], ALU.mult))
            k.did(dve.tensor_scalar(b1s[:, :], b1s[:, :], sc[:, 8:9], None, ALU.mult))
            k.wait()
            dve.sem_inc(S["scale_ready"], 1)
            for u in range(2 * E):
                dve.wait_ge(S["w_act"], u + 1)
                part = [(W1h[:, q, u, :] if u < E else W2h[:, q, u - E, :, :].rearrange("p c d -> p (c d)"))
                        for q in range(2)]
                dve.scalar_tensor_tensor(part[1], bank[u % 4][:, :], sc[:, 3:4] if u < E else sc[:, 7:8],
                                         part[0], ALU.mult, ALU.subtract).then_inc(S["w_dve"], 1)

            def stats(c, src, bs, mv, js):
                for j in js:
                    c.did(dve.bn_stats(bs[:, j, :], src[:, j, :]))
                hold(dve, c.sem, c.now(), S["dve_turns"])
                for j in js:
                    c.did(dve.bn_aggr(mv[:, j, :], bs[:, j, :]))

            def shift(nb, mv, rs, rstd_ready, nb_ready, used, B):
                dve.wait_ge(rstd_ready, B.n * 2 + 2)
                ge(dve, used, B.n * NT)
                dve.scalar_tensor_tensor(nb[:, :], mv[:, :, 0], -1.0, rs[:, :], ALU.mult, ALU.mult).then_inc(nb_ready, 1)

            def mask(M, mt):
                dve.wait_ge(S["bc_ready"], M.n + 1)
                if mt == 0:
                    dve.wait_ge(S["thr_ready"], M.n * 2 + 2)
                    dve.wait_ge(S["s_steps"], M.n * S_STEPS + S_STEPS)
                    ge(dve, S["o_ready"], (M.n - 1) * NT)
                dve.scalar_tensor_tensor(G[:, M.p, H - 1, mt, :], hb[:, :], s2c[:, M.p, mt, H - 1:H],
                                         thr[:, M.p, mt, :], ALU.add, ALU.is_gt).then_inc(S["gh_ready"], 1)

            def binary(M, h):
                dve.wait_ge(S["z_used"], M.n * FILLS + (h + 1) * NT)
                g = G[:, M.p, h].rearrange("p t n -> p (t n)")
                dve.tensor_scalar(g, g, 0.0, None, ALU.is_gt).then_inc(S["g_ready"], 1)

            def scaled_sums(R, nt):
                dve.wait_ge(S["o_ready"], R.n * NT + nt + 1)
                if nt == 0:
                    dve.wait_ge(S["exp_ready"], R.n + 1)
                ge(dve, S["sum_ready"], R.n * 2 - 1 + nt // 2)
                ge(dve, S["att_steps"], R.n * ATT_STEPS)
                f = Ex[:, R.p, 2:4, nt, :].rearrange("p q h -> p h q").unsqueeze(3).to_broadcast([P, H, 2, HD + 1])
                dve.tensor_tensor(T[:, nt], Ob[nt % 2][:, 0:H * VW].rearrange("p (h q v) -> p h q v", q=2, v=HD + 1),
                                  f, ALU.mult).then_inc(S["t_steps"], 1)

            def attention(R, half):
                c = Chain(dve, S["att_steps"], ATT_STEPS, R.n)
                c.k = 2 * half
                ts = slice(2 * half, 2 * half + 2)
                dve.wait_ge(S["sum_ready"], R.n * 2 + half + 1)
                ge(dve, S["x1_ready"], R.n * 2)
                c.did(dve.reciprocal(rec[:, ts, :], T[:, ts, :, 0, HD]))
                c.wait()
                c.did(dve.tensor_tensor(
                    att[:, ts, :].rearrange("p t (h d) -> p t h d", d=HD), T[:, ts, :, 0, 0:HD],
                    rec[:, ts, :].unsqueeze(3).to_broadcast([P, 2, H, HD]), ALU.mult))

            def stats2(B, js):
                c = Chain(dve, S["ln2"], LN_STEPS, B.n)
                c.k = 2 * js[0]
                stats(c, xr[:, bass.ds(B.n * NT, NT), :], bs2, mv2, js)

            rev = C(C_REV).unsqueeze(1).to_broadcast([P, NT, E])

            def body(at):
                L, F, M, R, Q = at(2), at(1), at(0), at(-1), at(-2)
                if M:
                    ac = Chain(dve, S["arg_steps"], ARG_STEPS, M.n)
                    dve.wait_ge(S["S_ready"], M.n + 1)
                    ge(dve, S["exp_ready"], M.n)
                    Sb = Sp.unsqueeze(1).to_broadcast([P, NT, H])
                    s2, s1 = s3[:, :, 0, 0:H], s3[:, :, 0, H:2 * H]
                    ac.did(dve.scalar_tensor_tensor(arg[:, 0], s2, SHIFT, Sb, ALU.add, ALU.subtract))
                    ac.did(dve.tensor_tensor(zt[:, :, :], s1, Sb, ALU.add))
                    dve.wait_ge(S["thr_ready"], M.n * 2 + 2)
                    ge(dve, S["o_ready"], (M.n - 1) * NT)
                    dve.tensor_scalar(adjn[:, M.p], thr[:, M.p], 1.0, -1.0, ALU.is_lt, ALU.mult) \
                       .then_inc(S["adjn_ready"], 1)
                    ac.wait()
                    ac.did(dve.scalar_tensor_tensor(Mt[:, :, :], zt[:, :, :], SLOPE, zt[:, :, :], ALU.mult, ALU.max))
                    ac.did(dve.tensor_scalar(arg[:, 1], arg[:, 0], SLOPE, (1 - SLOPE) * SHIFT, ALU.mult, ALU.add))
                    ac.after(3)
                    ac.did(dve.tensor_tensor(arg[:, 2], zt[:, :, :], Mt[:, :, :], ALU.subtract))
                    ac.did(dve.scalar_tensor_tensor(arg[:, 3], zt[:, :, :], SLOPE, Mt[:, :, :], ALU.mult, ALU.subtract))
                if Q:
                    attention(Q, 1)
                if M:
                    mask(M, 0)
                    vc = Chain(dve, S["v_steps"], X_STEPS, M.n)
                    dve.wait_ge(S["exp_ready"], M.n + 1)
                    ge(dve, S["rest_ready"], M.n - 1)
                    h3 = HP[:, :].rearrange("p (g d) -> p g d", d=HD)
                    Vg = V[:, M.p, 0].rearrange("p t h v -> p (t h) v")
                    eB = Ex[:, M.p, 0].rearrange("p t h -> p (t h)")
                    eD = Ex[:, M.p, 1].rearrange("p t h -> p (t h)")
                    vc.did(dve.tensor_tensor(Vg[:, :, 0:HD], h3, eB.unsqueeze(2).to_broadcast([P, NT * H, HD]), ALU.mult))
                    vc.did(dve.scalar_tensor_tensor(Vg[:, :, HD + 1:2 * HD + 1], h3, -1.0,
                                                    eD.unsqueeze(2).to_broadcast([P, NT * H, HD]), ALU.mult, ALU.mult))
                    vc.did(dve.tensor_copy(Vg[:, :, HD], eB))
                    vc.did(dve.tensor_scalar(Vg[:, :, 2 * HD + 1], eD, -1.0, None, ALU.mult))
                if Q:
                    rt = Chain(dve, S["rt_steps"], RT_STEPS, Q.n)
                    dve.wait_ge(S["x1_ready"], Q.n * 2 + 2)
                    stats2(Q, [2, 3])
                if F:
                    dve.wait_ge(ld_adj[F.p], F.h * 16 + 16)
                    ge(dve, S["awayT_ready"], F.n * 2)
                    dve.tensor_scalar(away[:, :, :], adji[:, F.p], 0.0, FAR, ALU.is_equal, ALU.mult) \
                       .then_inc(S["adj_cast"], 1)
                if Q:
                    shift(nb2, mv2, rs2, S["rstd2"], S["nb2_ready"], S["xn2_ready"], Q)
                if R:
                    scaled_sums(R, 0)
                if M:
                    mask(M, 1)
                if F:
                    st = Chain(dve, S["s_steps"], S_STEPS, F.n)
                    dve.wait_ge(S["h_ready"], F.n + 1)
                    ge(dve, S["sT_ready"], F.n)
                    st.did(dve.tensor_copy(s3[:, :, 0, :], s12p))
                    ge(dve, S["z_used"], (F.n - 1) * FILLS)
                    st.did(dve.tensor_copy(s2c[:, F.p], s12p[:, :, 0:H]))
                    st.after(1)
                    st.did(dve.tensor_tensor(s3[:, :, 1, :], s3[:, :, 0, :], s3hi[:, :, 0, :], ALU.subtract))
                    st.wait()
                    st.did(dve.tensor_tensor(s3[:, :, 2, :], s3[:, :, 1, :], s3hi[:, :, 1, :], ALU.subtract))
                if M:
                    binary(M, 0)
                    mask(M, 2)
                    mask(M, 3)
                if R:
                    scaled_sums(R, 1)
                if Q:
                    dve.wait_ge(S["gate_ready"], Q.n + 1)
                    rt.did(dve.tensor_tensor(g8[:, :, :], gp, bgb[:, :].unsqueeze(1).to_broadcast([P, NT, E]), ALU.add))
                if F:
                    mc = Chain(dve, S["mx_steps"], MX_STEPS, F.n)
                    dve.wait_ge(S["rows_ready"], F.n + 1)
                    mc.did(dve.tensor_reduce(mx[:, :], rows[0:H, F.p, :], AX.X, ALU.max))
                if Q:
                    rt.wait()
                    rt.did(dve.tensor_reduce(m01[:, 0, :], g8[:, :, :], AX.X, ALU.max))
                if M:
                    dve.wait_ge(S["rest_ready"], M.n + 1)
                    dve.tensor_tensor(V3[:, M.p].rearrange("p t h v -> p (t h v)"),
                                      V[:, M.p, 1].rearrange("p t h v -> p (t h v)"),
                                      Vhi[:, M.p, 1].rearrange("p t h v -> p (t h v)"), ALU.subtract) \
                       .then_inc(S["part3_ready"], 1)
                if Q:
                    rt.wait()
                    rt.did(dve.tensor_tensor(eq[:, :, :], g8[:, :, :], m01[:, 0, :].unsqueeze(2).to_broadcast([P, NT, E]),
                                             ALU.is_equal))
                if F:
                    mc.wait()
                    ge(dve, S["S_ready"], F.n)
                    mc.did(dve.tensor_scalar(diag[:, :], C(C_ID, H)[:, 0:H], mx[:, 0:1], None, ALU.mult))
                if Q:
                    rt.wait()
                    rt.did(dve.tensor_tensor(cand[:, :, :], eq[:, :, :], rev, ALU.mult))
                if R:
                    attention(R, 0)
                if Q:
                    rt.wait()
                    rt.did(dve.tensor_reduce(v01[:, 0, :], cand[:, :, :], AX.X, ALU.max))
                if M:
                    binary(M, 1)
                if Q:
                    rt.wait()
                    rt.did(dve.tensor_tensor(OH[:, 0], rev, v01[:, 0, :].unsqueeze(2).to_broadcast([P, NT, E]),
                                             ALU.is_equal))
                if L:
                    if isinstance(L.n, int):
                        dve.wait_ge(S["ld_x0"], 16)
                        if L.n * NT >= XSPLIT:
                            dve.wait_ge(S["ld_x1"], 16)
                    l1 = Chain(dve, S["ln1"], LN_STEPS, L.n)
                    ge(dve, S["rstd1"], L.n * 2)
                    xl = xr[:, bass.ds(L.n * NT, NT), :]
                    stats(l1, xl, bs1, mv1, [0, 1])
                if Q:
                    rt.wait()
                    rt.did(dve.scalar_tensor_tensor(g2[:, :, :], OH[:, 0], -1e30, g8[:, :, :], ALU.mult, ALU.add))
                if L:
                    stats(l1, xl, bs1, mv1, [2, 3])
                if Q:
                    rt.wait()
                    rt.did(dve.tensor_reduce(m01[:, 1, :], g2[:, :, :], AX.X, ALU.max))
                if Q:
                    dve.wait_ge(S["hi_ready"], Q.n + 1)
                    dve.scalar_tensor_tensor(rowt[:, Q.p, :, D // 2:D].bitcast(FP16), xn2[:, :, :], XSCALE,
                                             rowt[:, Q.p, :, 0:D // 2].bitcast(FP16), ALU.mult, ALU.subtract) \
                       .then_inc(S["lo_ready"], 1)
                if Q:
                    rt.wait()
                    rt.did(dve.tensor_tensor(eq[:, :, :], g2[:, :, :], m01[:, 1, :].unsqueeze(2).to_broadcast([P, NT, E]),
                                             ALU.is_equal))
                if R:
                    scaled_sums(R, 2)
                if Q:
                    rt.wait()
                    rt.did(dve.tensor_tensor(cand[:, :, :], eq[:, :, :], rev, ALU.mult))
                if L:
                    shift(nb1, mv1, rs1, S["rstd1"], S["nb1_ready"], S["xn_ready"], L)
                if Q:
                    rt.wait()
                    rt.did(dve.tensor_reduce(v01[:, 1, :], cand[:, :, :], AX.X, ALU.max))
                if R:
                    dve.wait_ge(S["x1_ready"], R.n * 2 + 1)
                    if Q:
                        dve.wait_ge(S["nb2_ready"], Q.n + 1)
                    stats2(R, [0, 1])
                if Q:
                    rt.wait()
                    rt.did(dve.tensor_tensor(OH[:, 1], rev, v01[:, 1, :].unsqueeze(2).to_broadcast([P, NT, E]),
                                             ALU.is_equal))
                    rt.wait()
                    ge(dve, S["rank_ready"], Q.n)
                    rt.did(dve.tensor_tensor(sel[:, :, :], OH[:, 0], OH[:, 1], ALU.add))
                    assert rt.k == RT_SEL
                    ge(dve, S["ed_ready"], Q.n)
                    rt.did(dve.tensor_tensor(dm[:, :], m01[:, 1, :], m01[:, 0, :], ALU.subtract))
                    assert rt.k == RT_DM
                if R:
                    scaled_sums(R, 3)
                if M:
                    binary(M, 2)
                if Q:
                    dve.wait_ge(S["ed_ready"], Q.n + 1)
                    rt.did(dve.tensor_scalar(den[:, :], ed[:, :], 1.0, None, ALU.add))
                    dve.wait_ge(S["rank_ready"], Q.n + 1)
                    rt.did(dve.tensor_tensor(pos[:, :, :], rkp, carry[:, :].unsqueeze(1).to_broadcast([P, NT, E]),
                                             ALU.add))
                    rt.after(RT_DM + 1)
                    rt.did(dve.reciprocal(PR[:, 0, bass.ds(Q.n * NT, NT)], den[:, :]))
                    rt.after(RT_DM + 2)
                    rt.did(dve.tensor_tensor(carry[:, :], totp, carry[:, :], ALU.add))
                    rt.did(dve.tensor_tensor(prod[:, :, :, :], OH[:, :, :, :],
                                             pos[:, :, :].unsqueeze(1).to_broadcast([P, 2, NT, E]), ALU.mult))
                    rt.after(RT_DM + 3)
                    rt.did(dve.tensor_tensor(PR[:, 1, bass.ds(Q.n * NT, NT)], ed[:, :],
                                             PR[:, 0, bass.ds(Q.n * NT, NT)], ALU.mult))
                    rt.after(RT_DM + 5)
                    rt.did(dve.tensor_reduce(slotf[:, :, :], prod[:, :, :, :], AX.X, ALU.add))
                    ge(dve, scattered[Q.p], Q.h * 16 * 2 * NT)
                    rt.did(dve.tensor_copy(rowt[:, Q.p, :, D + 1], v01[:, 0, :]))
                    rt.did(dve.tensor_copy(rowt[:, Q.p, :, D], C(C_TOK)[:, bass.ds(Q.n * NT, NT)]))
                    rt.after(RT_DM + 7)
                    rt.did(dve.tensor_copy(idx[:, Q.p], slotf[:, :, :]))
                    assert rt.k == RT_STEPS
            dve.wait_ge(S["small_ready"], 32)
            slots(dve, body, 17, -2)

            t = Chain(dve, S["tab_steps"], 0, 0)
            dve.wait_ge(S["rt_steps"], NB * RT_STEPS)

            def step(ins):
                t.did(ins)
                t.wait()
            step(dve.tensor_copy(cnti[:, 0, :], carry[:, :]))
            step(dve.tensor_tensor(cnt[:, 0, :], carry[:, :], C(C_BASE), ALU.subtract))
            step(dve.tensor_scalar(cnti[:, 1, :], cnt[:, 0, :], float(BLK - 1), None, ALU.add))
            step(dve.tensor_scalar(cnti[:, 1, :], cnti[:, 1, :], BLK.bit_length() - 1, None, ALU.arith_shift_right))
            step(dve.tensor_copy(cnt[:, 1, :], cnti[:, 1, :]))
            cur = 1
            for d in (1, 2, 4):
                step(dve.tensor_copy(cnt[:, cur + 1, 0:d], cnt[:, cur, 0:d]))
                step(dve.tensor_tensor(cnt[:, cur + 1, d:E], cnt[:, cur, d:E], cnt[:, cur, 0:E - d], ALU.add))
                cur += 1
            ends = cnt[:, cur, :].unsqueeze(1).to_broadcast([P, TAB, E])
            io = C(C_IOTA).unsqueeze(2).to_broadcast([P, TAB, E])
            step(dve.tensor_tensor(cube[:, :, :], io, ends, ALU.is_ge))
            step(dve.tensor_reduce(tf[:, 0, :], cube[:, :, :], AX.X, ALU.add))
            step(dve.tensor_tensor(cube[:, :, :], cube[:, :, :], ends, ALU.mult))
            step(dve.tensor_reduce(tf[:, 1, :], cube[:, :, :], AX.X, ALU.max))
            step(dve.tensor_tensor(tf[:, 2, :], C(C_IOTA), tf[:, 1, :], ALU.subtract))
            step(dve.tensor_scalar(tf[:, 3, :], tf[:, 0, :], float(CAP), None, ALU.mult))
            step(dve.scalar_tensor_tensor(tf[:, 4, :], tf[:, 2, :], float(BLK), tf[:, 3, :], ALU.mult, ALU.add))
            step(dve.tensor_scalar(tab[:, 0, :], tf[:, 4, :], float(E * CAP), None, ALU.min))
            step(dve.tensor_scalar(tab[:, 1, :], tf[:, 0, :], float(E - 1), None, ALU.min))
            step(dve.tensor_scalar(tf[:, 5, :], tf[:, 0, :], -1.0, float(E), ALU.mult, ALU.add))
            dve.sem_inc(S["tab_ready"], 1)

            def split(U):
                dve.wait_ge(S["hid_ready"], U.n * NC + NC)
                ge(dve, S["down_ready"], U.n - 1)
                c = Chain(dve, S["split_steps"], 2, U.n)
                c.did(dve.tensor_copy(hp[:, U.p, 0], h32[:, U.p]))
                c.wait()
                c.did(dve.tensor_tensor(hp[:, U.p, 1], h32[:, U.p], hp[:, U.p, 0], ALU.subtract))

            def work(at):
                X, U, Y = at(2), at(1), at(0)
                if U:
                    dve.wait_ge(ld_rows[U.q], U.f * 16 + 16)
                    ge(dve, back[U.q], U.f * 16 * BT)
                    c = Chain(dve, S["bidx_steps"], 2, U.n)
                    c.did(dve.tensor_scalar(bk[:, U.p, :], xb[:, U.q, :, D + 1], tf[:, 5, bass.ds(U.n, 1)],
                                            float(TOK), ALU.not_equal, ALU.mult))
                if U:
                    c.wait()
                    c.did(dve.tensor_tensor(bidx[:, U.q, :], bk[:, U.p, :], xb[:, U.q, :, D], ALU.add))
                    split(U)
                if Y:
                    ex = dve.value_load(tab[0:1, 1, bass.ds(Y.n, 1)], min_val=0, max_val=E - 1)
                    dve.wait_ge(S["down_ready"], Y.n + 1)
                    ge(dve, back[Y.q], Y.f * 16 * BT)
                    dve.scalar_tensor_tensor(ysb[:, Y.q], Yp[Y.p], sc[:, 11:12],
                                             b2b[:, bass.ds(ex, 1), :].to_broadcast([P, BT, D]),
                                             ALU.mult, ALU.add).then_inc(S["y_ready"], 1)
            steps(dve, work)

            def final(n, q, k):
                dve.wait_ge(ld_y[k], q * 32 + 32)
                for j in range(NT):
                    xt1 = xr[:, bass.ds(n * NT + j, 1), :].rearrange("p a d -> p (a d)")
                    dve.scalar_tensor_tensor(xt1, yin[:, k, 0, j, :], PR[:, 0, bass.ds(n * NT + j, 1)], xt1,
                                             ALU.mult, ALU.add).then_inc(S["o1_steps"], 1)
                for j in range(NT):
                    xt1 = xr[:, bass.ds(n * NT + j, 1), :].rearrange("p a d -> p (a d)")
                    dve.wait_ge(S["o1_steps"], n * NT + j + 1)
                    dve.scalar_tensor_tensor(yin[:, k, 1, j, :], yin[:, k, 1, j, :], PR[:, 1, bass.ds(n * NT + j, 1)],
                                             xt1, ALU.mult, ALU.add).then_inc(S["final_ready"], 1)
            with dve.Fori(0, 4) as q:
                for k in range(4):
                    final(q * 4 + k, q, k)

        @block.tensor
        def _(pe):
            mm = pe.matmul
            pe.wait_ge(S["ld_const"], 16)
            pe.wait_ge(S["ld_small"], 16 * (2 * H + 3))
            pe.transpose(bank[4][:, 0:D], Wr[:, :], ident)
            pe.transpose(bank[5][:, 0:E], Wgr[:, :], C(C_ID, E)[:, 0:E])
            pe.transpose(bank[6][:, 0:E * NC], b1r[:, :], C(C_ID, E * NC)[:, 0:E * NC]).then_inc(S["prep_pe"], 1)
            pe.wait_ge(S["prep_step"], 5)
            mm(bank[4][:, D:D + 2 * H], WT[:, :], Am[:, :], start=True, stop=True).then_inc(S["prep_pe"], 1)
            pe.wait_ge(S["prep_step"], 9)
            for q in range(3):
                last = pe.transpose(bank[5][0:1, 128 * (q + 1):128 * (q + 2)], sc[:, q:q + 1], ident)
            last.then_inc(S["prep_pe"], 1)
            pe.wait_ge(S["prep_step"], 12)
            mm(bank[4][:, 256:259], C(C_ONE, 1), tf[0:1, 0, 0:3], start=True, stop=True).then_inc(S["prep_pe"], 1)
            for u in range(2 * E):
                ge(pe, S["w_dve"], u - 3)
                ge(pe, S["w_act"], u - 3)
                for c in range(NC):
                    src = W1r[:, u * NC + c, :] if u < E else W2r[:, u - E, c * P:(c + 1) * P]
                    last = pe.transpose(bank[u % 4][:, c * P:(c + 1) * P], src, ident)
                last.then_inc(S["w_pe"], 1)
            pe.wait_ge(S["w_dve"], 2 * E)
            pe.wait_ge(S["const_ready"], 10)

            def broadcast(M):
                pe.wait_ge(S["rows_ready"], M.n + 1)
                ge(pe, S["gh_ready"], M.n * NT)
                mm(hb[:, :], selb[:, (H - 1) * P:H * P], rows[:, M.p, :], start=True, stop=True) \
                    .then_inc(S["bc_ready"], 1)

            def fill(M, k):
                h, mt = k // NT, k % NT
                if k == 0:
                    pe.wait_ge(S["thr_ready"], M.n * 2 + 2)
                ge(pe, S["z_used"], M.n * FILLS + k - 1)
                mm(zb[k % 2][:, :], negb[:, :], thr[:, M.p, mt, :], start=True, stop=False)
                mm(zb[k % 2][:, :], selb[:, h * P:(h + 1) * P], rows[:, M.p, :], start=False, stop=True) \
                    .then_inc(S["z_ready"], 1)

            def sums(R, nt, part):
                o = Ob[nt % 2][:, 0:H * VW].rearrange("p (h v) -> p h v", v=VW)
                if part == 0:
                    ge(pe, S["t_steps"], R.n * NT + nt - 1)
                    if nt == 0:
                        pe.wait_ge(S["part3_ready"], R.n + 1)
                        pe.wait_ge(S["adjn_ready"], R.n + 1)
                    for mt in range(NT):
                        for q in range(3):
                            v = V3[:, R.p, mt] if q == 2 else Vhi[:, R.p, q, mt]
                            mm(o[:, :, HD + 1:VW], adjn[:, R.p, mt, nt * P:(nt + 1) * P], v[:, :, HD + 1:VW],
                               start=(mt == 0 and q == 0), stop=False, skip_group_check=True)
                    return
                h = (part + H - 2) % H
                if nt == 0:
                    if h == H - 1:
                        pe.wait_ge(S["gh_ready"], R.n * NT + NT)
                    else:
                        pe.wait_ge(S["g_ready"], R.n * ACT_HEADS + h + 1)
                for mt in range(NT):
                    for q in range(3):
                        v = V3[:, R.p, mt] if q == 2 else Vhi[:, R.p, q, mt]
                        last = mm(o[:, h, :], G[:, R.p, h, mt, nt * P:(nt + 1) * P], v[:, h, :],
                                  start=False, stop=(part == H and mt == NT - 1 and q == 2), skip_group_check=True)
                if part == H:
                    last.then_inc(S["o_ready"], 1)

            def transpose_rows(F):
                if F:
                    pe.wait_ge(S["xn_ready"], F.n * NT + NT)
                    ge(pe, S["thr_ready"], F.n * 2)
                    for j in range(NT):
                        last = pe.transpose(TR[:, j * P:(j + 1) * P], xn[:, j, :], ident)
                    last.then_inc(S["xT_ready"], 1)

            def transpose_rows2(F, Q):
                if Q:
                    pe.wait_ge(S["xn2_ready"], Q.n * NT + NT)
                    if F:
                        pe.wait_ge(S["xnT_ready"], F.n + 1)
                    for j in range(NT):
                        last = pe.transpose(TR[:, j * P:(j + 1) * P], xn2[:, j, :], ident)
                    last.then_inc(S["x2T_ready"], 1)

            def products(F, Q, M):
                if F:
                    pe.wait_ge(S["xnT_ready"], F.n + 1)
                    if M:
                        pe.wait_ge(S["v_steps"], M.n * X_STEPS + X_STEPS)
                        pe.wait_ge(S["arg_steps"], M.n * ARG_STEPS + 2)
                    if Q:
                        ge(pe, S["rt_steps"], Q.n * RT_STEPS)
                    for j in range(NT):
                        mm(HP[:, j * P:(j + 1) * P], xnT[:, j * P:(j + 1) * P], Wr[:, :], start=True, stop=True)
                        last = mm(s12p[:, j, :], xnT[:, j * P:(j + 1) * P], Wa[:, :], start=True, stop=True)
                    last.then_inc(S["h_ready"], 1)

            def gate(Q):
                if Q:
                    pe.wait_ge(S["xn2T_ready"], Q.n + 1)
                    for j in range(NT):
                        last = mm(gp[:, j, :], xn2T[:, j * P:(j + 1) * P], WgT[:, :], start=True, stop=True)
                    last.then_inc(S["gate_ready"], 1)

            def transpose_s(F):
                if F:
                    pe.wait_ge(S["s_steps"], F.n * S_STEPS + S_STEPS)
                    for j in range(NT):
                        last = pe.transpose(rowp[:, j * P:(j + 1) * P],
                                            s3hi[:, j].rearrange("p q c -> p (q c)"), identb[:, :])
                    last.then_inc(S["sT_ready"], 1)

            def largest(F):
                if F:
                    pe.wait_ge(S["mx_steps"], F.n * MX_STEPS + MX_STEPS)
                    mm(Sp, C(C_ONE, H), diag[:, :], start=True, stop=True).then_inc(S["S_ready"], 1)

            def transpose_away(F, Q, g):
                if F:
                    if g == 0:
                        pe.wait_ge(S["adj_cast"], F.n + 1)
                        pe.wait_ge(S["xnT_ready"], F.n + 1)
                        if Q:
                            pe.wait_ge(S["rt_steps"], Q.n * RT_STEPS + 1)
                    else:
                        pe.wait_ge(S["thr_ready"], F.n * 2 + 1)
                    for mt in (2 * g, 2 * g + 1):
                        for nt in range(NT):
                            last = pe.transpose(AD[:, mt % 2, nt * P:(nt + 1) * P],
                                                away[:, nt, mt * P:(mt + 1) * P], identb[:, :])
                    last.then_inc(S["awayT_ready"], 1)

            def ranks(Q, F):
                if Q:
                    pe.wait_ge(S["rt_steps"], Q.n * RT_STEPS + RT_SEL)
                    if F:
                        pe.wait_ge(S["rows_ready"], F.n + 1)
                    mm(rkp, trib[:, :], sel[:, :, :], start=True, stop=False, skip_group_check=True)
                    for j in range(NT - 1):
                        mm(rkp[:, j + 1:NT, :], onesb[:, :], sel[:, j:j + 1, :].to_broadcast([P, NT - 1 - j, E]),
                           start=False, stop=(j == NT - 2), skip_group_check=True)
                    for j in range(NT):
                        last = mm(totp, onesb[:, :], sel[:, j, :], start=(j == 0), stop=(j == NT - 1),
                                  skip_group_check=True)
                    last.then_inc(S["rank_ready"], 1)

            def body(at):
                F, M, R, Q = at(1), at(0), at(-1), at(-2)
                if M:
                    broadcast(M)
                k = 0
                for nt in range(NT):
                    for part in range(H + 1):
                        if M and part % 2 == 0:
                            fill(M, k)
                            k += 1
                        if R:
                            sums(R, nt, part)
                        done = nt * (H + 1) + part
                        if done == 2:
                            transpose_rows(F)
                        if done == 4:
                            products(F, Q, M)
                        if done == 6:
                            transpose_rows2(F, Q)
                        if done == 7:
                            transpose_s(F)
                        if done == 9:
                            gate(Q)
                        if done == 11:
                            transpose_away(F, Q, 0)
                        if done == 13:
                            transpose_away(F, Q, 1)
                        if done == 15:
                            largest(F)
                        if done == 18:
                            ranks(Q, F)
            slots(pe, body, 17)

            def layers(at):
                X, U, Y = at(2), at(1), at(0)
                if X:
                    pe.wait_ge(ld_rows[X.q], X.f * 16 + 16)
                    ge(pe, S["xt_ready"], X.n - 1)
                    xv = xb[:, X.q, :, 0:D].bitcast(FP16).rearrange("p t (q d) -> p t q d", q=2)
                    for q in range(2):
                        for t in range(BT):
                            last = pe.transpose(XTp[X.p][:, q, t * P:(t + 1) * P], xv[:, t, q, :], identh[:, :])
                    last.then_inc(S["bt_ready"], 1)
                if Y:
                    ey = pe.value_load(tab[0:1, 1, bass.ds(Y.n, 1)], min_val=0, max_val=E - 1)
                if U:
                    pe.wait_ge(S["xt_ready"], U.n + 1)
                    ge(pe, S["hid_ready"], (U.n - 1) * NC)
                    ex = pe.value_load(tab[0:1, 1, bass.ds(U.n, 1)], min_val=0, max_val=E - 1)
                    for c in range(NC):
                        o = Up[U.p][c // 2][:, (c % 2) * BLK:(c % 2 + 1) * BLK]
                        for n, (wq, xq) in enumerate(((0, 0), (0, 1), (1, 0))):
                            w = W1h[:, wq, bass.ds(ex, 1), c * P:(c + 1) * P].rearrange("p e h -> p (e h)")
                            last = mm(o, w, xt[:, U.p, xq, :], start=(n == 0), stop=(n == 2))
                        last.then_inc(S["up_ready"], 1)
                if Y:
                    pe.wait_ge(S["split_steps"], Y.n * 2 + 2)
                    ge(pe, S["y_ready"], Y.n - 1)
                    for t in range(BT):
                        for c in range(NC):
                            for n, (hq, wq) in enumerate(((0, 0), (0, 1), (1, 0))):
                                w = W2h[:, wq, bass.ds(ey, 1), c, :].rearrange("p e d -> p (e d)")
                                last = mm(Yp[Y.p][:, t, :], hp[:, Y.p, hq, c, t * P:(t + 1) * P], w,
                                          start=(c == 0 and n == 0), stop=(c == NC - 1 and n == 2))
                    last.then_inc(S["down_ready"], 1)
            pe.wait_ge(S["tab_ready"], 1)
            steps(pe, layers)


_INS = ["x", "adj", "L0_gnn_W", "L0_gnn_a", "L0_ffn_Wg", "L0_ffn_bg", "L0_ffn_W1", "L0_ffn_b1", "L0_ffn_W2", "L0_ffn_b2"]


def kernel(**inputs):
    import numpy as np
    import concourse.bacc as bacc
    from concourse.bass_utils import run_bass_kernel_spmd

    nc = bacc.Bacc("TRN2", target_bir_lowering=False, num_devices=1)
    arrays, args = {}, []
    for name in _INS:
        arr = np.ascontiguousarray(inputs[name])
        arrays[f"in_{name}"] = arr
        args.append(nc.dram_tensor(f"in_{name}", arr.shape, mybir.dt.from_np(arr.dtype), kind="ExternalInput").ap())
    arrays["in_const"] = constants(np)
    args.append(nc.dram_tensor("in_const", (P, NCONST), F32, kind="ExternalInput").ap())
    args.append(nc.dram_tensor("out_0", (NB, N, D), F32, kind="ExternalOutput").ap())
    build(nc, *args)
    r = run_bass_kernel_spmd(nc, [arrays], core_ids=[0])
    return r.results[0]["out_0"]
```

```python
from contextlib import ExitStack

import concourse.bass as bass
from concourse import mybir

ALU = mybir.AluOpType
ACT = mybir.ActivationFunctionType
AX = mybir.AxisListType
F32 = mybir.dt.float32
BF16 = mybir.dt.bfloat16
FP16 = mybir.dt.float16
I32 = mybir.dt.int32

P = 128
NB = 16
N = 512
D = 128
NT = N // P
H = 4
HD = D // H
E = 8
HID = 512
NC = HID // P
TOK = NB * N
TILES = TOK // P
EPS = 1e-5
SLOPE = 0.2
SHIFT = 60.0
VW = 2 * (HD + 1)
BLK = 256
BT = BLK // P
CAP = TOK + BLK
BLOCKS = 2 * TOK // BLK + E - 1
TAB = BLOCKS + 1
STEPS = 8
XS_ROWS = E * CAP + BLK
ROW = D + 2
XSCALE = 1024.0

C_ID, C_TRI, C_SEL, C_MASK, C_REV, C_BASE, C_TOK, C_IOTA, C_HALF, C_ONE = range(10)
_W = [P, P, H * P, H, E, E, TILES, TAB, NT, P]
_O = [sum(_W[:k]) for k in range(len(_W))]
NCONST = sum(_W)


def constants(np):
    c = np.zeros((P, NCONST), np.float32)
    r = np.arange(P)

    def put(k, v):
        c[:, _O[k]:_O[k] + _W[k]] = v

    put(C_ID, np.eye(P))
    put(C_TRI, r[:, None] < r[None, :])
    for h in range(H):
        for part in range(3):
            c[8 * part + H + h, _O[C_SEL] + h * P:_O[C_SEL] + (h + 1) * P] = 1
    put(C_MASK, (r[:, None] // HD) == np.arange(H)[None, :])
    put(C_REV, E - np.arange(E)[None, :])
    put(C_BASE, np.arange(E)[None, :] * CAP)
    put(C_TOK, np.arange(TILES)[None, :] * P + r[:, None])
    put(C_IOTA, np.arange(TAB)[None, :])
    put(C_HALF, -0.5)
    put(C_ONE, 1.0)
    return c


class Batch:

    def __init__(self, base, i=None, unroll=2):
        self.p, self.q = base % 2, base % 4
        if i is None:
            self.n, self.h, self.f = base, base // 2, base // 4
        else:
            self.n, self.h = i * unroll + base, i * (unroll // 2) + base // 2
            self.f = i * (unroll // 4) + base // 4


def ge(eng, sem, value):
    if isinstance(value, int) and value <= 0:
        return
    eng.wait_ge(sem, value)


def hold(eng, sem, value, turns):
    if isinstance(value, int) and value <= 0:
        return
    eng.wait_ge(sem, value)
    eng.sem_inc(turns, 1)


class Chain:

    def __init__(self, eng, sem, per, n):
        self.eng, self.sem, self.per, self.n, self.k = eng, sem, per, n, 0

    def did(self, ins):
        self.k += 1
        ins.then_inc(self.sem, 1)

    def now(self):
        return self.n * self.per + self.k

    def wait(self):
        self.eng.wait_ge(self.sem, self.now())

    def after(self, k):
        self.eng.wait_ge(self.sem, self.n * self.per + k)


FAR = 1e30
ACT_HEADS = H - 1
FILLS = ACT_HEADS * NT
LN_STEPS, S_STEPS, MX_STEPS, ARG_STEPS, X_STEPS, ATT_STEPS, RT_STEPS = 8, 5, 2, 6, 2, 4, 24
RT_SEL, RT_DM = 13, 14


def build(nc, x, adj, W, a, Wg, bg, W1, b1, W2, b2, const, out):
    with ExitStack() as ctx:
        def sb(name, shape, dt=F32):
            return ctx.enter_context(nc.sbuf_tensor(name, shape, dt))

        def ps(name, shape, dt=F32):
            return ctx.enter_context(nc.psum_tensor(name, shape, dt))

        def sem(name):
            return ctx.enter_context(nc.semaphore(name))

        xs = nc.dram_tensor("expert_rows", [XS_ROWS, ROW], F32, kind="Internal").ap()
        ybuf = nc.dram_tensor("expert_out", [2 * TOK, D], F32, kind="Internal").ap()

        cst = sb("cst", [P, NCONST])

        def C(k, rows=P):
            return cst[0:rows, _O[k]:_O[k] + _W[k]]

        ident = C(C_ID)
        identb = sb("identb", [P, P], BF16)
        identh = sb("identh", [P, P], FP16)
        trib = sb("trib", [P, P], BF16)
        onesb = sb("onesb", [P, P], BF16)
        negb = sb("negb", [P, P], BF16)
        selb = sb("selb", [24, H * P], BF16)
        xr = sb("xr", [P, TILES, D])
        adji = sb("adji", [P, 2, NT, N], I32)
        away = sb("away", [P, NT, N], BF16)
        thr = sb("thr", [P, 2, NT, N], BF16)
        adjn = sb("adjn", [P, 2, NT, N], BF16)
        G = sb("G", [P, 2, H, NT, N], BF16)
        mv1 = sb("mv1", [P, NT, 2])
        bs1 = sb("bs1", [P, NT, 6])
        rs1 = sb("rs1", [P, NT])
        nb1 = sb("nb1", [P, NT])
        xn = sb("xn", [P, NT, D])
        xnT = sb("xnT", [P, N])
        s3 = sb("s3", [P, NT, 3, 8])
        s2c = sb("s2c", [P, 2, NT, H])
        rows = sb("rows", [24, 2, N], BF16)
        mxp = sb("mxp", [P, H])
        mx = sb("mx", [H, 1])
        diag = sb("diag", [H, H])
        arg = sb("arg", [P, 4, NT, H])
        zt = sb("zt", [P, NT, H])
        Mt = sb("Mt", [P, NT, H])
        Ex = sb("Ex", [P, 2, 4, NT, H])
        V = sb("V", [P, 2, 2, NT, H, VW])
        V3 = sb("V3", [P, 2, NT, H, VW], BF16)
        T = sb("T", [P, NT, H, 2, HD + 1])
        rec = sb("rec", [P, NT, H])
        att = sb("att", [P, NT, D])
        mv2 = sb("mv2", [P, NT, 2])
        bs2 = sb("bs2", [P, NT, 6])
        rs2 = sb("rs2", [P, NT])
        nb2 = sb("nb2", [P, NT])
        xn2 = sb("xn2", [P, NT, D])
        xn2T = sb("xn2T", [P, N])
        g8 = sb("g8", [P, NT, E])
        m01 = sb("m01", [P, 2, NT])
        v01 = sb("v01", [P, 2, NT])
        eq = sb("eq", [P, NT, E])
        cand = sb("cand", [P, NT, E])
        OH = sb("OH", [P, 2, NT, E])
        g2 = sb("g2", [P, NT, E])
        sel = sb("sel", [P, NT, E], BF16)
        dm = sb("dm", [P, NT])
        ed = sb("ed", [P, NT])
        den = sb("den", [P, NT])
        PR = sb("PR", [P, 2, TILES])
        pos = sb("pos", [P, NT, E])
        carry = sb("carry", [P, E])
        prod = sb("prod", [P, 2, NT, E])
        slotf = sb("slotf", [P, 2, NT])
        idx = sb("idx", [P, 2, 2, NT], I32)
        rowt = sb("rowt", [P, 2, NT, ROW])
        Wr = sb("Wr", [P, D])
        WT = sb("WT", [P, D])
        acol = sb("acol", [P, 2])
        Am = sb("Am", [P, 2 * H])
        Wa = sb("Wa", [P, 2 * H])
        Wgr = sb("Wgr", [E, D])
        WgT = sb("WgT", [P, E])
        bgb = sb("bgb", [P, E])
        b1r = sb("b1r", [E * NC, P])
        b1s = sb("b1s", [P, E * NC])
        b2b = sb("b2b", [P, E, D])
        W1h = sb("W1h", [P, 2, E, HID], FP16)
        W2h = sb("W2h", [P, 2, E, NC, D], FP16)
        sc = sb("sc", [P, 16])
        Gf = G[:, :, :, :, :].rearrange("p a h t n -> p (a h t n)").bitcast(F32)
        W1r = Gf[:, 0:E * NC * D].rearrange("p (t d) -> p t d", d=D)
        W2r = Gf[:, E * NC * D:2 * E * NC * D].rearrange("p (e h) -> p e h", h=HID)
        tf = sb("tf", [P, 8, TAB])
        cube = sb("cube", [P, TAB, E])
        cnt = sb("cnt", [P, 6, E])
        cnti = sb("cnti", [P, 2, E], I32)
        tab = sb("tab", [P, 2, TAB], I32)
        padrow = sb("padrow", [P, BT, ROW])
        h32 = Gf[:, 0:2 * NC * BLK].rearrange("p (a c n) -> p a c n", a=2, c=NC)
        hp = G[:, :, :, :, :].rearrange("p a h t n -> p (a h t n)")[:, 4 * NC * BLK:8 * NC * BLK] \
            .bitcast(FP16).rearrange("p (a q c n) -> p a q c n", a=2, q=2, c=NC)
        xb = sb("xb", [P, 4, BT, ROW])
        xt = sb("xt", [P, 2, 2, BLK], FP16)
        ysb = sb("ysb", [P, 4, BT, D])
        bk = sb("bk", [P, 2, BT])
        bidx = sb("bidx", [P, 4, BT], I32)
        yin = adji[:, :, :, :].rearrange("p a t n -> p (a t n)").bitcast(F32) \
            .rearrange("p (b k t d) -> p b k t d", b=4, k=2, d=D)

        bank = [ps(f"bank{k}", [P, 512]) for k in range(8)]
        zb = [bank[0], bank[1]]
        hb = bank[6]
        Ob = [bank[2], bank[3]]
        TR = bank[4]
        HP = bank[5]
        MS = bank[7]
        AD = bank[4][:, :].bitcast(BF16).rearrange("p (a n) -> p a n", a=2)
        s12p = MS[:, 0:32].rearrange("p (t c) -> p t c", c=8)
        Sp = TR[:, 32:36]
        gp = TR[:, 0:32].rearrange("p (t e) -> p t e", e=E)
        rkp = MS[:, 96:128].rearrange("p (t e) -> p t e", e=E)
        totp = MS[:, 64:72]
        mxT = MS[0:H, 128:256]
        rowp = MS[0:24, 256:512].bitcast(BF16)
        Vhi = V[:, :, :, :, :, :].rearrange("p a q t h v -> p (a q t h v)").bitcast(BF16) \
            .rearrange("p (a q t h v w) -> p a q t h v w", a=2, q=2, t=NT, h=H, w=2)[:, :, :, :, :, :, 1]
        s3hi = s3[:, :, :, :].rearrange("p t q c -> p (t q c)").bitcast(BF16) \
            .rearrange("p (t q c w) -> p t q c w", t=NT, q=3, w=2)[:, :, :, :, 1]
        Up = [[bank[0], bank[1]], [bank[2], bank[3]]]
        XTp = [bank[4][:, :].bitcast(FP16)[:, 0:2 * BLK].rearrange("p (q n) -> p q n", q=2),
               bank[5][:, :].bitcast(FP16)[:, 0:2 * BLK].rearrange("p (q n) -> p q n", q=2)]
        Yp = [bank[6][:, 0:BT * D].rearrange("p (t d) -> p t d", d=D),
              bank[7][:, 0:BT * D].rearrange("p (t d) -> p t d", d=D)]

        names = """ld_const ld_small ld_w1 ld_w2 ld_x0 ld_x1 ld_adj0 ld_adj1
            const_ready prep_step prep_pe prep_act w_pe w_act w_dve scale_ready small_ready
            ln1 rstd1 nb1_ready xn_ready xT_ready xnT_ready h_ready s_steps sT_ready rows_ready mx_steps S_ready
            arg_steps exp_ready v_steps rest_ready part3_ready
            adj_cast awayT_ready thr_ready adjn_ready z_ready z_used bc_ready gh_ready g_ready
            o_ready t_steps sum_ready att_steps x1_ready
            ln2 rstd2 nb2_ready xn2_ready x2T_ready xn2T_ready gate_ready rt_steps ed_ready rank_ready
            hi_ready lo_ready scattered0 scattered1 tab_steps ends_ready tab_ready pads_ready
            ld_rows0 ld_rows1 ld_rows2 ld_rows3 bt_ready xt_ready up_ready hid_ready split_steps down_ready y_ready
            bidx_steps back0 back1 back2 back3 ld_y0 ld_y1 ld_y2 ld_y3 first_ready second_ready final_ready stored0 stored1 stored2 stored3 pool_turns dve_turns"""
        S = {n: sem(n) for n in names.split()}
        ld_adj = [S["ld_adj0"], S["ld_adj1"]]
        scattered = [S["scattered0"], S["scattered1"]]
        ld_rows = [S[f"ld_rows{k}"] for k in range(4)]
        back = [S[f"back{k}"] for k in range(4)]
        ld_y = [S[f"ld_y{k}"] for k in range(4)]
        stored = [S[f"stored{k}"] for k in range(4)]

        xd = x.rearrange("b (t p) d -> p (b t) d", p=P)
        outd = out.rearrange("b (t p) d -> p (b t) d", p=P)
        adjd = adj.rearrange("b (t p) m -> b p t m", p=P)
        yd = ybuf.rearrange("(k t p) d -> p k t d", k=2, p=P)
        XSPLIT = 3 * NT
        SMALL = 8

        def slots(eng, body, last, first=-1):
            for s in range(first, 4):
                body(lambda k, s=s: Batch(s + k) if 0 <= s + k < NB else None)
            with eng.Fori(0, 5) as i:
                for u in range(2):
                    body(lambda k, u=u: Batch(4 + u + k, i))
            for s in range(14, last + 1):
                body(lambda k, s=s: Batch(s + k) if 0 <= s + k < NB else None)

        def blocks(eng, body):
            for k in range(4):
                body(Batch(k))
            with eng.Fori(0, BLOCKS // 4 - 1) as i:
                for k in range(4):
                    body(Batch(4 + k, i, 4))
            for k in range(BLOCKS // 4 * 4, BLOCKS):
                body(Batch(k))

        def steps(eng, body):
            def fixed(s, first):
                at = lambda k: Batch(s + k) if 0 <= s + k < BLOCKS else None
                at.first = first
                return at

            def looped(u, i):
                at = lambda k: Batch(2 + u + k, i, STEPS)
                at.first = u == 0
                return at
            for s in range(-2, 2):
                body(fixed(s, s == -2))
            with eng.Fori(0, (BLOCKS - 4) // STEPS) as i:
                for u in range(STEPS):
                    body(looped(u, i))
            rest = 2 + (BLOCKS - 4) // STEPS * STEPS
            for s in range(rest, BLOCKS):
                body(fixed(s, s == rest))

        def pad_rows(eng, experts):
            eng.wait_ge(S["ends_ready"], 1)
            for e in experts:
                r = eng.value_load(cnti[0:1, 0, e:e + 1], min_val=e * CAP, max_val=e * CAP + TOK)
                eng.dma_start(xs[bass.ds(r, BLK), :].rearrange("(t p) w -> p t w", p=P), padrow[:, :, :]) \
                   .then_inc(S["pads_ready"], 16)

        block = ctx.enter_context(nc.Block())

        @block.sync
        def _(sp):
            sp.dma_start(cst[:, :], const).then_inc(S["ld_const"], 16)
            sp.dma_start(Wr[:, :], W).then_inc(S["ld_small"], 16)
            for k in range(2):
                for h in range(H):
                    lo = HD * (1 - k)
                    sp.dma_start(acol[HD * h:HD * (h + 1), k:k + 1],
                                 a[h:h + 1, lo:lo + HD].rearrange("h d -> d h")).then_inc(S["ld_small"], 16)
            sp.dma_start(Wgr[:, :], Wg).then_inc(S["ld_small"], 16)
            sp.dma_start(b1r[:, :], b1.rearrange("e (c p) -> (e c) p", p=P)).then_inc(S["ld_small"], 16)
            sp.dma_start(W1r, W1.rearrange("e (c p) d -> p (e c) d", p=P)).then_inc(S["ld_w1"], 16)
            sp.dma_start(W2r, W2.rearrange("e d h -> d e h")).then_inc(S["ld_w2"], 16)
            sp.dma_start(xr[:, 0:XSPLIT, :], xd[:, 0:XSPLIT, :]).then_inc(S["ld_x0"], 16)

            def load_adj(B):
                ge(sp, S["adj_cast"], B.n - 1)
                sp.dma_start(adji[:, B.p], adjd[bass.ds(B.n, 1)].rearrange("b p t m -> p (b t) m")) \
                  .then_inc(ld_adj[B.p], 16)
            load_adj(Batch(0))
            load_adj(Batch(1))
            sp.dma_start(xr[:, XSPLIT:TILES, :], xd[:, XSPLIT:TILES, :]).then_inc(S["ld_x1"], 16)
            with sp.Fori(0, (NB - 2) // 2) as i:
                load_adj(Batch(2, i))
                load_adj(Batch(3, i))

            pad_rows(sp, range(E // 2))
            sp.dma_start(xs[E * CAP:E * CAP + BLK, :].rearrange("(t p) w -> p t w", p=P), padrow[:, :, :]) \
              .then_inc(S["pads_ready"], 16)
            sp.wait_ge(S["tab_ready"], 1)
            sp.wait_ge(S["pads_ready"], 16 * (E + 1))
            sp.wait_ge(scattered[0], 16 * 2 * NT * NB // 2)
            sp.wait_ge(scattered[1], 16 * 2 * NT * NB // 2)

            def load_rows(B):
                ge(sp, S["bt_ready"], B.n - 3)
                ge(sp, S["bidx_steps"], B.n * 2 - 6)
                r = sp.value_load(tab[0:1, 0, bass.ds(B.n, 1)], min_val=0, max_val=E * CAP)
                sp.dma_start(xb[:, B.q], xs[bass.ds(r, BLK), :].rearrange("(t p) w -> p t w", p=P)) \
                  .then_inc(ld_rows[B.q], 16)
            blocks(sp, load_rows)

            for k in range(4):
                sp.wait_ge(back[k], 16 * BT * ((BLOCKS + 3 - k) // 4))

            def load_y(n, q, k):
                ge(sp, stored[k], q * 16)
                for c in range(2):
                    sp.dma_start(yin[:, k, c], yd[:, c, bass.ds(n * NT, NT), :]).then_inc(ld_y[k], 16)
            for k in range(4):
                load_y(k, 0, k)
            with sp.Fori(1, 4) as q:
                for k in range(4):
                    load_y(q * 4 + k, q, k)
            for k in range(4):
                sp.wait_ge(stored[k], 16 * 4)

        @block.gpsimd
        def _(pool):
            def rstd(name, mv, rs, B, ready, scale=1.0):
                hold(pool, ready, B.n * LN_STEPS + LN_STEPS, S["pool_turns"])
                c = Chain(pool, S[name], 2, B.n)
                c.did(pool.tensor_scalar(rs[:, :], mv[:, :, 1], scale ** -2, EPS * scale ** -2,
                                         ALU.mult, ALU.add))
                hold(pool, S[name], c.now(), S["pool_turns"])
                c.did(pool.tensor_tensor(rs[:, :], rs[:, :], C(C_HALF), ALU.pow))

            def scatter(Z, js):
                if js[0] == 0:
                    hold(pool, S["rt_steps"], Z.n * RT_STEPS + RT_STEPS, S["pool_turns"])
                    hold(pool, S["hi_ready"], Z.n + 1, S["pool_turns"])
                    hold(pool, S["lo_ready"], Z.n + 1, S["pool_turns"])
                for j in js:
                    for k in range(2):
                        pool.indirect_dma_start(
                            xs, bass.IndirectOffsetOnAxis(ap=idx[:, Z.p, k, j:j + 1], axis=0),
                            rowt[:, Z.p, j, :], None).then_inc(scattered[Z.p], 16)

            def residual(R, half):
                ts = slice(2 * half, 2 * half + 2)
                hold(pool, S["t_steps"], R.n * NT + 2 * half + 2, S["pool_turns"])
                pool.tensor_tensor(T[:, ts, :, 0, :], T[:, ts, :, 0, :], T[:, ts, :, 1, :], ALU.subtract) \
                    .then_inc(S["sum_ready"], 1)

            def add(R, half):
                hold(pool, S["att_steps"], R.n * ATT_STEPS + 2 * half + 2, S["pool_turns"])
                xh = xr[:, bass.ds(R.n * NT + 2 * half, 2), :]
                pool.tensor_tensor(xh, xh, att[:, 2 * half:2 * half + 2, :], ALU.add).then_inc(S["x1_ready"], 1)

            def body(at):
                L, M, R, Q, Z = at(2), at(0), at(-1), at(-2), at(-3)
                if Q:
                    add(Q, 1)
                if Q:
                    hold(pool, S["xn2_ready"], Q.n * NT, S["pool_turns"])
                    hold(pool, S["nb2_ready"], Q.n, S["pool_turns"])
                    rstd("rstd2", mv2, rs2, Q, S["ln2"], XSCALE)
                if M:
                    hold(pool, S["v_steps"], M.n * X_STEPS + X_STEPS, S["pool_turns"])
                    hold(pool, S["o_ready"], (M.n - 1) * NT, S["pool_turns"])
                    pool.tensor_tensor(V[:, M.p, 1].rearrange("p t h v -> p (t h v)"),
                                       V[:, M.p, 0].rearrange("p t h v -> p (t h v)"),
                                       Vhi[:, M.p, 0].rearrange("p t h v -> p (t h v)"), ALU.subtract) \
                        .then_inc(S["rest_ready"], 1)
                if Z:
                    scatter(Z, [0, 1])
                if R:
                    residual(R, 0)
                if Z:
                    scatter(Z, [2])
                if R:
                    add(R, 0)
                if Q:
                    hold(pool, S["hi_ready"], Q.n + 1, S["pool_turns"])
                    pool.tensor_tensor(rowt[:, Q.p, :, D // 2:D].bitcast(FP16), xn2[:, :, :],
                                       rowt[:, Q.p, :, 0:D // 2].bitcast(FP16), ALU.subtract) \
                        .then_inc(S["lo_ready"], 1)
                if L:
                    hold(pool, S["xn_ready"], L.n * NT, S["pool_turns"])
                    hold(pool, S["nb1_ready"], L.n, S["pool_turns"])
                    rstd("rstd1", mv1, rs1, L, S["ln1"])
                if Z:
                    scatter(Z, [3])
                if R:
                    residual(R, 1)

            hold(pool, S["ld_const"], 16, S["pool_turns"])
            pool.dma_start(b2b[:, :, :].rearrange("p e d -> p (e d)"),
                           b2.rearrange("e d -> (e d)").partition_broadcast(P)).then_inc(S["small_ready"], 16)
            pool.dma_start(bgb[:, :], bg.partition_broadcast(P)).then_inc(S["small_ready"], 16)
            slots(pool, body, 18, -2)

            def send(B):
                hold(pool, S["bidx_steps"], B.n * 2 + 2, S["pool_turns"])
                hold(pool, S["y_ready"], B.n + 1, S["pool_turns"])
                for t in range(BT):
                    pool.indirect_dma_start(
                        ybuf, bass.IndirectOffsetOnAxis(ap=bidx[:, B.q, t:t + 1], axis=0),
                        ysb[:, B.q, t, :], None, bounds_check=2 * TOK - 1, oob_is_err=False) \
                        .then_inc(back[B.q], 16)
            blocks(pool, send)

        @block.scalar
        def _(act):
            act.wait_ge(S["scale_ready"], 1)
            for u in range(2 * E):
                act.wait_ge(S["w_pe"], u + 1)
                dst = W1h[:, 0, u, :] if u < E else W2h[:, 0, u - E, :, :].rearrange("p c d -> p (c d)")
                act.activation(dst, bank[u % 4][:, :], ACT.Copy,
                               scale=sc[:, 3:4] if u < E else sc[:, 7:8]).then_inc(S["w_act"], 1)

            def relu(M, ks):
                for k in ks:
                    h, mt = k // NT, k % NT
                    act.wait_ge(S["z_ready"], M.n * FILLS + k + 1)
                    if k == 0:
                        act.wait_ge(S["s_steps"], M.n * S_STEPS + S_STEPS)
                        ge(act, S["o_ready"], (M.n - 1) * NT)
                    act.activation(G[:, M.p, h, mt, :], zb[k % 2][:, :], ACT.Relu,
                                   bias=s2c[:, M.p, mt, h:h + 1]).then_inc(S["z_used"], 1)

            def normalise(dst, src, rs, nb, ready):
                for j in range(NT):
                    act.activation(dst[:, j, :], src[:, j, :], ACT.Identity, bias=nb[:, j:j + 1],
                                   scale=rs[:, j:j + 1]).then_inc(ready, 1)

            def body(at):
                F, M, Q, Z = at(1), at(0), at(-2), at(-3)
                if F:
                    act.wait_ge(S["nb1_ready"], F.n + 1)
                    ge(act, S["xT_ready"], F.n)
                    normalise(xn, xr[:, bass.ds(F.n * NT, NT), :], rs1, nb1, S["xn_ready"])
                if Z:
                    act.wait_ge(S["rt_steps"], Z.n * RT_STEPS + RT_DM)
                    act.activation(ed[:, :], dm[:, :], ACT.Exp).then_inc(S["ed_ready"], 1)
                if M:
                    relu(M, [0, 1])
                    act.wait_ge(S["arg_steps"], M.n * ARG_STEPS + ARG_STEPS)
                    ge(act, S["t_steps"], (M.n - 1) * NT)
                    act.activation(Ex[:, M.p], arg[:, :, :, :], ACT.Exp).then_inc(S["exp_ready"], 1)
                if F:
                    act.wait_ge(S["xT_ready"], F.n + 1)
                    ge(act, S["h_ready"], F.n)
                    act.activation(xnT[:, :], TR[:, :], ACT.Copy).then_inc(S["xnT_ready"], 1)
                if M:
                    relu(M, [2, 3])
                if Q:
                    act.wait_ge(S["nb2_ready"], Q.n + 1)
                    ge(act, S["x2T_ready"], Q.n)
                    ge(act, S["lo_ready"], Q.n)
                    normalise(xn2, xr[:, bass.ds(Q.n * NT, NT), :], rs2, nb2, S["xn2_ready"])
                if M:
                    relu(M, [4])
                if Q:
                    act.wait_ge(S["x2T_ready"], Q.n + 1)
                    ge(act, S["gate_ready"], Q.n)
                    act.activation(xn2T[:, :], TR[:, :], ACT.Copy).then_inc(S["xn2T_ready"], 1)
                if M:
                    relu(M, [5])
                if F:
                    act.wait_ge(S["sT_ready"], F.n + 1)
                    ge(act, S["z_ready"], (F.n - 1) * FILLS)
                    ge(act, S["bc_ready"], F.n - 1)
                    act.activation(rows[:, F.p, :], rowp, ACT.Copy).then_inc(S["rows_ready"], 1)
                if M:
                    relu(M, [6])
                if Q:
                    act.wait_ge(S["xn2_ready"], Q.n * NT + NT)
                    ge(act, scattered[Q.p], Q.h * 16 * 2 * NT)
                    act.activation(rowt[:, Q.p, :, 0:D // 2].bitcast(FP16), xn2[:, :, :], ACT.Copy) \
                       .then_inc(S["hi_ready"], 1)
                for g in range(2):
                    if M:
                        relu(M, [7 + g])
                    if F:
                        act.wait_ge(S["awayT_ready"], F.n * 2 + g + 1)
                        if g == 0:
                            ge(act, S["z_ready"], (F.n - 1) * FILLS)
                            ge(act, S["gh_ready"], (F.n - 1) * NT)
                            ge(act, S["adjn_ready"], F.n - 1)
                        act.activation(thr[:, F.p, 2 * g:2 * g + 2, :], AD[:, :, 0:N], ACT.Copy) \
                           .then_inc(S["thr_ready"], 1)
                if M:
                    relu(M, [9, 10, 11])
            slots(act, body, 18)

            def hidden(at):
                X, U = at(2), at(1)
                if X:
                    act.wait_ge(S["bt_ready"], X.n + 1)
                    ge(act, S["up_ready"], (X.n - 1) * NC)
                    act.activation(xt[:, X.p], XTp[X.p], ACT.Copy).then_inc(S["xt_ready"], 1)
                if U:
                    ge(act, S["split_steps"], (U.n - 1) * 2)
                    ex = act.value_load(tab[0:1, 1, bass.ds(U.n, 1)], min_val=0, max_val=E - 1)
                    for c in range(NC):
                        if c % 2 == 0:
                            act.wait_ge(S["up_ready"], U.n * NC + c + 2)
                        act.activation(h32[:, U.p, c, :], Up[U.p][c // 2][:, (c % 2) * BLK:(c % 2 + 1) * BLK],
                                       ACT.Relu, bias=b1s[:, bass.ds(ex * NC + c, 1)], scale=sc[:, 10:11]) \
                           .then_inc(S["hid_ready"], 1)
            pad_rows(act, range(E // 2, E))
            act.wait_ge(S["tab_ready"], 1)
            steps(act, hidden)

            def first(n, q, k):
                act.wait_ge(ld_y[k], q * 32 + 32)
                for j in range(NT):
                    act.activation(yin[:, k, 0, j, :], yin[:, k, 0, j, :], ACT.Copy,
                                   scale=PR[:, 0, bass.ds(n * NT + j, 1)]).then_inc(S["first_ready"], 1)

            def store(n, k):
                act.wait_ge(S["final_ready"], n + 1)
                act.dma_start(outd[:, bass.ds(n * NT, NT), :], yin[:, k, 1]).then_inc(stored[k], 16)
            for k in range(4):
                first(k, 0, k)
                if k:
                    store(k - 1, k - 1)
            with act.Fori(1, 4) as q:
                for k in range(4):
                    first(q * 4 + k, q, k)
                    store(q * 4 + k - 1, (k - 1) % 4)
            store(15, 3)

        @block.vector
        def _(dve):
            dve.wait_ge(S["ld_const"], 16)
            for dst, src in ((identb, ident), (identh, ident), (trib, C(C_TRI)), (onesb, C(C_ONE)),
                             (selb, C(C_SEL, 24))):
                dve.tensor_copy(dst[:, :], src).then_inc(S["const_ready"], 1)
            dve.tensor_scalar(negb[:, :], ident, -1.0, None, ALU.mult).then_inc(S["const_ready"], 1)
            dve.tensor_copy(carry[:, :], C(C_BASE)).then_inc(S["const_ready"], 1)
            dve.memset(padrow[:, :, 0:D], 0.0).then_inc(S["const_ready"], 1)
            dve.memset(padrow[:, :, D:D + 1], float(2 * TOK)).then_inc(S["const_ready"], 1)
            dve.memset(padrow[:, :, D + 1:D + 2], 0.0).then_inc(S["const_ready"], 1)
            dve.wait_ge(S["const_ready"], 10)

            dve.wait_ge(S["ld_small"], 16 * (2 * H + 3))
            k = Chain(dve, S["prep_step"], 0, 0)
            k.did(dve.tensor_scalar(Am[:, 0:H], C(C_MASK), acol[:, 0:1], None, ALU.mult))
            k.did(dve.tensor_scalar(Am[:, H:2 * H], C(C_MASK), acol[:, 1:2], None, ALU.mult))
            dve.wait_ge(S["prep_pe"], 1)
            k.did(dve.tensor_copy(WT[:, :], bank[4][:, 0:D]))
            k.did(dve.tensor_scalar(WgT[:, :], bank[5][:, 0:E], 1.0 / XSCALE, None, ALU.mult))
            k.did(dve.tensor_copy(b1s[:, :], bank[6][:, 0:E * NC]))
            dve.wait_ge(S["prep_pe"], 2)
            k.did(dve.tensor_copy(Wa[:, :], bank[4][:, D:D + 2 * H]))
            dve.wait_ge(S["ld_w1"], 16)
            k.did(dve.tensor_reduce(sc[:, 0:1], W1r, AX.XY, ALU.max, apply_absolute_value=True))
            dve.wait_ge(S["ld_w2"], 16)
            k.did(dve.tensor_reduce(sc[:, 1:2], W2r, AX.XY, ALU.max, apply_absolute_value=True))
            k.wait()
            k.did(dve.tensor_reduce(sc[:, 2:3], b1s[:, :], AX.X, ALU.max, apply_absolute_value=True))
            dve.wait_ge(S["prep_pe"], 3)
            k.did(dve.tensor_reduce(tf[0:1, 0, 0:1], bank[5][0:1, 128:256], AX.X, ALU.max))
            k.did(dve.tensor_reduce(tf[0:1, 0, 1:2], bank[5][0:1, 256:384], AX.X, ALU.max))
            k.did(dve.tensor_reduce(tf[0:1, 0, 2:3], bank[5][0:1, 384:512], AX.X, ALU.max))
            dve.wait_ge(S["prep_pe"], 4)
            k.did(dve.tensor_scalar(sc[:, 0:1], bank[4][:, 256:257], 1e-20, None, ALU.max))
            k.did(dve.tensor_scalar(sc[:, 1:2], bank[4][:, 257:258], 1e-20, None, ALU.max))
            k.wait()
            k.did(dve.scalar_tensor_tensor(sc[:, 2:3], sc[:, 0:1], 128.0, bank[4][:, 258:259], ALU.mult, ALU.add))
            k.wait()
            k.did(dve.tensor_scalar(sc[:, 4:7].bitcast(I32), sc[:, 0:3].bitcast(I32), 0x7F800000, None,
                                    ALU.bitwise_and))
            k.wait()
            k.did(dve.reciprocal(sc[:, 12:15], sc[:, 4:7]))
            k.wait()
            k.did(dve.tensor_scalar(sc[:, 3:4], sc[:, 12:13], 2.0 ** 13, None, ALU.mult))
            k.did(dve.tensor_scalar(sc[:, 7:8], sc[:, 13:14], 2.0 ** 13, None, ALU.mult))
            k.did(dve.tensor_scalar(sc[:, 8:9], sc[:, 14:15], 2.0 ** 13, None, ALU.mult))
            k.did(dve.tensor_scalar(sc[:, 9:10], sc[:, 4:5], 2.0 ** -13 / XSCALE, None, ALU.mult))
            k.did(dve.tensor_scalar(sc[:, 11:12], sc[:, 6:7], 2.0 ** -13, None, ALU.mult))
            k.did(dve.tensor_scalar(sc[:, 15:16], sc[:, 5:6], 2.0 ** -13, None, ALU.mult))
            k.wait()
            k.did(dve.tensor_tensor(sc[:, 10:11], sc[:, 9:10], sc[:, 8:9], ALU.mult))
            k.did(dve.tensor_tensor(sc[:, 11:12], sc[:, 11:12], sc[:, 15:16], ALU.mult))
            k.did(dve.tensor_scalar(b1s[:, :], b1s[:, :], sc[:, 8:9], None, ALU.mult))
            k.wait()
            dve.sem_inc(S["scale_ready"], 1)
            for u in range(2 * E):
                dve.wait_ge(S["w_act"], u + 1)
                part = [(W1h[:, q, u, :] if u < E else W2h[:, q, u - E, :, :].rearrange("p c d -> p (c d)"))
                        for q in range(2)]
                dve.scalar_tensor_tensor(part[1], bank[u % 4][:, :], sc[:, 3:4] if u < E else sc[:, 7:8],
                                         part[0], ALU.mult, ALU.subtract).then_inc(S["w_dve"], 1)

            def stats(c, src, bs, mv, js):
                for j in js:
                    c.did(dve.bn_stats(bs[:, j, :], src[:, j, :]))
                hold(dve, c.sem, c.now(), S["dve_turns"])
                for j in js:
                    c.did(dve.bn_aggr(mv[:, j, :], bs[:, j, :]))

            def shift(nb, mv, rs, rstd_ready, nb_ready, used, B):
                dve.wait_ge(rstd_ready, B.n * 2 + 2)
                ge(dve, used, B.n * NT)
                dve.scalar_tensor_tensor(nb[:, :], mv[:, :, 0], -1.0, rs[:, :], ALU.mult, ALU.mult).then_inc(nb_ready, 1)

            def mask(M, mt):
                dve.wait_ge(S["bc_ready"], M.n + 1)
                if mt == 0:
                    dve.wait_ge(S["thr_ready"], M.n * 2 + 2)
                    dve.wait_ge(S["s_steps"], M.n * S_STEPS + S_STEPS)
                    ge(dve, S["o_ready"], (M.n - 1) * NT)
                dve.scalar_tensor_tensor(G[:, M.p, H - 1, mt, :], hb[:, :], s2c[:, M.p, mt, H - 1:H],
                                         thr[:, M.p, mt, :], ALU.add, ALU.is_gt).then_inc(S["gh_ready"], 1)

            def binary(M, h):
                dve.wait_ge(S["z_used"], M.n * FILLS + (h + 1) * NT)
                g = G[:, M.p, h].rearrange("p t n -> p (t n)")
                dve.tensor_scalar(g, g, 0.0, None, ALU.is_gt).then_inc(S["g_ready"], 1)

            def scaled_sums(R, nt):
                dve.wait_ge(S["o_ready"], R.n * NT + nt + 1)
                if nt == 0:
                    dve.wait_ge(S["exp_ready"], R.n + 1)
                ge(dve, S["sum_ready"], R.n * 2 - 1 + nt // 2)
                ge(dve, S["att_steps"], R.n * ATT_STEPS)
                f = Ex[:, R.p, 2:4, nt, :].rearrange("p q h -> p h q").unsqueeze(3).to_broadcast([P, H, 2, HD + 1])
                dve.tensor_tensor(T[:, nt], Ob[nt % 2][:, 0:H * VW].rearrange("p (h q v) -> p h q v", q=2, v=HD + 1),
                                  f, ALU.mult).then_inc(S["t_steps"], 1)

            def attention(R, half):
                c = Chain(dve, S["att_steps"], ATT_STEPS, R.n)
                c.k = 2 * half
                ts = slice(2 * half, 2 * half + 2)
                dve.wait_ge(S["sum_ready"], R.n * 2 + half + 1)
                ge(dve, S["x1_ready"], R.n * 2)
                c.did(dve.reciprocal(rec[:, ts, :], T[:, ts, :, 0, HD]))
                c.wait()
                c.did(dve.tensor_tensor(
                    att[:, ts, :].rearrange("p t (h d) -> p t h d", d=HD), T[:, ts, :, 0, 0:HD],
                    rec[:, ts, :].unsqueeze(3).to_broadcast([P, 2, H, HD]), ALU.mult))

            def stats2(B, js):
                c = Chain(dve, S["ln2"], LN_STEPS, B.n)
                c.k = 2 * js[0]
                stats(c, xr[:, bass.ds(B.n * NT, NT), :], bs2, mv2, js)

            rev = C(C_REV).unsqueeze(1).to_broadcast([P, NT, E])

            def body(at):
                L, F, M, R, Q, Z = at(2), at(1), at(0), at(-1), at(-2), at(-3)
                if M:
                    ac = Chain(dve, S["arg_steps"], ARG_STEPS, M.n)
                    dve.wait_ge(S["S_ready"], M.n + 1)
                    ge(dve, S["exp_ready"], M.n)
                    Sb = Sp.unsqueeze(1).to_broadcast([P, NT, H])
                    s2, s1 = s3[:, :, 0, 0:H], s3[:, :, 0, H:2 * H]
                    ac.did(dve.scalar_tensor_tensor(arg[:, 0], s2, SHIFT, Sb, ALU.add, ALU.subtract))
                    ac.did(dve.tensor_tensor(zt[:, :, :], s1, Sb, ALU.add))
                    ac.wait()
                    ac.did(dve.scalar_tensor_tensor(Mt[:, :, :], zt[:, :, :], SLOPE, zt[:, :, :], ALU.mult, ALU.max))
                    ac.did(dve.tensor_scalar(arg[:, 1], arg[:, 0], SLOPE, (1 - SLOPE) * SHIFT, ALU.mult, ALU.add))
                    ac.after(3)
                    ac.did(dve.tensor_tensor(arg[:, 2], zt[:, :, :], Mt[:, :, :], ALU.subtract))
                    ac.did(dve.scalar_tensor_tensor(arg[:, 3], zt[:, :, :], SLOPE, Mt[:, :, :], ALU.mult, ALU.subtract))
                if R:
                    binary(R, 2)
                if Q:
                    attention(Q, 1)
                if Z:
                    rt = Chain(dve, S["rt_steps"], RT_STEPS, Z.n)
                    rt.k = RT_DM
                    dve.wait_ge(S["ed_ready"], Z.n + 1)
                    rt.did(dve.tensor_scalar(den[:, :], ed[:, :], 1.0, None, ALU.add))
                    dve.wait_ge(S["rank_ready"], Z.n + 1)
                    rt.did(dve.tensor_tensor(pos[:, :, :], rkp, carry[:, :].unsqueeze(1).to_broadcast([P, NT, E]),
                                             ALU.add))
                if M:
                    mask(M, 0)
                if Z:
                    rt.after(RT_DM + 2)
                    rt.did(dve.tensor_tensor(carry[:, :], totp, carry[:, :], ALU.add))
                    rt.did(dve.reciprocal(PR[:, 0, bass.ds(Z.n * NT, NT)], den[:, :]))
                    rt.did(dve.tensor_tensor(prod[:, :, :, :], OH[:, :, :, :],
                                             pos[:, :, :].unsqueeze(1).to_broadcast([P, 2, NT, E]), ALU.mult))
                if Q:
                    dve.wait_ge(S["x1_ready"], Q.n * 2 + 2)
                    stats2(Q, [2, 3])
                if M:
                    vc = Chain(dve, S["v_steps"], X_STEPS, M.n)
                    dve.wait_ge(S["exp_ready"], M.n + 1)
                    ge(dve, S["rest_ready"], M.n - 1)
                    h3 = HP[:, :].rearrange("p (g d) -> p g d", d=HD)
                    Vg = V[:, M.p, 0].rearrange("p t h (q v) -> p (t h) q v", q=2)
                    e = Ex[:, M.p, 0:2].rearrange("p q t h -> p (t h) q")
                    vc.did(dve.tensor_tensor(Vg[:, :, :, 0:HD], h3.unsqueeze(2).to_broadcast([P, NT * H, 2, HD]),
                                             e.unsqueeze(3).to_broadcast([P, NT * H, 2, HD]), ALU.mult))
                    vc.did(dve.tensor_copy(Vg[:, :, :, HD], e))
                if Z:
                    rt.after(RT_DM + 5)
                    rt.did(dve.tensor_tensor(PR[:, 1, bass.ds(Z.n * NT, NT)], ed[:, :],
                                             PR[:, 0, bass.ds(Z.n * NT, NT)], ALU.mult))
                    rt.did(dve.tensor_reduce(slotf[:, :, :], prod[:, :, :, :], AX.X, ALU.add))
                    ge(dve, scattered[Z.p], Z.h * 16 * 2 * NT)
                    rt.did(dve.tensor_copy(rowt[:, Z.p, :, D + 1], v01[:, 0, :]))
                    rt.did(dve.tensor_copy(rowt[:, Z.p, :, D], C(C_TOK)[:, bass.ds(Z.n * NT, NT)]))
                if Q:
                    shift(nb2, mv2, rs2, S["rstd2"], S["nb2_ready"], S["xn2_ready"], Q)
                if Z:
                    rt.after(RT_DM + 7)
                    rt.did(dve.tensor_copy(idx[:, Z.p], slotf[:, :, :]))
                    assert rt.k == RT_STEPS
                if F:
                    dve.wait_ge(ld_adj[F.p], F.h * 16 + 16)
                    ge(dve, S["awayT_ready"], F.n * 2)
                    dve.tensor_scalar(away[:, :, :], adji[:, F.p], 0.0, FAR, ALU.is_equal, ALU.mult) \
                       .then_inc(S["adj_cast"], 1)
                if M:
                    dve.wait_ge(S["thr_ready"], M.n * 2 + 2)
                    ge(dve, S["o_ready"], (M.n - 1) * NT)
                    dve.tensor_scalar(adjn[:, M.p], thr[:, M.p], 1.0, -1.0, ALU.is_lt, ALU.mult) \
                       .then_inc(S["adjn_ready"], 1)
                    mask(M, 1)
                if R:
                    scaled_sums(R, 0)
                if F:
                    st = Chain(dve, S["s_steps"], S_STEPS, F.n)
                    dve.wait_ge(S["h_ready"], F.n + 1)
                    ge(dve, S["sT_ready"], F.n)
                    st.did(dve.tensor_copy(s3[:, :, 0, :], s12p))
                    ge(dve, S["z_used"], (F.n - 1) * FILLS)
                    st.did(dve.tensor_copy(s2c[:, F.p], s12p[:, :, 0:H]))
                    st.after(1)
                    st.did(dve.tensor_tensor(s3[:, :, 1, :], s3[:, :, 0, :], s3hi[:, :, 0, :], ALU.subtract))
                    st.wait()
                    st.did(dve.tensor_tensor(s3[:, :, 2, :], s3[:, :, 1, :], s3hi[:, :, 1, :], ALU.subtract))
                    st.did(dve.tensor_reduce(mxp[:, :], s3[:, :, 0, 0:H].rearrange("p t h -> p h t"), AX.X, ALU.max))
                if M:
                    binary(M, 0)
                    mask(M, 2)
                    mask(M, 3)
                if R:
                    scaled_sums(R, 1)
                if Q:
                    rt = Chain(dve, S["rt_steps"], RT_STEPS, Q.n)
                    dve.wait_ge(S["gate_ready"], Q.n + 1)
                    rt.did(dve.tensor_tensor(g8[:, :, :], gp, bgb[:, :].unsqueeze(1).to_broadcast([P, NT, E]), ALU.add))
                if F:
                    mc = Chain(dve, S["mx_steps"], MX_STEPS, F.n)
                    dve.wait_ge(S["sT_ready"], F.n + 1)
                    dve.wait_ge(S["rows_ready"], F.n + 1)
                    mc.did(dve.tensor_reduce(mx[:, :], mxT, AX.X, ALU.max))
                if Q:
                    rt.wait()
                    rt.did(dve.tensor_reduce(m01[:, 0, :], g8[:, :, :], AX.X, ALU.max))
                if M:
                    dve.wait_ge(S["rest_ready"], M.n + 1)
                    dve.tensor_tensor(V3[:, M.p].rearrange("p t h v -> p (t h v)"),
                                      V[:, M.p, 1].rearrange("p t h v -> p (t h v)"),
                                      Vhi[:, M.p, 1].rearrange("p t h v -> p (t h v)"), ALU.subtract) \
                       .then_inc(S["part3_ready"], 1)
                if Q:
                    rt.wait()
                    rt.did(dve.tensor_tensor(eq[:, :, :], g8[:, :, :], m01[:, 0, :].unsqueeze(2).to_broadcast([P, NT, E]),
                                             ALU.is_equal))
                if F:
                    mc.wait()
                    ge(dve, S["S_ready"], F.n)
                    mc.did(dve.tensor_scalar(diag[:, :], C(C_ID, H)[:, 0:H], mx[:, 0:1], None, ALU.mult))
                if Q:
                    rt.wait()
                    rt.did(dve.tensor_tensor(cand[:, :, :], eq[:, :, :], rev, ALU.mult))
                if R:
                    attention(R, 0)
                if Q:
                    rt.wait()
                    rt.did(dve.tensor_reduce(v01[:, 0, :], cand[:, :, :], AX.X, ALU.max))
                if M:
                    binary(M, 1)
                if Q:
                    rt.wait()
                    rt.did(dve.tensor_tensor(OH[:, 0], rev, v01[:, 0, :].unsqueeze(2).to_broadcast([P, NT, E]),
                                             ALU.is_equal))
                if L:
                    if isinstance(L.n, int):
                        dve.wait_ge(S["ld_x0"], 16)
                        if L.n * NT >= XSPLIT:
                            dve.wait_ge(S["ld_x1"], 16)
                    l1 = Chain(dve, S["ln1"], LN_STEPS, L.n)
                    ge(dve, S["rstd1"], L.n * 2)
                    xl = xr[:, bass.ds(L.n * NT, NT), :]
                    stats(l1, xl, bs1, mv1, [0, 1])
                if Q:
                    rt.wait()
                    rt.did(dve.scalar_tensor_tensor(g2[:, :, :], OH[:, 0], -1e30, g8[:, :, :], ALU.mult, ALU.add))
                if L:
                    stats(l1, xl, bs1, mv1, [2, 3])
                if Q:
                    rt.wait()
                    rt.did(dve.tensor_reduce(m01[:, 1, :], g2[:, :, :], AX.X, ALU.max))
                if Q:
                    rt.wait()
                    rt.did(dve.tensor_tensor(eq[:, :, :], g2[:, :, :], m01[:, 1, :].unsqueeze(2).to_broadcast([P, NT, E]),
                                             ALU.is_equal))
                if R:
                    scaled_sums(R, 2)
                if Q:
                    rt.wait()
                    rt.did(dve.tensor_tensor(cand[:, :, :], eq[:, :, :], rev, ALU.mult))
                if L:
                    shift(nb1, mv1, rs1, S["rstd1"], S["nb1_ready"], S["xn_ready"], L)
                if Q:
                    rt.wait()
                    rt.did(dve.tensor_reduce(v01[:, 1, :], cand[:, :, :], AX.X, ALU.max))
                if R:
                    dve.wait_ge(S["x1_ready"], R.n * 2 + 1)
                    if Q:
                        dve.wait_ge(S["nb2_ready"], Q.n + 1)
                    stats2(R, [0, 1])
                if Q:
                    rt.wait()
                    rt.did(dve.tensor_tensor(OH[:, 1], rev, v01[:, 1, :].unsqueeze(2).to_broadcast([P, NT, E]),
                                             ALU.is_equal))
                    rt.wait()
                    ge(dve, S["rank_ready"], Q.n)
                    rt.did(dve.tensor_tensor(sel[:, :, :], OH[:, 0], OH[:, 1], ALU.add))
                    assert rt.k == RT_SEL
                    ge(dve, S["ed_ready"], Q.n)
                    rt.did(dve.tensor_tensor(dm[:, :], m01[:, 1, :], m01[:, 0, :], ALU.subtract))
                    assert rt.k == RT_DM
                if R:
                    scaled_sums(R, 3)
            dve.wait_ge(S["small_ready"], 32)
            slots(dve, body, 18, -2)

            t = Chain(dve, S["tab_steps"], 0, 0)
            dve.wait_ge(S["rt_steps"], NB * RT_STEPS)

            def step(ins):
                t.did(ins)
                t.wait()
            step(dve.tensor_copy(cnti[:, 0, :], carry[:, :]))
            dve.sem_inc(S["ends_ready"], 1)
            step(dve.tensor_tensor(cnt[:, 0, :], carry[:, :], C(C_BASE), ALU.subtract))
            step(dve.tensor_scalar(cnti[:, 1, :], cnt[:, 0, :], float(BLK - 1), None, ALU.add))
            step(dve.tensor_scalar(cnti[:, 1, :], cnti[:, 1, :], BLK.bit_length() - 1, None, ALU.arith_shift_right))
            step(dve.tensor_copy(cnt[:, 1, :], cnti[:, 1, :]))
            cur = 1
            for d in (1, 2, 4):
                step(dve.tensor_copy(cnt[:, cur + 1, 0:d], cnt[:, cur, 0:d]))
                step(dve.tensor_tensor(cnt[:, cur + 1, d:E], cnt[:, cur, d:E], cnt[:, cur, 0:E - d], ALU.add))
                cur += 1
            ends = cnt[:, cur, :].unsqueeze(1).to_broadcast([P, TAB, E])
            io = C(C_IOTA).unsqueeze(2).to_broadcast([P, TAB, E])
            step(dve.tensor_tensor(cube[:, :, :], io, ends, ALU.is_ge))
            step(dve.tensor_reduce(tf[:, 0, :], cube[:, :, :], AX.X, ALU.add))
            step(dve.tensor_tensor(cube[:, :, :], cube[:, :, :], ends, ALU.mult))
            step(dve.tensor_reduce(tf[:, 1, :], cube[:, :, :], AX.X, ALU.max))
            step(dve.tensor_tensor(tf[:, 2, :], C(C_IOTA), tf[:, 1, :], ALU.subtract))
            step(dve.tensor_scalar(tf[:, 3, :], tf[:, 0, :], float(CAP), None, ALU.mult))
            step(dve.scalar_tensor_tensor(tf[:, 4, :], tf[:, 2, :], float(BLK), tf[:, 3, :], ALU.mult, ALU.add))
            step(dve.tensor_scalar(tab[:, 0, :], tf[:, 4, :], float(E * CAP), None, ALU.min))
            step(dve.tensor_scalar(tab[:, 1, :], tf[:, 0, :], float(E - 1), None, ALU.min))
            step(dve.tensor_scalar(tf[:, 5, :], tf[:, 0, :], -1.0, float(E), ALU.mult, ALU.add))
            dve.sem_inc(S["tab_ready"], 1)

            def split(U):
                dve.wait_ge(S["hid_ready"], U.n * NC + NC)
                ge(dve, S["down_ready"], U.n - 1)
                c = Chain(dve, S["split_steps"], 2, U.n)
                c.did(dve.tensor_copy(hp[:, U.p, 0], h32[:, U.p]))
                c.wait()
                c.did(dve.tensor_tensor(hp[:, U.p, 1], h32[:, U.p], hp[:, U.p, 0], ALU.subtract))

            def work(at):
                X, U, Y = at(2), at(1), at(0)
                if U:
                    dve.wait_ge(ld_rows[U.q], U.f * 16 + 16)
                    ge(dve, back[U.q], U.f * 16 * BT)
                    c = Chain(dve, S["bidx_steps"], 2, U.n)
                    c.did(dve.tensor_scalar(bk[:, U.p, :], xb[:, U.q, :, D + 1], tf[:, 5, bass.ds(U.n, 1)],
                                            float(TOK), ALU.not_equal, ALU.mult))
                if U:
                    c.wait()
                    c.did(dve.tensor_tensor(bidx[:, U.q, :], bk[:, U.p, :], xb[:, U.q, :, D], ALU.add))
                    split(U)
                if Y:
                    ex = dve.value_load(tab[0:1, 1, bass.ds(Y.n, 1)], min_val=0, max_val=E - 1)
                    dve.wait_ge(S["down_ready"], Y.n + 1)
                    ge(dve, back[Y.q], Y.f * 16 * BT)
                    dve.scalar_tensor_tensor(ysb[:, Y.q], Yp[Y.p], sc[:, 11:12],
                                             b2b[:, bass.ds(ex, 1), :].to_broadcast([P, BT, D]),
                                             ALU.mult, ALU.add).then_inc(S["y_ready"], 1)
            steps(dve, work)

            def second(n, q, k):
                dve.wait_ge(ld_y[k], q * 32 + 32)
                for j in range(NT):
                    dve.scalar_tensor_tensor(yin[:, k, 1, j, :], yin[:, k, 1, j, :], PR[:, 1, bass.ds(n * NT + j, 1)],
                                             xr[:, bass.ds(n * NT + j, 1), :].rearrange("p a d -> p (a d)"),
                                             ALU.mult, ALU.add).then_inc(S["second_ready"], 1)
                dve.wait_ge(S["first_ready"], n * NT + NT)
                dve.wait_ge(S["second_ready"], n * NT + NT)
                yk = yin[:, k].rearrange("p c t d -> p c (t d)")
                dve.tensor_tensor(yk[:, 1], yk[:, 1], yk[:, 0], ALU.add).then_inc(S["final_ready"], 1)
            with dve.Fori(0, 4) as q:
                for k in range(4):
                    second(q * 4 + k, q, k)

        @block.tensor
        def _(pe):
            mm = pe.matmul
            pe.wait_ge(S["ld_const"], 16)
            pe.wait_ge(S["ld_small"], 16 * (2 * H + 3))
            pe.transpose(bank[4][:, 0:D], Wr[:, :], ident)
            pe.transpose(bank[5][:, 0:E], Wgr[:, :], C(C_ID, E)[:, 0:E])
            pe.transpose(bank[6][:, 0:E * NC], b1r[:, :], C(C_ID, E * NC)[:, 0:E * NC]).then_inc(S["prep_pe"], 1)
            pe.wait_ge(S["prep_step"], 5)
            mm(bank[4][:, D:D + 2 * H], WT[:, :], Am[:, :], start=True, stop=True).then_inc(S["prep_pe"], 1)
            pe.wait_ge(S["prep_step"], 9)
            for q in range(3):
                last = pe.transpose(bank[5][0:1, 128 * (q + 1):128 * (q + 2)], sc[:, q:q + 1], ident)
            last.then_inc(S["prep_pe"], 1)
            pe.wait_ge(S["prep_step"], 12)
            mm(bank[4][:, 256:259], C(C_ONE, 1), tf[0:1, 0, 0:3], start=True, stop=True).then_inc(S["prep_pe"], 1)
            for u in range(2 * E):
                ge(pe, S["w_dve"], u - 3)
                ge(pe, S["w_act"], u - 3)
                for c in range(NC):
                    src = W1r[:, u * NC + c, :] if u < E else W2r[:, u - E, c * P:(c + 1) * P]
                    last = pe.transpose(bank[u % 4][:, c * P:(c + 1) * P], src, ident)
                last.then_inc(S["w_pe"], 1)
            pe.wait_ge(S["w_dve"], 2 * E)
            pe.wait_ge(S["const_ready"], 10)

            def broadcast(M):
                pe.wait_ge(S["rows_ready"], M.n + 1)
                ge(pe, S["gh_ready"], M.n * NT)
                mm(hb[:, :], selb[:, (H - 1) * P:H * P], rows[:, M.p, :], start=True, stop=True) \
                    .then_inc(S["bc_ready"], 1)

            def fill(M, k):
                h, mt = k // NT, k % NT
                if k == 0:
                    pe.wait_ge(S["thr_ready"], M.n * 2 + 2)
                ge(pe, S["z_used"], M.n * FILLS + k - 1)
                mm(zb[k % 2][:, :], negb[:, :], thr[:, M.p, mt, :], start=True, stop=False)
                mm(zb[k % 2][:, :], selb[:, h * P:(h + 1) * P], rows[:, M.p, :], start=False, stop=True) \
                    .then_inc(S["z_ready"], 1)

            def sums(R, nt, part):
                o = Ob[nt % 2][:, 0:H * VW].rearrange("p (h v) -> p h v", v=VW)
                if part == 0:
                    ge(pe, S["t_steps"], R.n * NT + nt - 1)
                    if nt == 0:
                        pe.wait_ge(S["part3_ready"], R.n + 1)
                        pe.wait_ge(S["adjn_ready"], R.n + 1)
                    for mt in range(NT):
                        for q in range(3):
                            v = V3[:, R.p, mt] if q == 2 else Vhi[:, R.p, q, mt]
                            mm(o[:, :, HD + 1:VW], adjn[:, R.p, mt, nt * P:(nt + 1) * P], v[:, :, HD + 1:VW],
                               start=(mt == 0 and q == 0), stop=False, skip_group_check=True)
                    return
                h = (part + H - 2) % H
                if nt == 0:
                    if h == H - 1:
                        pe.wait_ge(S["gh_ready"], R.n * NT + NT)
                    else:
                        pe.wait_ge(S["g_ready"], R.n * ACT_HEADS + h + 1)
                for mt in range(NT):
                    for q in range(3):
                        v = V3[:, R.p, mt] if q == 2 else Vhi[:, R.p, q, mt]
                        last = mm(o[:, h, :], G[:, R.p, h, mt, nt * P:(nt + 1) * P], v[:, h, :],
                                  start=False, stop=(part == H and mt == NT - 1 and q == 2), skip_group_check=True)
                if part == H:
                    last.then_inc(S["o_ready"], 1)

            def transpose_rows(F, M):
                if F:
                    pe.wait_ge(S["xn_ready"], F.n * NT + NT)
                    if M:
                        pe.wait_ge(S["arg_steps"], M.n * ARG_STEPS + 2)
                    for j in range(NT):
                        last = pe.transpose(TR[:, j * P:(j + 1) * P], xn[:, j, :], ident)
                    last.then_inc(S["xT_ready"], 1)

            def transpose_rows2(F, Q):
                if Q:
                    pe.wait_ge(S["xn2_ready"], Q.n * NT + NT)
                    if F:
                        pe.wait_ge(S["xnT_ready"], F.n + 1)
                    for j in range(NT):
                        last = pe.transpose(TR[:, j * P:(j + 1) * P], xn2[:, j, :], ident)
                    last.then_inc(S["x2T_ready"], 1)

            def products(F, Z, M):
                if F:
                    pe.wait_ge(S["xnT_ready"], F.n + 1)
                    if M:
                        pe.wait_ge(S["v_steps"], M.n * X_STEPS + X_STEPS)
                    if Z:
                        pe.wait_ge(S["rt_steps"], Z.n * RT_STEPS + RT_DM + 3)
                    for j in range(NT):
                        mm(HP[:, j * P:(j + 1) * P], xnT[:, j * P:(j + 1) * P], Wr[:, :], start=True, stop=True)
                        last = mm(s12p[:, j, :], xnT[:, j * P:(j + 1) * P], Wa[:, :], start=True, stop=True)
                    last.then_inc(S["h_ready"], 1)

            def gate(Q):
                if Q:
                    pe.wait_ge(S["xn2T_ready"], Q.n + 1)
                    for j in range(NT):
                        last = mm(gp[:, j, :], xn2T[:, j * P:(j + 1) * P], WgT[:, :], start=True, stop=True)
                    last.then_inc(S["gate_ready"], 1)

            def transpose_s(F):
                if F:
                    pe.wait_ge(S["s_steps"], F.n * S_STEPS + S_STEPS)
                    for j in range(NT):
                        pe.transpose(rowp[:, j * P:(j + 1) * P],
                                            s3hi[:, j].rearrange("p q c -> p (q c)"), identb[:, :])
                    pe.transpose(mxT, mxp[:, :], ident).then_inc(S["sT_ready"], 1)

            def largest(F):
                if F:
                    pe.wait_ge(S["mx_steps"], F.n * MX_STEPS + MX_STEPS)
                    pe.wait_ge(S["thr_ready"], F.n * 2 + 2)
                    mm(Sp, C(C_ONE, H), diag[:, :], start=True, stop=True).then_inc(S["S_ready"], 1)

            def transpose_away(F, Q, g):
                if F:
                    if g == 0:
                        pe.wait_ge(S["adj_cast"], F.n + 1)
                        pe.wait_ge(S["xnT_ready"], F.n + 1)
                        if Q:
                            pe.wait_ge(S["rt_steps"], Q.n * RT_STEPS + 1)
                    else:
                        pe.wait_ge(S["thr_ready"], F.n * 2 + 1)
                    for mt in (2 * g, 2 * g + 1):
                        for nt in range(NT):
                            last = pe.transpose(AD[:, mt % 2, nt * P:(nt + 1) * P],
                                                away[:, nt, mt * P:(mt + 1) * P], identb[:, :])
                    last.then_inc(S["awayT_ready"], 1)

            def ranks(Z):
                if Z:
                    pe.wait_ge(S["rt_steps"], Z.n * RT_STEPS + RT_SEL)
                    pe.wait_ge(S["rows_ready"], min(Z.n + 4, NB) if isinstance(Z.n, int) else Z.n + 4)
                    mm(rkp, trib[:, :], sel[:, :, :], start=True, stop=False, skip_group_check=True)
                    for j in range(NT - 1):
                        mm(rkp[:, j + 1:NT, :], onesb[:, :], sel[:, j:j + 1, :].to_broadcast([P, NT - 1 - j, E]),
                           start=False, stop=(j == NT - 2), skip_group_check=True)
                    for j in range(NT):
                        last = mm(totp, onesb[:, :], sel[:, j, :], start=(j == 0), stop=(j == NT - 1),
                                  skip_group_check=True)
                    last.then_inc(S["rank_ready"], 1)

            def body(at):
                F, M, R, Q, Z = at(1), at(0), at(-1), at(-2), at(-3)
                if M:
                    broadcast(M)
                k = 0
                for nt in range(NT):
                    for part in range(H + 1):
                        if M and part % 2 == 0:
                            fill(M, k)
                            k += 1
                        if R:
                            sums(R, nt, part)
                        done = nt * (H + 1) + part
                        if done == 1:
                            ranks(Z)
                        if done == 2:
                            transpose_rows(F, M)
                        if done == 7:
                            products(F, Z, M)
                        if done == 8:
                            transpose_rows2(F, Q)
                        if done == 10:
                            transpose_s(F)
                        if done == 11:
                            gate(Q)
                        if done == 13:
                            transpose_away(F, Q, 0)
                        if done == 15:
                            transpose_away(F, Q, 1)
                        if done == 17:
                            largest(F)
            slots(pe, body, 18)

            held = {}

            def layers(at):
                X, U, Y = at(2), at(1), at(0)
                if X:
                    pe.wait_ge(ld_rows[X.q], X.f * 16 + 16)
                    ge(pe, S["xt_ready"], X.n - 1)
                    xv = xb[:, X.q, :, 0:D].bitcast(FP16).rearrange("p t (q d) -> p t q d", q=2)
                    for q in range(2):
                        for t in range(BT):
                            last = pe.transpose(XTp[X.p][:, q, t * P:(t + 1) * P], xv[:, t, q, :], identh[:, :])
                    last.then_inc(S["bt_ready"], 1)
                if Y:
                    ey = held.pop("e", None)
                    if ey is None or at.first:
                        ey = pe.value_load(tab[0:1, 1, bass.ds(Y.n, 1)], min_val=0, max_val=E - 1)
                if U:
                    pe.wait_ge(S["xt_ready"], U.n + 1)
                    ge(pe, S["hid_ready"], (U.n - 1) * NC)
                    ex = held["e"] = pe.value_load(tab[0:1, 1, bass.ds(U.n, 1)], min_val=0, max_val=E - 1)
                    for c in range(NC):
                        o = Up[U.p][c // 2][:, (c % 2) * BLK:(c % 2 + 1) * BLK]
                        for n, (wq, xq) in enumerate(((0, 0), (0, 1), (1, 0))):
                            w = W1h[:, wq, bass.ds(ex, 1), c * P:(c + 1) * P].rearrange("p e h -> p (e h)")
                            last = mm(o, w, xt[:, U.p, xq, :], start=(n == 0), stop=(n == 2))
                        last.then_inc(S["up_ready"], 1)
                if Y:
                    pe.wait_ge(S["split_steps"], Y.n * 2 + 2)
                    ge(pe, S["y_ready"], Y.n - 1)
                    for c in range(NC):
                        w = [W2h[:, q, bass.ds(ey, 1), c, :].rearrange("p e d -> p (e d)") for q in range(2)]
                        for n, (hq, wq) in enumerate(((0, 0), (1, 0), (0, 1))):
                            for t in range(BT):
                                last = mm(Yp[Y.p][:, t, :], hp[:, Y.p, hq, c, t * P:(t + 1) * P], w[wq],
                                          start=(c == 0 and n == 0 and t == 0),
                                          stop=(c == NC - 1 and n == 2), skip_group_check=True)
                    last.then_inc(S["down_ready"], 1)
            pe.wait_ge(S["tab_ready"], 1)
            steps(pe, layers)


_INS = ["x", "adj", "L0_gnn_W", "L0_gnn_a", "L0_ffn_Wg", "L0_ffn_bg", "L0_ffn_W1", "L0_ffn_b1", "L0_ffn_W2", "L0_ffn_b2"]


def kernel(**inputs):
    import numpy as np
    import concourse.bacc as bacc
    from concourse.bass_utils import run_bass_kernel_spmd

    nc = bacc.Bacc("TRN2", target_bir_lowering=False, num_devices=1)
    arrays, args = {}, []
    for name in _INS:
        arr = np.ascontiguousarray(inputs[name])
        arrays[f"in_{name}"] = arr
        args.append(nc.dram_tensor(f"in_{name}", arr.shape, mybir.dt.from_np(arr.dtype), kind="ExternalInput").ap())
    arrays["in_const"] = constants(np)
    args.append(nc.dram_tensor("in_const", (P, NCONST), F32, kind="ExternalInput").ap())
    args.append(nc.dram_tensor("out_0", (NB, N, D), F32, kind="ExternalOutput").ap())
    build(nc, *args)
    r = run_bass_kernel_spmd(nc, [arrays], core_ids=[0])
    return r.results[0]["out_0"]
```
